# Optimizing a Trainium2 kernel written in Bass

```python
import numpy as np
import jax
import jax.numpy as jnp

def _softmax(x, axis=-1):
    return jax.nn.softmax(x, axis=axis)

def _gelu(x):
    return jax.nn.gelu(x, approximate=True)

def _silu(x):
    return jax.nn.silu(x)

def _sigmoid(x):
    return jax.nn.sigmoid(x)

def _layernorm(x, axis=-1, eps=1e-05):
    m = jnp.mean(x, axis=axis, keepdims=True)
    v = jnp.var(x, axis=axis, keepdims=True)
    return (x - m) / jnp.sqrt(v + eps)

def _scatter_add(tgt, idx, src, axis=0):
    return tgt.at[idx].add(src)

def _segment_sum(src, seg, n):
    return jax.ops.segment_sum(src, seg, n)
kernel_name = 'mk_hybrid_d1_jaxref_r8_a47c65'

def setup_inputs(seed: int=0):
    np.random.seed(seed)
    _w = jnp.asarray

    def _L0_attn_a_setup():
        import jax, jax.numpy as jnp
        import numpy as np
        B, S, H = (4, 256, 256)
        key = jax.random.key(seed)
        k1, k2, k3 = jax.random.split(key, 3)
        xav_qkv = float(np.sqrt(6.0 / (H + 3 * H)))
        xav_out = float(np.sqrt(6.0 / (H + H)))
        return {'hidden_states': jax.random.normal(k1, (B, S, H), dtype=jnp.float32), 'w_qkv': jax.random.uniform(k2, (3 * H, H), minval=-xav_qkv, maxval=xav_qkv, dtype=jnp.float32), 'b_qkv': jnp.zeros((3 * H,), dtype=jnp.float32), 'w_out': jax.random.uniform(k3, (H, H), minval=-xav_out, maxval=xav_out, dtype=jnp.float32), 'b_out': jnp.zeros((H,), dtype=jnp.float32)}
    _L0_attn_a_in = _L0_attn_a_setup()

    def _L0_attn_b_setup():
        import jax, jax.numpy as jnp
        import numpy as np
        ROPE_BASE = 10000.0
        ROPE_SCALE = 1.0
        ATTN_SCALE = 0.08838834764831845
        WINDOW = 128
        EPS = 1e-06

        def rms_norm(x, scale):
            var = jnp.mean(jnp.square(x), axis=-1, keepdims=True)
            return x * jax.lax.rsqrt(var + EPS) * scale

        def apply_rope(x, positions):
            H = x.shape[-1]
            frac = jnp.arange(0, H, 2, dtype=jnp.float32) / H
            timescale = ROPE_BASE ** frac
            sinusoid = positions[..., None].astype(jnp.float32) / timescale
            sinusoid = sinusoid / ROPE_SCALE
            sin = jnp.sin(sinusoid)[:, :, None, :]
            cos = jnp.cos(sinusoid)[:, :, None, :]
            x1, x2 = jnp.split(x, 2, axis=-1)
            return jnp.concatenate([x1 * cos - x2 * sin, x2 * cos + x1 * sin], axis=-1).astype(x.dtype)
        key = jax.random.key(seed)
        ks = jax.random.split(key, 4)
        B, T, D, N, K, H = (1, 512, 256, 16, 8, 128)
        return {'x': jax.random.normal(ks[0], (B, T, D), jnp.float32), 'q_kernel': jax.random.normal(ks[1], (N, D, H), jnp.float32) * D ** (-0.5), 'kv_kernel': jax.random.normal(ks[2], (2, K, D, H), jnp.float32) * D ** (-0.5), 'out_kernel': jax.random.normal(ks[3], (N, H, D), jnp.float32) * (N * H) ** (-0.5), 'q_norm_scale': jnp.ones((H,), jnp.float32), 'k_norm_scale': jnp.ones((H,), jnp.float32)}
    _L0_attn_b_in = _L0_attn_b_setup()

    def _L0_ffn_setup():
        import jax, jax.numpy as jnp
        import numpy as np
        TOP_K = 6
        CAP_FACTOR = 2

        def _moe_block(x2d, wg_router, w_gate, w_up, w_down, ws_gate, ws_up, ws_down):
            T, D = x2d.shape
            E = wg_router.shape[0]
            scores = jax.nn.softmax(x2d @ wg_router.T, axis=-1)
            topk_w, topk_idx = jax.lax.top_k(scores, TOP_K)
            topk_w = topk_w / (jnp.sum(topk_w, axis=-1, keepdims=True) + 1e-20)
            flat_idx = topk_idx.reshape(-1)
            oh = jax.nn.one_hot(flat_idx, E, dtype=jnp.int32)
            pos = jnp.cumsum(oh, axis=0) - 1
            pos_in_e = jnp.take_along_axis(pos, flat_idx[:, None], axis=1)[:, 0]
            C = CAP_FACTOR * (T * TOP_K // E)
            valid = pos_in_e < C
            safe_pos = jnp.where(valid, pos_in_e, 0)
            tok_id = jnp.repeat(jnp.arange(T), TOP_K)
            vmask = valid[:, None].astype(x2d.dtype)
            x_rep = x2d[tok_id] * vmask
            xe = jnp.zeros((E, C, D), x2d.dtype).at[flat_idx, safe_pos].add(x_rep)
            g = jnp.einsum('ecd,edf->ecf', xe, w_gate)
            u = jnp.einsum('ecd,edf->ecf', xe, w_up)
            ye = jnp.einsum('ecf,efd->ecd', jax.nn.silu(g) * u, w_down)
            y_tok = ye[flat_idx, safe_pos] * vmask
            y = jnp.sum(y_tok.reshape(T, TOP_K, D) * topk_w[..., None], axis=1)
            sh = jax.nn.silu(x2d @ ws_gate) * (x2d @ ws_up) @ ws_down
            return y + sh
        key = jax.random.key(seed)
        ks = jax.random.split(key, 9)
        B, S, D, F, E = (1, 256, 256, 176, 32)
        FS = F * 2
        s = 0.02
        return {'hidden_states': jax.random.normal(ks[0], (B, S, D), jnp.float32), 'wg_router': jax.random.normal(ks[1], (E, D), jnp.float32) * s, 'w_gate': jax.random.normal(ks[2], (E, D, F), jnp.float32) * s, 'w_up': jax.random.normal(ks[3], (E, D, F), jnp.float32) * s, 'w_down': jax.random.normal(ks[4], (E, F, D), jnp.float32) * s, 'ws_gate': jax.random.normal(ks[5], (D, FS), jnp.float32) * s, 'ws_up': jax.random.normal(ks[6], (D, FS), jnp.float32) * s, 'ws_down': jax.random.normal(ks[7], (FS, D), jnp.float32) * s}
    _L0_ffn_in = _L0_ffn_setup()
    _d = {'L0_attn_a_hidden_states': _L0_attn_a_in['hidden_states'], 'L0_attn_a_w_qkv': _L0_attn_a_in['w_qkv'], 'L0_attn_a_b_qkv': _L0_attn_a_in['b_qkv'], 'L0_attn_a_w_out': _L0_attn_a_in['w_out'], 'L0_attn_a_b_out': _L0_attn_a_in['b_out'], 'L0_attn_b_q_kernel': _L0_attn_b_in['q_kernel'], 'L0_attn_b_kv_kernel': _L0_attn_b_in['kv_kernel'], 'L0_attn_b_out_kernel': _L0_attn_b_in['out_kernel'], 'L0_attn_b_q_norm_scale': _L0_attn_b_in['q_norm_scale'], 'L0_attn_b_k_norm_scale': _L0_attn_b_in['k_norm_scale'], 'L0_ffn_wg_router': _L0_ffn_in['wg_router'], 'L0_ffn_w_gate': _L0_ffn_in['w_gate'], 'L0_ffn_w_up': _L0_ffn_in['w_up'], 'L0_ffn_w_down': _L0_ffn_in['w_down'], 'L0_ffn_ws_gate': _L0_ffn_in['ws_gate'], 'L0_ffn_ws_up': _L0_ffn_in['ws_up'], 'L0_ffn_ws_down': _L0_ffn_in['ws_down']}
    _x0 = _d['L0_attn_a_hidden_states']
    _d['L0_attn_a_hidden_states'] = jax.random.normal(jax.random.fold_in(jax.random.key(seed), 1), (2, 512, 256), dtype=_x0.dtype)
    del _x0
    return _d

def reference(L0_attn_a_hidden_states, L0_attn_a_w_qkv, L0_attn_a_b_qkv, L0_attn_a_w_out, L0_attn_a_b_out, L0_attn_b_q_kernel, L0_attn_b_kv_kernel, L0_attn_b_out_kernel, L0_attn_b_q_norm_scale, L0_attn_b_k_norm_scale, L0_ffn_wg_router, L0_ffn_w_gate, L0_ffn_w_up, L0_ffn_w_down, L0_ffn_ws_gate, L0_ffn_ws_up, L0_ffn_ws_down):

    def _L0_attn_a_ref(hidden_states, w_qkv, b_qkv, w_out, b_out):
        import jax, jax.numpy as jnp
        import numpy as np
        B, S, H = (4, 256, 256)
        Bc, Sc, Hc = hidden_states.shape
        scaling = jnp.sqrt(jnp.asarray(Hc, hidden_states.dtype))
        qkv = jnp.einsum('bsh,oh->bso', hidden_states, w_qkv) + b_qkv
        q, k, v = jnp.split(qkv, 3, axis=-1)
        scores = jnp.einsum('bqh,bkh->bqk', q, k) / scaling
        probs = jax.nn.softmax(scores, axis=-1)
        context = jnp.einsum('bqk,bkh->bqh', probs, v)
        out = jnp.einsum('bsh,oh->bso', context, w_out) + b_out
        return out

    def _L0_attn_b_ref(x, q_kernel, kv_kernel, out_kernel, q_norm_scale, k_norm_scale):
        import jax, jax.numpy as jnp
        import numpy as np
        ROPE_BASE = 10000.0
        ROPE_SCALE = 1.0
        ATTN_SCALE = 0.08838834764831845
        WINDOW = 128
        EPS = 1e-06

        def rms_norm(x, scale):
            var = jnp.mean(jnp.square(x), axis=-1, keepdims=True)
            return x * jax.lax.rsqrt(var + EPS) * scale

        def apply_rope(x, positions):
            H = x.shape[-1]
            frac = jnp.arange(0, H, 2, dtype=jnp.float32) / H
            timescale = ROPE_BASE ** frac
            sinusoid = positions[..., None].astype(jnp.float32) / timescale
            sinusoid = sinusoid / ROPE_SCALE
            sin = jnp.sin(sinusoid)[:, :, None, :]
            cos = jnp.cos(sinusoid)[:, :, None, :]
            x1, x2 = jnp.split(x, 2, axis=-1)
            return jnp.concatenate([x1 * cos - x2 * sin, x2 * cos + x1 * sin], axis=-1).astype(x.dtype)
        B, T, D = x.shape
        N, _, H = q_kernel.shape
        K = kv_kernel.shape[1]
        G = N // K
        q = jnp.einsum('btd,ndh->btnh', x, q_kernel)
        kv = jnp.einsum('bsd,ckdh->cbskh', x, kv_kernel)
        k, v = (kv[0], kv[1])
        q = rms_norm(q, q_norm_scale)
        k = rms_norm(k, k_norm_scale)
        positions = jnp.broadcast_to(jnp.arange(T)[None, :], (B, T))
        q = apply_rope(q, positions)
        k = apply_rope(k, positions)
        i = jnp.arange(T)[:, None]
        j = jnp.arange(T)[None, :]
        mask = (j <= i) & (i - j < WINDOW)
        qg = q.reshape(B, T, K, G, H)
        logits = jnp.einsum('btkgh,bskh->bkgts', qg * ATTN_SCALE, k)
        logits = jnp.where(mask[None, None, None], logits, jnp.finfo(logits.dtype).min)
        probs = jax.nn.softmax(logits, axis=-1)
        enc = jnp.einsum('bkgts,bskh->btkgh', probs, v).reshape(B, T, N, H)
        return jnp.einsum('btnh,nhd->btd', enc, out_kernel)

    def _L0_ffn_ref(hidden_states, wg_router, w_gate, w_up, w_down, ws_gate, ws_up, ws_down):
        import jax, jax.numpy as jnp
        import numpy as np
        TOP_K = 6
        CAP_FACTOR = 2

        def _moe_block(x2d, wg_router, w_gate, w_up, w_down, ws_gate, ws_up, ws_down):
            T, D = x2d.shape
            E = wg_router.shape[0]
            scores = jax.nn.softmax(x2d @ wg_router.T, axis=-1)
            topk_w, topk_idx = jax.lax.top_k(scores, TOP_K)
            topk_w = topk_w / (jnp.sum(topk_w, axis=-1, keepdims=True) + 1e-20)
            flat_idx = topk_idx.reshape(-1)
            oh = jax.nn.one_hot(flat_idx, E, dtype=jnp.int32)
            pos = jnp.cumsum(oh, axis=0) - 1
            pos_in_e = jnp.take_along_axis(pos, flat_idx[:, None], axis=1)[:, 0]
            C = CAP_FACTOR * (T * TOP_K // E)
            valid = pos_in_e < C
            safe_pos = jnp.where(valid, pos_in_e, 0)
            tok_id = jnp.repeat(jnp.arange(T), TOP_K)
            vmask = valid[:, None].astype(x2d.dtype)
            x_rep = x2d[tok_id] * vmask
            xe = jnp.zeros((E, C, D), x2d.dtype).at[flat_idx, safe_pos].add(x_rep)
            g = jnp.einsum('ecd,edf->ecf', xe, w_gate)
            u = jnp.einsum('ecd,edf->ecf', xe, w_up)
            ye = jnp.einsum('ecf,efd->ecd', jax.nn.silu(g) * u, w_down)
            y_tok = ye[flat_idx, safe_pos] * vmask
            y = jnp.sum(y_tok.reshape(T, TOP_K, D) * topk_w[..., None], axis=1)
            sh = jax.nn.silu(x2d @ ws_gate) * (x2d @ ws_up) @ ws_down
            return y + sh
        B, S, D = hidden_states.shape
        x2d = hidden_states.reshape(-1, D)
        out = _moe_block(x2d, wg_router, w_gate, w_up, w_down, ws_gate, ws_up, ws_down)
        return out.reshape(B, S, D)
    x = L0_attn_a_hidden_states
    x = x + _L0_attn_a_ref(_layernorm(x, axis=-1), L0_attn_a_w_qkv, L0_attn_a_b_qkv, L0_attn_a_w_out, L0_attn_a_b_out)
    x = x + _L0_ffn_ref(_layernorm(x, axis=-1), L0_ffn_wg_router, L0_ffn_w_gate, L0_ffn_w_up, L0_ffn_w_down, L0_ffn_ws_gate, L0_ffn_ws_up, L0_ffn_ws_down)
    x = x + _L0_attn_b_ref(_layernorm(x, axis=-1), L0_attn_b_q_kernel, L0_attn_b_kv_kernel, L0_attn_b_out_kernel, L0_attn_b_q_norm_scale, L0_attn_b_k_norm_scale)
    x = x + _L0_ffn_ref(_layernorm(x, axis=-1), L0_ffn_wg_router, L0_ffn_w_gate, L0_ffn_w_up, L0_ffn_w_down, L0_ffn_ws_gate, L0_ffn_ws_up, L0_ffn_ws_down)
    return x

_drawn_inputs = setup_inputs


def setup_inputs(seed=0):
    import zlib

    import numpy as np

    out = dict(_drawn_inputs(seed))
    spreads = {'L0_attn_a_b_qkv': (0.0, 0.1),
     'L0_attn_a_b_out': (0.0, 0.1),
     'L0_attn_b_q_norm_scale': (1.0, 0.57),
     'L0_attn_b_k_norm_scale': (1.0, 0.6)}
    factors = {'L0_ffn_wg_router': 5.714,
     'L0_ffn_w_gate': 5.085,
     'L0_ffn_w_up': 5.002,
     'L0_ffn_w_down': 5.002}
    for name, (base, spread) in spreads.items():
        noise = np.random.default_rng([zlib.crc32(name.encode()), seed]).standard_normal(out[name].shape)
        drawn = base * np.exp(spread * noise) if base else spread * noise
        out[name] = jnp.asarray(drawn.astype(out[name].dtype))
    for name, factor in factors.items():
        out[name] = (out[name] * factor).astype(out[name].dtype)
    return out
```

```python
from contextlib import ExitStack

import concourse.bass as bass
import numpy as np
from concourse import mybir

ALU = mybir.AluOpType
ACT = mybir.ActivationFunctionType
F32 = mybir.dt.float32
F32R = mybir.dt.float32r
BF16 = mybir.dt.bfloat16
I32 = mybir.dt.int32
U16 = mybir.dt.uint16
U32 = mybir.dt.uint32
X = mybir.AxisListType.X

P = 128
D = 256
DC = D // P
TOK = 1024
TILES = TOK // P
BATCHES = 2
BT = TILES // BATCHES
SEQ = BT * P

E = 32
TOP_K = 6
F_EXP = 176
F_SH = 352
CAP = 2 * (TOK * TOP_K // E)
HID = E * F_EXP + F_SH
HT = (HID + P - 1) // P
GATES = E + 1
SW = 3 * D

NQ = 16
NKV = 8
HD = 128
WINDOW = 128
QKV_B = (NQ + 2 * NKV) * HD
CH = 4
K_CHUNKS = NKV // CH
Q_CHUNKS = NQ // CH
CHUNKS = 2 * K_CHUNKS + Q_CHUNKS
SCALE_B = 0.08838834764831845
EPS_LN = 1e-5
EPS_RMS = 1e-6
MASKED = -1e30
OVER = 21504
STEPS_RSQRT = 12
STEPS_A = 2 * BT + STEPS_RSQRT + 2 * BT
STEPS_B = 2 * BT + STEPS_RSQRT + BT * (2 * STEPS_RSQRT + 1) + 3 * NKV * BT
RSQRT_MAGIC = float(0x5F3759DF)


class Steps:

    def __init__(self, engine, sem, base=0):
        self.engine, self.sem, self.base, self.n = engine, sem, base, 0

    def did(self, instruction):
        self.n += 1
        return instruction.then_inc(self.sem, 1)

    def wait(self):
        self.engine.wait_ge(self.sem, self.base + self.n)


def program(nc, x_in, w_qkv_a, b_qkv_a, w_out_a, b_out_a, w_qkv_b, w_out_b, q_scale, k_scale, w_router,
            w_moe, identity_in, before_in, select_in, rope_in, mask_in, out):
    with ExitStack() as ctx:
        def sb(name, shape, dt=F32):
            return ctx.enter_context(nc.sbuf_tensor(name, shape, dt))

        def sem(name):
            return ctx.enter_context(nc.semaphore(name))

        x_tok = sb("x_tok", [P, TILES, D])
        xn = sb("xn", [P, BT, D])
        xT_hi = sb("xT_hi", [P, DC, TOK], F32R)
        xT_lo = sb("xT_lo", [P, DC, TOK], F32R)
        w_out_b_sb = sb("w_out_b_sb", [P, NQ, D])
        halves = sb("halves", [P, 2, DC * QKV_B], F32R)
        raw = sb("raw", [P, 2, SW])
        sel = sb("sel", [3 * GATES, 2, P], BF16)
        combT = sb("combT", [3 * GATES, TOK], BF16)
        identity = sb("identity", [P, P])
        identity_bf = sb("identity_bf", [P, P], BF16)
        before = sb("before", [P, 2, P], BF16)
        mask = sb("mask", [P, 2, HD])
        w_router_sb = sb("w_router_sb", [P, DC, E])
        b_qkv_sb = sb("b_qkv_sb", [P, 6])
        stats = sb("stats", [P, BT, 6])
        mean_var = sb("mean_var", [P, BT, 2])
        rstd = sb("rstd", [P, 3, NQ])
        ss = sb("ss", [P, 2, CHUNKS * CH])
        rqs = sb("rqs", [P, 2, NQ])
        rk = sb("rk", [P, 2, NKV])
        mx = sb("mx", [P, 4, 2])
        nb = sb("nb", [P, 4, 2])
        lsum = sb("lsum", [P, 4, 2])
        rl = sb("rl", [P, 4, 2])
        small = sb("small", [P, 4, TILES])
        turn = sb("turn", [P, 1])
        top = sb("top", [P, TILES, 8])
        over = sb("over", [P, OVER])

        def part(start, *shape):
            n = int(np.prod(shape))
            v = over[:, start:start + n]
            names = " ".join(f"d{k}" for k in range(len(shape)))
            if len(shape) > 1:
                v = v.rearrange(f"p ({names}) -> p {names}",
                                **{f"d{k}": s for k, s in enumerate(shape[:-1])})
            return v, start + n

        w_raw_b, _ = part(0, DC * QKV_B)
        qT, at = part(0, 2, NQ, P)
        kT, at = part(at, 3, NKV, P)
        v_b, at = part(at, 3, NKV * HD)
        s_b, at = part(at, 2, 2, 2 * P)
        p_b, at = part(at, 2, 2, 2 * P)
        pT_b, at = part(at, 2, 2, 2 * P)
        encT, at = part(at, NQ, P)
        roped, at = part(at, 2, CH, HD)
        squares, at = part(at, 2, CH * HD)
        rope_a, at = part(at, 2, CH, HD)
        rope_b, at = part(at, 2, CH, HD)
        tables, at = part(at, 4, BT, HD)
        assert at <= OVER
        rope_raw, at = part(8192, 2, BT, HD)
        scales_raw, at = part(at, 4, HD)
        w_raw_a, at = part(8192, DC, 3 * D)
        w_out_a_sb, at = part(at, DC, D)
        qkT, at = part(at, 2 * DC, SEQ)
        v_a, at = part(at, BT, D)
        p_a, at = part(at, 2, SEQ)
        pT_a, at = part(at, BT, SEQ)
        ctxT, at = part(at, DC, SEQ)
        b_out_sb, at = part(at, D)
        yT, at = part(14336, DC, TOK)
        gated, at = part(at, 2, SEQ)
        upc, at = part(at, 2, SEQ)
        hid, at = part(at, 2, SEQ)
        route, at = part(at, 6, TILES, E)
        assert at <= OVER
        matches, _ = part(14336 + DC * TOK, TILES, E, TOP_K)
        comb_sb, _ = part(13312, 2, SEQ)
        picked = sb("picked", [P, TILES, E], BF16)
        gates = sb("gates", [P, TILES, 3 * GATES], BF16)
        expert_ids = sb("expert_ids", [P, E])
        top_ids = sb("top_ids", [P, TILES, 8], U32)

        bank = [ctx.enter_context(nc.psum_tensor(f"bank{k}", [P, 512], F32)) for k in range(8)]

        x_loaded = sem("x_loaded")
        ids_ready = sem("ids_ready")
        identity_ready = sem("identity_ready")
        const_loaded = sem("const_loaded")
        wa_loaded = sem("wa_loaded")
        wo_a_loaded = sem("wo_a_loaded")
        wb_loaded = sem("wb_loaded")
        rope_loaded = sem("rope_loaded")
        stored = sem("stored")

        def phase(prefix, names):
            return {n: sem(f"{prefix}_{n}") for n in names.split()}

        a = phase("a", "step xn xnT xhi xlo whi wlo qk_mm qk v_mm v s_mm max exp p pt_mm pt ctx_mm ctx"
                       " o_mm x bias")
        f = [phase(f"f{k}", "step xn xnT xhi xlo logits_mm logit exp picked pos_mm gates combT_mm combT"
                            " whi wlo g_mm u_mm c_mm silu comb upc hid hhi hlo d_mm raw0 raw1 sel0 sel1 y0 y1 yt_mm x")
             for k in range(2)]
        bb = phase("b", "step xn xnT xhi xlo whi wlo tab proj sq rot_a rot_b sum rk rot krot t_mm t v"
                        " s_mm max exp p pt_mm pt e_mm e o_mm x")
        block = ctx.enter_context(nc.Block())

        def split(t, n):
            return t.rearrange("p (c n) -> p c n", c=n)

        def rsqrt(steps, value, eps, scale, n):
            v, y, t = (rstd[:, k, 0:n] for k in (2, 0, 1))
            steps.did(nc.vector.tensor_scalar(v, value, scale, eps, ALU.mult, ALU.add))
            steps.wait()
            steps.did(nc.vector.tensor_scalar(t.bitcast(I32), v.bitcast(I32), 1, None,
                                              ALU.logical_shift_right))
            steps.wait()
            steps.did(nc.vector.tensor_scalar(y.bitcast(I32), t.bitcast(I32), -1.0, RSQRT_MAGIC,
                                              ALU.mult, ALU.add))
            for _ in range(3):
                steps.wait()
                steps.did(nc.vector.scalar_tensor_tensor(t, v, -0.5, y, ALU.mult, ALU.mult))
                steps.wait()
                steps.did(nc.vector.tensor_tensor(t, t, y, ALU.mult))
                steps.wait()
                steps.did(nc.vector.scalar_tensor_tensor(y, t, 1.5, y, ALU.add, ALU.mult))
            steps.wait()

        def normalise(steps, first, ready):
            tiles = [x_tok[:, bass.ds(first + i, 1), :].rearrange("p o d -> p (o d)") for i in range(BT)]
            for i in range(BT):
                steps.did(nc.vector.bn_stats(stats[:, i, :], tiles[i]))
            steps.wait()
            nc.vector.memset(turn[:, :], 0.0)
            for i in range(BT):
                steps.did(nc.vector.bn_aggr(mean_var[:, i, :], stats[:, i, :]))
            steps.wait()
            rsqrt(steps, mean_var[:, :, 1], EPS_LN, 1.0, BT)
            for i in range(BT):
                nc.vector.tensor_scalar(xn[:, i, :], tiles[i], mean_var[:, i, 0:1], rstd[:, 0, i:i + 1],
                                        ALU.subtract, ALU.mult).then_inc(ready, 1)

        def transpose_batch(done):
            for c in range(DC):
                for i in range(BT):
                    last = nc.tensor.transpose(bank[c][:, i * P:(i + 1) * P], xn[:, i, c * P:(c + 1) * P],
                                               identity[:, :])
                last.then_inc(done, 1)

        def matmul3(out, hi, lo, rhs_hi, rhs_lo, start, stop):
            nc.tensor.matmul(out, hi, rhs_lo, start=start, stop=False)
            nc.tensor.matmul(out, lo, rhs_hi, start=False, stop=False)
            return nc.tensor.matmul(out, hi, rhs_hi, start=False, stop=stop)

        wa_hi = halves[:, 0, 0:DC * 3 * D].rearrange("p (c n) -> p c n", c=DC)
        wa_lo = halves[:, 1, 0:DC * 3 * D].rearrange("p (c n) -> p c n", c=DC)
        wb_hi = halves[:, 0, :].rearrange("p (c n) -> p c n", c=DC)
        wb_lo = halves[:, 1, :].rearrange("p (c n) -> p c n", c=DC)
        wf_hi = halves[:, 0, 0:2 * SW].rearrange("p (k n) -> p k n", k=2)
        wf_lo = halves[:, 1, 0:2 * SW].rearrange("p (k n) -> p k n", k=2)
        h_hi = halves[:, 0, 2 * SW:2 * SW + 2 * SEQ].rearrange("p (k n) -> p k n", k=2)
        h_lo = halves[:, 1, 2 * SW:2 * SW + 2 * SEQ].rearrange("p (k n) -> p k n", k=2)

        def ffn_loads(sp, s):
            raws, sels = (s["raw0"], s["raw1"]), (s["sel0"], s["sel1"])
            for par in range(2):
                sp.dma_start(raw[:, par, :], w_moe[par]).then_inc(raws[par], 16)
                sp.dma_start(sel[:, par, :].bitcast(U16), select_in[par]).then_inc(sels[par], 16)

            def load(j, par):
                sp.wait_ge(s["whi"], j - 1)
                sp.wait_ge(s["wlo"], j - 1)
                sp.dma_start(raw[:, par, :], w_moe[bass.ds(j, 1)].rearrange("o p n -> p (o n)")) \
                    .then_inc(raws[par], 16)
                sp.wait_ge(s["c_mm"], 2 * j - 2)
                sp.dma_start(sel[:, par, :].bitcast(U16), select_in[bass.ds(j, 1)].rearrange("o p n -> p (o n)")) \
                    .then_inc(sels[par], 16)

            with sp.Fori(1, HT // 2) as k:
                load(2 * k, 0)
                load(2 * k + 1, 1)
            load(HT - 1, 0)

        @block.sync
        def _(sp):
            xv = x_in.rearrange("(b i p) d -> b p i d", b=BATCHES, p=P)
            for b in range(BATCHES):
                sp.dma_start(x_tok[:, b * BT:(b + 1) * BT, :], xv[b]).then_inc(x_loaded, 16)
            sp.dma_start(identity[:, :], identity_in).then_inc(const_loaded, 16)
            sp.dma_start(w_raw_a[:, :, :], w_qkv_a.rearrange("(c p) n -> p c n", p=P)).then_inc(wa_loaded, 16)
            sp.dma_start(b_qkv_sb[:, :], b_qkv_a).then_inc(wa_loaded, 16)
            sp.dma_start(w_out_a_sb[:, :, :], w_out_a.rearrange("(c p) n -> p c n", p=P)) \
                .then_inc(wo_a_loaded, 16)
            sp.dma_start(b_out_sb, b_out_a.partition_broadcast(P)).then_inc(wo_a_loaded, 16)
            sp.dma_start(before[:, :, :].bitcast(U16), before_in).then_inc(const_loaded, 16)
            sp.dma_start(mask[:, :, :], mask_in).then_inc(const_loaded, 16)
            sp.dma_start(w_router_sb[:, :, :], w_router.rearrange("(c p) n -> p c n", p=P)) \
                .then_inc(const_loaded, 16)
            sp.dma_start(w_out_b_sb[:, :, :], w_out_b.rearrange("n p d -> p n d")).then_inc(wb_loaded, 16)
            ffn_loads(sp, f[0])
            sp.wait_ge(a["x"], 2 * BATCHES)
            sp.dma_start(w_raw_b, w_qkv_b.rearrange("p c n -> p (c n)")).then_inc(wb_loaded, 16)
            sp.dma_start(rope_raw, rope_in).then_inc(rope_loaded, 16)
            for k, s in enumerate((q_scale, k_scale)):
                sp.dma_start(scales_raw[:, 2 * k, :], s.partition_broadcast(P)).then_inc(rope_loaded, 16)
                for half in range(2):
                    sp.dma_start(scales_raw[:, 2 * k + 1, half * HD // 2:(half + 1) * HD // 2],
                                 s[(1 - half) * HD // 2:(2 - half) * HD // 2].partition_broadcast(P)) \
                        .then_inc(rope_loaded, 16)
            sp.wait_ge(f[0]["whi"], HT)
            sp.wait_ge(f[0]["wlo"], HT)
            sp.wait_ge(f[0]["c_mm"], 2 * HT)
            ffn_loads(sp, f[1])
            sp.wait_ge(f[1]["x"], TILES // 2)
            ov = out.rearrange("(b i p) d -> b p i d", b=BATCHES, p=P)
            for b in range(BATCHES):
                sp.dma_start(ov[b], x_tok[:, b * BT:(b + 1) * BT, :]).then_inc(stored, 16)
            sp.wait_ge(stored, 16 * BATCHES)

        def attention_a_pe(pe):
            pe.wait_ge(const_loaded, 64)
            pe.wait_ge(a["whi"], 1)
            pe.wait_ge(a["wlo"], 1)
            pe.wait_ge(wo_a_loaded, 32)
            with pe.Fori(0, BATCHES) as b:
                pe.wait_ge(a["xn"], BT * b + BT)
                transpose_batch(a["xnT"])
                pe.wait_ge(a["xhi"], DC * b + DC)
                pe.wait_ge(a["xlo"], DC * b + DC)
                for m in range(2 * DC):
                    for c in range(DC):
                        last = matmul3(bank[2 + m][:, :], wa_hi[:, c, m * P:(m + 1) * P],
                                       wa_lo[:, c, m * P:(m + 1) * P], xT_hi[:, c, 0:SEQ], xT_lo[:, c, 0:SEQ],
                                       c == 0, c == DC - 1)
                    last.then_inc(a["qk_mm"], 1)
                for i in range(BT):
                    for c in range(DC):
                        last = matmul3(bank[6 + i // 2][:, (i % 2) * D:(i % 2 + 1) * D],
                                       xT_hi[:, c, i * P:(i + 1) * P], xT_lo[:, c, i * P:(i + 1) * P],
                                       wa_hi[:, c, 2 * D:3 * D], wa_lo[:, c, 2 * D:3 * D],
                                       c == 0, c == DC - 1)
                    if i % 2:
                        last.then_inc(a["v_mm"], 1)
                pe.wait_ge(a["qk"], 2 * DC * b + 2 * DC)

                def scores(q):
                    if q >= 2:
                        pe.wait_ge(a["exp"], BT * b + q - 1)
                    for c in range(DC):
                        last = nc.tensor.matmul(bank[q % 2][:, :], qkT[:, c, q * P:(q + 1) * P],
                                                qkT[:, DC + c, :], start=c == 0, stop=c == DC - 1)
                    last.then_inc(a["s_mm"], 1)

                def probs_transposed(q):
                    pe.wait_ge(a["p"], BT * b + q + 1)
                    if q >= 2:
                        pe.wait_ge(a["pt"], BT * b + q - 1)
                    for k in range(BT):
                        last = nc.tensor.transpose(bank[2 + q % 2][:, k * P:(k + 1) * P],
                                                   p_a[:, q % 2, k * P:(k + 1) * P], identity[:, :])
                    last.then_inc(a["pt_mm"], 1)

                scores(0)
                for q in range(1, BT):
                    scores(q)
                    probs_transposed(q - 1)
                probs_transposed(BT - 1)
                pe.wait_ge(a["pt"], BT * b + BT)
                pe.wait_ge(a["v"], 2 * b + 2)
                for m in range(DC):
                    for k in range(BT):
                        last = nc.tensor.matmul(bank[4 + m][:, :], v_a[:, k, m * P:(m + 1) * P], pT_a[:, k, :],
                                                start=k == 0, stop=k == BT - 1)
                    last.then_inc(a["ctx_mm"], 1)
                pe.wait_ge(a["ctx"], DC * b + DC)
                for i in range(BT):
                    for c in range(DC):
                        last = nc.tensor.matmul(bank[6 + i // 2][:, (i % 2) * D:(i % 2 + 1) * D],
                                                ctxT[:, c, i * P:(i + 1) * P], w_out_a_sb[:, c, :],
                                                start=c == 0, stop=c == DC - 1)
                    if i % 2:
                        last.then_inc(a["o_mm"], 1)

        def ffn_pe(pe, s):
            for hb in range(BATCHES):
                pe.wait_ge(s["xn"], BT * (hb + 1))
                if hb:
                    pe.wait_ge(s["xhi"], DC * hb)
                    pe.wait_ge(s["xlo"], DC * hb)
                transpose_batch(s["xnT"])
            for i in range(TILES):
                hb = i // BT
                if i % BT == 0:
                    pe.wait_ge(s["xhi"], DC * (hb + 1))
                    pe.wait_ge(s["xlo"], DC * (hb + 1))
                for n, half in enumerate((xT_lo, xT_hi)):
                    for c in range(DC):
                        last = nc.tensor.matmul(bank[2][:, i * E:(i + 1) * E],
                                                half[:, c, i * P:(i + 1) * P].bitcast(F32),
                                                w_router_sb[:, c, :], start=n + c == 0, stop=n + c == 2)
            last.then_inc(s["logits_mm"], 1)
            pe.wait_ge(s["picked"], 1)
            for i in range(TILES):
                for k in range(i + 1):
                    last = nc.tensor.matmul(bank[3][:, i * E:(i + 1) * E], before[:, 0 if k == i else 1, :],
                                            picked[:, k, :], start=k == 0, stop=k == i)
            last.then_inc(s["pos_mm"], 1)
            pe.wait_ge(identity_ready, 1)
            pe.wait_ge(s["gates"], 1)
            for i in range(TILES):
                last = nc.tensor.transpose(bank[7][:, :].bitcast(BF16)[0:3 * GATES, i * P:(i + 1) * P],
                                           gates[:, i, :], identity_bf[:, :])
            last.then_inc(s["combT_mm"], 1)

            def up(k, par, h, unit=None):
                j = 2 * k + par
                u = 2 * j + h
                tok = slice(h * SEQ, (h + 1) * SEQ)
                if h == 0:
                    pe.wait_ge(s["whi"], j + 1)
                    pe.wait_ge(s["wlo"], j + 1)
                if unit is None or unit >= 2:
                    pe.wait_ge(s["silu"], u - 1)
                for c in range(DC):
                    w = slice(c * P, (c + 1) * P)
                    last = matmul3(bank[4 + 3 * h][:, :], wf_hi[:, par, w], wf_lo[:, par, w],
                                   xT_hi[:, c, tok], xT_lo[:, c, tok], c == 0, c == DC - 1)
                last.then_inc(s["g_mm"], 1)
                if unit is None or unit >= 1:
                    pe.wait_ge(s["upc"], u)
                for c in range(DC):
                    w = slice(D + c * P, D + (c + 1) * P)
                    last = matmul3(bank[5][:, :], wf_hi[:, par, w], wf_lo[:, par, w],
                                   xT_hi[:, c, tok], xT_lo[:, c, tok], c == 0, c == DC - 1)
                last.then_inc(s["u_mm"], 1)
                if h == 0:
                    pe.wait_ge((s["sel0"], s["sel1"])[par], 16 * k + 16)
                if unit is None or unit >= 1:
                    pe.wait_ge(s["comb"], u)
                nc.tensor.matmul(bank[6][:, :], sel[:, par, :], combT[:, tok], start=True, stop=True) \
                    .then_inc(s["c_mm"], 1)

            def down(j, par, h, first=False, end=False):
                u = 2 * j + h
                pe.wait_ge(s["hhi"], u + 1)
                pe.wait_ge(s["hlo"], u + 1)
                for m in range(DC):
                    w = slice(2 * D + m * P, 2 * D + (m + 1) * P)
                    last = matmul3(bank[2 * h + m][:, :], wf_hi[:, par, w], wf_lo[:, par, w],
                                   h_hi[:, h, :], h_lo[:, h, :], first, end)
                last.then_inc(s["d_mm"], 1)

            pe.wait_ge(s["combT"], 1)
            up(0, 0, 0, unit=0)
            up(0, 0, 1, unit=1)
            down(0, 0, 0, first=True)
            up(0, 1, 0, unit=2)
            down(0, 0, 1, first=True)
            up(0, 1, 1, unit=3)
            down(1, 1, 0)
            with pe.Fori(1, HT // 2) as k:
                for par in range(2):
                    up(k, par, 0)
                    down(2 * k + par - 1, 1 - par, 1)
                    up(k, par, 1)
                    down(2 * k + par, par, 0)
            up(HT // 2, 0, 0)
            down(HT - 2, 1, 1)
            up(HT // 2, 0, 1)
            down(HT - 1, 0, 0, end=True)
            down(HT - 1, 0, 1, end=True)
            for i in range(TILES):
                if i % BT == 0:
                    pe.wait_ge(s["y0"], i // BT + 1)
                    pe.wait_ge(s["y1"], i // BT + 1)
                for m in range(DC):
                    last = nc.tensor.transpose(bank[4 + i // 2][:, (i % 2) * D + m * P:(i % 2) * D + (m + 1) * P],
                                               yT[:, m, i * P:(i + 1) * P], identity[:, :])
                if i % 2:
                    last.then_inc(s["yt_mm"], 1)

        def attention_b_pe(pe):
            pe.wait_ge(bb["whi"], DC)
            pe.wait_ge(bb["wlo"], DC)
            pe.wait_ge(wb_loaded, 32)
            with pe.Fori(0, BATCHES) as b:
                pe.wait_ge(bb["xn"], BT * b + BT)
                transpose_batch(bb["xnT"])
                pe.wait_ge(bb["xhi"], DC * b + DC)
                pe.wait_ge(bb["xlo"], DC * b + DC)

                def project(i, c):
                    n = CHUNKS * i + c
                    if n >= 2:
                        prev = CHUNKS * ((n - 2) // CHUNKS), (n - 2) % CHUNKS
                        if prev[1] < K_CHUNKS + Q_CHUNKS:
                            done = (K_CHUNKS + Q_CHUNKS) * (prev[0] // CHUNKS) + prev[1] + 1
                            pe.wait_ge(bb["sq"], (K_CHUNKS + Q_CHUNKS) * BT * b + done)
                            pe.wait_ge(bb["rot_b"], (K_CHUNKS + Q_CHUNKS) * BT * b + done)
                        else:
                            pe.wait_ge(bb["v"], K_CHUNKS * BT * b + K_CHUNKS * (prev[0] // CHUNKS)
                                       + prev[1] - K_CHUNKS - Q_CHUNKS + 1)
                    w = slice(c * CH * HD, (c + 1) * CH * HD)
                    for k in range(DC):
                        t = slice(i * P, (i + 1) * P)
                        last = matmul3(bank[n % 2][:, :], xT_hi[:, k, t], xT_lo[:, k, t], wb_hi[:, k, w],
                                       wb_lo[:, k, w], k == 0, k == DC - 1)
                    last.then_inc(bb["proj"], 1)

                def transposed(i, c):
                    n = (K_CHUNKS + Q_CHUNKS) * i + c
                    base = (K_CHUNKS + Q_CHUNKS) * BT * b
                    if c < K_CHUNKS:
                        pe.wait_ge(bb["krot"], K_CHUNKS * BT * b + K_CHUNKS * i + c + 1)
                    else:
                        pe.wait_ge(bb["rot"], base + n + 1)
                    if n >= 1:
                        pe.wait_ge(bb["t"], base + n)
                    if c == 0 and i >= 2:
                        pe.wait_ge(bb["x"], BT * b + i - 1)
                    for k in range(CH):
                        last = nc.tensor.transpose(bank[2][:, k * P:(k + 1) * P], roped[:, c % 2, k, :],
                                                   identity[:, :])
                    last.then_inc(bb["t_mm"], 1)

                def scores(i, g):
                    n = NKV * i + g
                    base = NKV * BT * b
                    if g == 0:
                        pe.wait_ge(bb["t"], (K_CHUNKS + Q_CHUNKS) * (BT * b + i + 1))
                    if n >= 2:
                        pe.wait_ge(bb["max"], base + n - 1)
                    for h in range(2):
                        for k in range(2) if i else (1,):
                            last = nc.tensor.matmul(bank[5 + n % 2][:, (2 * h + k) * P:(2 * h + k + 1) * P],
                                                    qT[:, i % 2, 2 * g + h, :], kT[:, (i - 1 + k) % 3, g, :],
                                                    start=True, stop=True)
                    last.then_inc(bb["s_mm"], 1)

                def probs_transposed(i, g):
                    n = NKV * i + g
                    base = NKV * BT * b
                    pe.wait_ge(bb["p"], base + n + 1)
                    if n >= 2:
                        pe.wait_ge(bb["pt"], base + n - 1)
                    for k in range(2) if i else (1,):
                        for h in range(2):
                            last = nc.tensor.transpose(bank[3 + n % 2][:, (2 * k + h) * P:(2 * k + h + 1) * P],
                                                       p_b[:, n % 2, h, k * P:(k + 1) * P], identity[:, :])
                    last.then_inc(bb["pt_mm"], 1)

                def encode(i, g):
                    n = NKV * i + g
                    base = NKV * BT * b
                    pe.wait_ge(bb["pt"], base + n + 1)
                    if g == 0:
                        pe.wait_ge(bb["v"], K_CHUNKS * (BT * b + i + 1))
                    if n >= 1:
                        pe.wait_ge(bb["e"], base + n)
                    for k in range(2) if i else (1,):
                        last = nc.tensor.matmul(bank[7][:, (g % 2) * D:(g % 2 + 1) * D],
                                                v_b[:, (i - 1 + k) % 3, g * HD:(g + 1) * HD],
                                                pT_b[:, n % 2, k, :], start=(k == 0 or i == 0), stop=k == 1)
                    last.then_inc(bb["e_mm"], 1)

                for c in range(CHUNKS):
                    project(0, c)
                    if 2 <= c:
                        transposed(0, c - 2)
                scores(0, 0)
                for i in range(BT):
                    for g in range(NKV):
                        if g + 1 < NKV:
                            scores(i, g + 1)
                        if i + 1 < BT:
                            project(i + 1, g)
                        probs_transposed(i, g)
                        if g:
                            encode(i, g - 1)
                        if i + 1 < BT and g >= 2:
                            transposed(i + 1, g - 2)
                    encode(i, NKV - 1)
                    if i + 1 < BT:
                        scores(i + 1, 0)
                    pe.wait_ge(bb["e"], NKV * (BT * b + i + 1))
                    if i == BT - 1:
                        pe.wait_ge(bb["x"], BT * b + i)
                    for n in range(NQ):
                        last = nc.tensor.matmul(bank[2][:, 0:D], encT[:, n, :], w_out_b_sb[:, n, :],
                                                start=n == 0, stop=n == NQ - 1)
                    last.then_inc(bb["o_mm"], 1)

        @block.tensor
        def _(pe):
            attention_a_pe(pe)
            ffn_pe(pe, f[0])
            attention_b_pe(pe)
            ffn_pe(pe, f[1])

        def attention_a_act(act):
            act.wait_ge(wa_loaded, 32)
            nc.scalar.activation(wa_hi, w_raw_a, ACT.Copy).then_inc(a["whi"], 1)
            with act.Fori(0, BATCHES) as b:
                for c in range(DC):
                    act.wait_ge(a["xnT"], DC * b + c + 1)
                    nc.scalar.activation(xT_hi[:, c, 0:SEQ], bank[c][:, :], ACT.Copy).then_inc(a["xhi"], 1)
                for m in range(2 * DC):
                    act.wait_ge(a["qk_mm"], 2 * DC * b + m + 1)
                    nc.scalar.activation(qkT[:, m, :], bank[2 + m][:, :], ACT.Identity,
                                         bias=b_qkv_sb[:, m:m + 1]).then_inc(a["qk"], 1)

                def exponentials(q):
                    act.wait_ge(a["max"], BT * b + q + 1)
                    if q >= 2:
                        act.wait_ge(a["pt_mm"], BT * b + q - 1)
                    nc.scalar.activation(p_a[:, q % 2, :], bank[q % 2][:, :], ACT.Exp, bias=nb[:, q, 0:1],
                                         scale=1.0 / 16.0, accum_out=lsum[:, q, 0:1]).then_inc(a["exp"], 1)

                def copy_probs(q):
                    act.wait_ge(a["pt_mm"], BT * b + q + 1)
                    nc.scalar.activation(pT_a[:, :, q * P:(q + 1) * P], split(bank[2 + q % 2][:, :], BT),
                                         ACT.Copy).then_inc(a["pt"], 1)

                exponentials(0)
                for q in range(1, BT):
                    exponentials(q)
                    copy_probs(q - 1)
                copy_probs(BT - 1)
                for m in range(DC):
                    act.wait_ge(a["ctx_mm"], DC * b + m + 1)
                    nc.scalar.activation(ctxT[:, m, :], bank[4 + m][:, :], ACT.Identity,
                                         bias=b_qkv_sb[:, 2 * DC + m:2 * DC + m + 1]).then_inc(a["ctx"], 1)

        def ffn_act(act, s):
            for hb in range(BATCHES):
                for c in range(DC):
                    act.wait_ge(s["xnT"], DC * hb + c + 1)
                    nc.scalar.activation(xT_hi[:, c, hb * SEQ:(hb + 1) * SEQ], bank[c][:, :], ACT.Copy) \
                        .then_inc(s["xhi"], 1)
            act.wait_ge(s["logit"], 1)
            nc.scalar.activation(route[:, 1], route[:, 0], ACT.Exp).then_inc(s["exp"], 1)

            def weights(k, par):
                act.wait_ge((s["raw0"], s["raw1"])[par], 16 * k + 16)
                nc.scalar.activation(wf_hi[:, par, :], raw[:, par, :], ACT.Copy).then_inc(s["whi"], 1)

            weights(0, 0)
            weights(0, 1)
            act.wait_ge(s["combT_mm"], 1)
            nc.scalar.activation(combT[:, :], bank[7][:, :].bitcast(BF16)[0:3 * GATES, :], ACT.Copy) \
                .then_inc(s["combT"], 1)

            def unit(j, h, number=None):
                u = 2 * j + h
                late = number is None or number >= 2
                act.wait_ge(s["g_mm"], u + 1)
                if late:
                    act.wait_ge(s["hid"], u - 1)
                nc.scalar.activation(gated[:, h, :], bank[4 + 3 * h][:, :], ACT.Silu).then_inc(s["silu"], 1)
                act.wait_ge(s["c_mm"], u + 1)
                if late:
                    act.wait_ge(s["upc"], u - 1)
                nc.scalar.activation(comb_sb[:, h, :], bank[6][:, :], ACT.Copy).then_inc(s["comb"], 1)
                act.wait_ge(s["hid"], u + 1)
                if late:
                    act.wait_ge(s["d_mm"], u - 1)
                nc.scalar.activation(h_hi[:, h, :], hid[:, h, :], ACT.Copy).then_inc(s["hhi"], 1)

            def tile(k, par, number=None, more=True):
                j = 2 * k + par
                unit(j, 0, None if number is None else 2 * number)
                if more:
                    act.wait_ge(s["d_mm"], 2 * j)
                    weights(k + par, 1 - par)
                unit(j, 1, None if number is None else 2 * number + 1)

            tile(0, 0, number=0, more=False)
            tile(0, 1, number=1)
            with act.Fori(1, HT // 2) as k:
                for par in range(2):
                    tile(k, par)
            tile(HT // 2, 0, more=False)
            for h in range(2):
                act.wait_ge(s["d_mm"], 2 * (HT - 1) + h + 1)
                nc.scalar.activation(yT[:, 0, h * SEQ:(h + 1) * SEQ], bank[2 * h][:, :], ACT.Copy) \
                    .then_inc(s["y0"], 1)

        def attention_b_act(act):
            act.wait_ge(wb_loaded, 32)
            w_raw = split(w_raw_b, DC)
            for c in range(DC):
                nc.scalar.activation(wb_hi[:, c, :], w_raw[:, c, :], ACT.Copy).then_inc(bb["whi"], 1)
            with act.Fori(0, BATCHES) as b:
                for c in range(DC):
                    act.wait_ge(bb["xnT"], DC * b + c + 1)
                    nc.scalar.activation(xT_hi[:, c, 0:SEQ], bank[c][:, :], ACT.Copy).then_inc(bb["xhi"], 1)

                def square(i, c):
                    act.wait_ge(bb["proj"], CHUNKS * (BT * b + i) + c + 1)
                    src = bank[c % 2][:, :]
                    if c < K_CHUNKS + Q_CHUNKS:
                        n = (K_CHUNKS + Q_CHUNKS) * i + c
                        if n >= 2:
                            act.wait_ge(bb["sum"], (K_CHUNKS + Q_CHUNKS) * BT * b + n - 1)
                        nc.scalar.activation(squares[:, c % 2, :], src, ACT.Square).then_inc(bb["sq"], 1)
                    else:
                        k = (c - K_CHUNKS - Q_CHUNKS) * CH * HD
                        nc.scalar.activation(v_b[:, i % 3, k:k + CH * HD], src, ACT.Copy).then_inc(bb["v"], 1)

                def copy_transposed(i, c):
                    act.wait_ge(bb["t_mm"], (K_CHUNKS + Q_CHUNKS) * (BT * b + i) + c + 1)
                    if c < K_CHUNKS:
                        dst = kT[:, i % 3, c * CH:(c + 1) * CH, :]
                    else:
                        dst = qT[:, i % 2, (c - K_CHUNKS) * CH:(c - K_CHUNKS + 1) * CH, :]
                    nc.scalar.activation(dst, split(bank[2][:, :], CH), ACT.Copy).then_inc(bb["t"], 1)

                def exponentials(i, g):
                    n = NKV * i + g
                    keys = slice(0 if i else P, 2 * P)
                    act.wait_ge(bb["max"], NKV * BT * b + n + 1)
                    if n >= 2:
                        act.wait_ge(bb["pt_mm"], NKV * BT * b + n - 1)
                    for h in range(2):
                        last = nc.scalar.activation(p_b[:, n % 2, h, keys], s_b[:, n % 2, h, keys], ACT.Exp,
                                                    bias=nb[:, n % 4, h:h + 1],
                                                    scale=rqs[:, i % 2, 2 * g + h:2 * g + h + 1],
                                                    accum_out=lsum[:, n % 4, h:h + 1])
                    last.then_inc(bb["exp"], 1)

                def copy_probs(i, g):
                    n = NKV * i + g
                    act.wait_ge(bb["pt_mm"], NKV * BT * b + n + 1)
                    if n >= 2:
                        act.wait_ge(bb["e_mm"], NKV * BT * b + n - 1)
                    k = slice(0 if i else 1, 2)
                    nc.scalar.activation(pT_b[:, n % 2, k, :], split(bank[3 + n % 2][:, :], 2)[:, k, :],
                                         ACT.Copy).then_inc(bb["pt"], 1)

                def copy_encoded(i, g):
                    act.wait_ge(bb["e_mm"], NKV * (BT * b + i) + g + 1)
                    if g == 0 and i:
                        act.wait_ge(bb["o_mm"], BT * b + i)
                    nc.scalar.activation(encT[:, 2 * g:2 * g + 2, :],
                                         split(bank[7][:, (g % 2) * D:(g % 2 + 1) * D], 2),
                                         ACT.Copy).then_inc(bb["e"], 1)

                for c in range(CHUNKS):
                    square(0, c)
                    if c >= 2:
                        copy_transposed(0, c - 2)
                exponentials(0, 0)
                for i in range(BT):
                    for g in range(NKV):
                        if g + 1 < NKV:
                            exponentials(i, g + 1)
                        if i + 1 < BT:
                            square(i + 1, g)
                        copy_probs(i, g)
                        if g:
                            copy_encoded(i, g - 1)
                        if i + 1 < BT and g >= 2:
                            copy_transposed(i + 1, g - 2)
                    copy_encoded(i, NKV - 1)
                    if i + 1 < BT:
                        exponentials(i + 1, 0)

        @block.scalar
        def _(act):
            attention_a_act(act)
            ffn_act(act, f[0])
            attention_b_act(act)
            ffn_act(act, f[1])

        def spread(t, n):
            return t.unsqueeze(2).to_broadcast([P, t.shape[1], n])

        def attention_a_dve(dve):
            dve.wait_ge(const_loaded, 64)
            nc.vector.tensor_copy(identity_bf[:, :], identity[:, :]).then_inc(identity_ready, 1)
            dve.wait_ge(a["whi"], 1)
            nc.vector.tensor_tensor(wa_lo, w_raw_a, wa_hi.bitcast(F32), ALU.subtract).then_inc(a["wlo"], 1)
            dve.wait_ge(x_loaded, 16 * BATCHES)
            with dve.Fori(0, BATCHES) as b:
                steps = Steps(dve, a["step"], b * STEPS_A)
                normalise(steps, BT * b, a["xn"])
                for c in range(DC):
                    dve.wait_ge(a["xhi"], DC * b + c + 1)
                    nc.vector.tensor_tensor(xT_lo[:, c, 0:SEQ], bank[c][:, :], xT_hi[:, c, 0:SEQ].bitcast(F32),
                                            ALU.subtract).then_inc(a["xlo"], 1)
                for k in range(2):
                    dve.wait_ge(a["v_mm"], 2 * b + k + 1)
                    nc.vector.tensor_copy(v_a[:, 2 * k:2 * k + 2, :], split(bank[6 + k][:, :], 2)) \
                        .then_inc(a["v"], 1)

                def maximum(q):
                    dve.wait_ge(a["s_mm"], BT * b + q + 1)
                    steps.did(nc.vector.reduce_max(mx[:, q, 0:1], bank[q % 2][:, :], axis=X))
                    steps.wait()
                    nc.vector.tensor_scalar(nb[:, q, 0:1], mx[:, q, 0:1], -1.0 / 16.0, None, ALU.mult) \
                        .then_inc(a["max"], 1)

                def probabilities(q):
                    dve.wait_ge(a["exp"], BT * b + q + 1)
                    steps.did(nc.vector.reciprocal(rl[:, q, 0:1], lsum[:, q, 0:1]))
                    steps.wait()
                    nc.vector.tensor_scalar(p_a[:, q % 2, :], p_a[:, q % 2, :], rl[:, q, 0:1], None, ALU.mult) \
                        .then_inc(a["p"], 1)

                maximum(0)
                for q in range(1, BT):
                    maximum(q)
                    probabilities(q - 1)
                probabilities(BT - 1)
                dve.wait_ge(a["bias"], b + 1)
                for k in range(2):
                    dve.wait_ge(a["o_mm"], 2 * b + k + 1)
                    xt = x_tok[:, bass.ds(BT * b + 2 * k, 2), :]
                    nc.vector.tensor_tensor(xt, xt, split(bank[6 + k][:, :], 2), ALU.add).then_inc(a["x"], 1)
                assert steps.n == STEPS_A, steps.n

        def ffn_dve(dve, s, x_ready, x_count):
            steps = Steps(dve, s["step"])
            dve.wait_ge(x_ready, x_count)
            for hb in range(BATCHES):
                if hb:
                    dve.wait_ge(s["xnT"], DC * hb)
                normalise(steps, BT * hb, s["xn"])
                for c in range(DC):
                    dve.wait_ge(s["xhi"], DC * hb + c + 1)
                    tok = slice(hb * SEQ, (hb + 1) * SEQ)
                    nc.vector.tensor_tensor(xT_lo[:, c, tok], bank[c][:, :], xT_hi[:, c, tok].bitcast(F32),
                                            ALU.subtract).then_inc(s["xlo"], 1)

            dve.wait_ge(s["logits_mm"], 1)
            logits = split(bank[2][:, 0:TILES * E], TILES)
            steps.did(nc.vector.reduce_max(small[:, 0, :], logits, axis=X))
            steps.wait()
            nc.vector.tensor_tensor(route[:, 0], logits, spread(small[:, 0, :], E), ALU.subtract) \
                .then_inc(s["logit"], 1)

            def weights(j, par):
                dve.wait_ge(s["whi"], j + 1)
                nc.vector.tensor_tensor(wf_lo[:, par, :], raw[:, par, :], wf_hi[:, par, :].bitcast(F32),
                                        ALU.subtract).then_inc(s["wlo"], 1)

            dve.wait_ge(s["exp"], 1)
            steps.did(nc.vector.reduce_sum(small[:, 1, :], route[:, 1], axis=X))
            steps.wait()
            steps.did(nc.vector.reciprocal(small[:, 2, :], small[:, 1, :]))
            steps.wait()
            steps.did(nc.vector.tensor_tensor(route[:, 2], route[:, 1], spread(small[:, 2, :], E), ALU.mult))
            steps.wait()
            for i in range(TILES):
                steps.did(nc.vector.max(top[:, i, :], route[:, 2, i, :]))
            steps.wait()
            for i in range(TILES):
                steps.did(nc.vector.max_index(top_ids[:, i, :], top[:, i, :], route[:, 2, i, :]))
            steps.did(nc.vector.reduce_sum(small[:, 0, :], top[:, :, 0:TOP_K], axis=X))
            steps.wait()
            steps.did(nc.vector.tensor_scalar(small[:, 1, :], small[:, 0, :], 1e-20, None, ALU.add))
            ids = expert_ids[:, :].unsqueeze(1).unsqueeze(3).to_broadcast([P, TILES, E, TOP_K])
            chosen = top_ids[:, :, 0:TOP_K].unsqueeze(2).to_broadcast([P, TILES, E, TOP_K])
            dve.wait_ge(ids_ready, 1)
            for i in range(TILES):
                steps.did(nc.vector.tensor_tensor(matches[:, i], ids[:, i], chosen[:, i], ALU.is_equal))
            steps.wait()
            steps.did(nc.vector.reciprocal(small[:, 2, :], small[:, 1, :]))
            steps.did(nc.vector.reduce_sum(route[:, 3], matches, axis=X))
            steps.wait()
            nc.vector.tensor_copy(picked[:, :, :], route[:, 3]).then_inc(s["picked"], 1)
            steps.did(nc.vector.tensor_tensor(route[:, 4], route[:, 2], route[:, 3], ALU.mult))
            steps.wait()
            steps.did(nc.vector.tensor_tensor(route[:, 5], route[:, 4], spread(small[:, 2, :], E), ALU.mult))
            steps.did(nc.vector.memset(gates[:, :, E:3 * GATES:GATES], 0.0))
            steps.wait()
            steps.did(nc.vector.memset(gates[:, :, E:E + 1], 1.0))
            dve.wait_ge(s["pos_mm"], 1)
            steps.did(nc.vector.scalar_tensor_tensor(route[:, 4], split(bank[3][:, 0:TILES * E], TILES),
                                                     float(CAP), route[:, 5], ALU.is_lt, ALU.mult))
            rest = route[:, 4]
            for k in range(3):
                piece = gates[:, :, k * GATES:k * GATES + E]
                steps.wait()
                steps.did(nc.vector.tensor_copy(piece, rest))
                if k < 2:
                    steps.wait()
                    steps.did(nc.vector.tensor_tensor(route[:, k], rest, piece, ALU.subtract))
                    rest = route[:, k]
            steps.wait()
            dve.sem_inc(s["gates"], 1)
            weights(0, 0)
            weights(1, 1)

            def unit(j, h, number=None):
                u = 2 * j + h
                late = number is None or number >= 2
                dve.wait_ge(s["u_mm"], u + 1)
                dve.wait_ge(s["comb"], u + 1)
                nc.vector.tensor_tensor(upc[:, h, :], bank[5][:, :], comb_sb[:, h, :], ALU.mult) \
                    .then_inc(s["upc"], 1)
                dve.wait_ge(s["silu"], u + 1)
                dve.wait_ge(s["upc"], u + 1)
                if late:
                    dve.wait_ge(s["hhi"], u - 1)
                nc.vector.tensor_tensor(hid[:, h, :], gated[:, h, :], upc[:, h, :], ALU.mult) \
                    .then_inc(s["hid"], 1)
                dve.wait_ge(s["hhi"], u + 1)
                if late:
                    dve.wait_ge(s["d_mm"], u - 1)
                nc.vector.tensor_tensor(h_lo[:, h, :], hid[:, h, :], h_hi[:, h, :].bitcast(F32),
                                        ALU.subtract).then_inc(s["hlo"], 1)

            def tile(j, par, number=None, more=True):
                unit(j, 0, None if number is None else 2 * number)
                if more:
                    weights(j + 1, 1 - par)
                unit(j, 1, None if number is None else 2 * number + 1)

            tile(0, 0, number=0, more=False)
            tile(1, 1, number=1)
            with dve.Fori(2, HT - 1, 2) as j:
                for par in range(2):
                    tile(j + par, par)
            tile(HT - 1, 0, more=False)
            for h in range(2):
                dve.wait_ge(s["d_mm"], 2 * (HT - 1) + h + 1)
                nc.vector.tensor_copy(yT[:, 1, h * SEQ:(h + 1) * SEQ], bank[2 * h + 1][:, :]) \
                    .then_inc(s["y1"], 1)
            for k in range(TILES // 2):
                dve.wait_ge(s["yt_mm"], k + 1)
                xt = x_tok[:, 2 * k:2 * k + 2, :]
                nc.vector.tensor_tensor(xt, xt, split(bank[4 + k][:, :], 2), ALU.add).then_inc(s["x"], 1)

        def attention_b_dve(dve):
            w_raw = split(w_raw_b, DC)
            for c in range(DC):
                dve.wait_ge(bb["whi"], c + 1)
                nc.vector.tensor_tensor(wb_lo[:, c, :], w_raw[:, c, :], wb_hi[:, c, :].bitcast(F32),
                                        ALU.subtract).then_inc(bb["wlo"], 1)
            dve.wait_ge(f[0]["x"], TILES // 2)
            dve.wait_ge(bb["tab"], 4)
            KQ = K_CHUNKS + Q_CHUNKS
            with dve.Fori(0, BATCHES) as b:
                steps = Steps(dve, bb["step"], b * STEPS_B)
                normalise(steps, BT * b, bb["xn"])
                for c in range(DC):
                    dve.wait_ge(bb["xhi"], DC * b + c + 1)
                    nc.vector.tensor_tensor(xT_lo[:, c, 0:SEQ], bank[c][:, :], xT_hi[:, c, 0:SEQ].bitcast(F32),
                                            ALU.subtract).then_inc(bb["xlo"], 1)

                def rotate(i, c):
                    n = KQ * i + c
                    tab = 2 if c < K_CHUNKS else 0
                    heads = split(bank[c % 2][:, :], CH)
                    dve.wait_ge(bb["sq"], KQ * BT * b + n + 1)
                    if n >= 2:
                        dve.wait_ge(bb["rot"], KQ * BT * b + n - 1)
                    cos = tables[:, tab, i, :].unsqueeze(1).to_broadcast([P, CH, HD])
                    nc.vector.tensor_tensor(rope_a[:, c % 2], heads, cos, ALU.mult).then_inc(bb["rot_a"], 1)
                    for half in range(2):
                        to = slice(half * HD // 2, (half + 1) * HD // 2)
                        of = slice((1 - half) * HD // 2, (2 - half) * HD // 2)
                        sin = tables[:, tab + 1, i, to].unsqueeze(1).to_broadcast([P, CH, HD // 2])
                        last = nc.vector.tensor_tensor(rope_b[:, c % 2, :, to], heads[:, :, of], sin, ALU.mult)
                    last.then_inc(bb["rot_b"], 1)

                def sums(i, c):
                    dve.wait_ge(bb["sq"], KQ * (BT * b + i) + c + 1)
                    nc.vector.reduce_sum(ss[:, i % 2, c * CH:(c + 1) * CH], split(squares[:, c % 2, :], CH),
                                         axis=X).then_inc(bb["sum"], 1)
                    if c == K_CHUNKS - 1:
                        dve.wait_ge(bb["sum"], KQ * (BT * b + i) + c + 1)
                        rsqrt(steps, ss[:, i % 2, 0:NKV], EPS_RMS, 1.0 / HD, NKV)
                        nc.vector.tensor_copy(rk[:, i % 2, :], rstd[:, 0, 0:NKV]).then_inc(bb["rk"], 1)
                    if c == KQ - 1:
                        dve.wait_ge(bb["sum"], KQ * (BT * b + i) + c + 1)
                        rsqrt(steps, ss[:, i % 2, NKV:NKV + NQ], EPS_RMS, 1.0 / HD, NQ)
                        steps.did(nc.vector.tensor_scalar(rqs[:, i % 2, :], rstd[:, 0, 0:NQ], SCALE_B, None,
                                                          ALU.mult))
                        steps.wait()

                def maximum(i, g):
                    n = NKV * i + g
                    keys = slice(0 if i else P, 2 * P)
                    dve.wait_ge(bb["s_mm"], NKV * BT * b + n + 1)
                    nc.vector.memset(turn[:, :], 0.0)
                    for h in range(2):
                        of = slice(2 * P * h + (0 if i else P), 2 * P * (h + 1))
                        steps.did(nc.vector.tensor_tensor_reduce(
                            out=s_b[:, n % 2, h, keys], in0=bank[5 + n % 2][:, of],
                            in1=mask[:, :, :].rearrange("p k s -> p (k s)")[:, keys], scale=1.0, scalar=-3e38,
                            op0=ALU.add, op1=ALU.max, accum_out=mx[:, n % 4, h:h + 1]))
                    steps.wait()
                    nc.vector.scalar_tensor_tensor(nb[:, n % 4, :], mx[:, n % 4, :], -1.0,
                                                   rqs[:, i % 2, 2 * g:2 * g + 2], ALU.mult, ALU.mult) \
                        .then_inc(bb["max"], 1)

                def probabilities(i, g):
                    n = NKV * i + g
                    keys = slice(0 if i else P, 2 * P)
                    dve.wait_ge(bb["exp"], NKV * BT * b + n + 1)
                    steps.did(nc.vector.reciprocal(rl[:, n % 4, :], lsum[:, n % 4, :]))
                    steps.wait()
                    for h in range(2):
                        last = nc.vector.tensor_scalar(p_b[:, n % 2, h, keys], p_b[:, n % 2, h, keys],
                                                       rl[:, n % 4, h:h + 1], None, ALU.mult)
                    last.then_inc(bb["p"], 1)

                for c in range(KQ):
                    rotate(0, c)
                    sums(0, c)
                maximum(0, 0)
                for i in range(BT):
                    for g in range(NKV):
                        probabilities(i, g)
                        if g + 1 < NKV:
                            maximum(i, g + 1)
                        if i + 1 < BT and g < KQ:
                            rotate(i + 1, g)
                            sums(i + 1, g)
                    if i + 1 < BT:
                        maximum(i + 1, 0)
                    dve.wait_ge(bb["o_mm"], BT * b + i + 1)
                    xt = x_tok[:, bass.ds(BT * b + i, 1), :].rearrange("p o d -> p (o d)")
                    nc.vector.tensor_tensor(xt, xt, bank[2][:, 0:D], ALU.add).then_inc(bb["x"], 1)
                assert steps.n == STEPS_B, steps.n

        @block.vector
        def _(dve):
            attention_a_dve(dve)
            ffn_dve(dve, f[0], a["x"], 2 * BATCHES)
            attention_b_dve(dve)
            ffn_dve(dve, f[1], bb["x"], TILES)

        @block.gpsimd
        def _(pool):
            nc.gpsimd.iota(expert_ids[:, :], pattern=[[1, E]], base=0, channel_multiplier=0,
                           allow_small_or_imprecise_dtypes=True).then_inc(ids_ready, 1)
            pool.wait_ge(wo_a_loaded, 32)
            with pool.Fori(0, BATCHES) as b:
                pool.wait_ge(a["xn"], BT * b + BT)
                xt = x_tok[:, bass.ds(BT * b, BT), :]
                nc.gpsimd.tensor_tensor(xt, xt, b_out_sb.unsqueeze(1).to_broadcast([P, BT, D]), ALU.add) \
                    .then_inc(a["bias"], 1)
            pool.wait_ge(rope_loaded, 16 * 7)
            pool.wait_ge(f[0]["x"], TILES // 2)
            for k in range(4):
                nc.gpsimd.tensor_tensor(tables[:, k], rope_raw[:, k % 2],
                                        scales_raw[:, k, :].unsqueeze(1).to_broadcast([P, BT, HD]), ALU.mult) \
                    .then_inc(bb["tab"], 1)
            KQ = K_CHUNKS + Q_CHUNKS
            with pool.Fori(0, BATCHES) as b:
                for i in range(BT):
                    for c in range(KQ):
                        n = KQ * i + c
                        pool.wait_ge(bb["rot_a"], KQ * BT * b + n + 1)
                        pool.wait_ge(bb["rot_b"], KQ * BT * b + n + 1)
                        if n >= 2:
                            pool.wait_ge(bb["t_mm"], KQ * BT * b + n - 1)
                        nc.gpsimd.tensor_tensor(roped[:, c % 2], rope_a[:, c % 2], rope_b[:, c % 2], ALU.add) \
                            .then_inc(bb["rot"], 1)
                        if c == K_CHUNKS - 1:
                            pool.wait_ge(bb["rk"], BT * b + i + 1)
                            pool.wait_ge(bb["rot"], KQ * BT * b + n + 1)
                            for k in range(K_CHUNKS):
                                nc.gpsimd.tensor_tensor(roped[:, k], roped[:, k],
                                                        spread(rk[:, i % 2, k * CH:(k + 1) * CH], HD),
                                                        ALU.mult).then_inc(bb["krot"], 1)


def constants():
    one = np.uint16(0x3F80)
    identity = np.eye(P, dtype=np.float32)
    before = np.stack([np.triu(np.full((P, P), one), 1), np.full((P, P), one)], 1)
    owner = np.minimum(np.arange(HT * P) // F_EXP, E)
    owner = np.where(np.arange(HT * P) < HID, owner, -1).reshape(HT, 1, 1, P)
    select = np.broadcast_to(owner == np.arange(GATES).reshape(1, 1, GATES, 1), (HT, 3, GATES, P))
    select = select.reshape(HT, 3 * GATES, P) * one
    frac = np.arange(0, HD, 2, dtype=np.float32) / HD
    angle = np.arange(SEQ, dtype=np.float32)[:, None] / np.float32(10000.0) ** frac
    cos, sin = np.cos(angle), np.sin(angle)
    rope = np.stack([np.concatenate([cos, cos], 1), np.concatenate([-sin, sin], 1)])
    rope = np.ascontiguousarray(rope.reshape(2, BT, P, HD).transpose(2, 0, 1, 3)).astype(np.float32)
    q, s = np.arange(P)[:, None], np.arange(P)[None, :]
    mask = np.stack([np.where(s > q, 0, MASKED), np.where(s <= q, 0, MASKED)], 1).astype(np.float32)
    return identity, before, select, rope, mask


def kernel(L0_attn_a_hidden_states, L0_attn_a_w_qkv, L0_attn_a_b_qkv, L0_attn_a_w_out, L0_attn_a_b_out,
           L0_attn_b_q_kernel, L0_attn_b_kv_kernel, L0_attn_b_out_kernel, L0_attn_b_q_norm_scale,
           L0_attn_b_k_norm_scale, L0_ffn_wg_router, L0_ffn_w_gate, L0_ffn_w_up, L0_ffn_w_down,
           L0_ffn_ws_gate, L0_ffn_ws_up, L0_ffn_ws_down):
    import concourse.bacc as bacc
    from concourse.bass_utils import run_bass_kernel_spmd

    def arr(t):
        return np.asarray(t)

    x = arr(L0_attn_a_hidden_states)
    kv = arr(L0_attn_b_kv_kernel)
    w_qkv_b = np.concatenate([kv[0], arr(L0_attn_b_q_kernel), kv[1]])
    w_qkv_b = w_qkv_b.transpose(1, 0, 2).reshape(DC, P, QKV_B).transpose(1, 0, 2)

    def hidden_tiles(experts, shared):
        w = np.concatenate([arr(experts).transpose(1, 0, 2).reshape(D, E * F_EXP), arr(shared)], 1)
        w = np.pad(w, ((0, 0), (0, HT * P - HID)))
        return w.reshape(DC, P, HT, P).transpose(2, 1, 0, 3).reshape(HT, P, D)

    w_down = np.concatenate([arr(L0_ffn_w_down).reshape(E * F_EXP, D), arr(L0_ffn_ws_down)])
    w_down = np.pad(w_down, ((0, HT * P - HID), (0, 0))).reshape(HT, P, D)
    w_moe = np.concatenate([hidden_tiles(L0_ffn_w_gate, L0_ffn_ws_gate),
                            hidden_tiles(L0_ffn_w_up, L0_ffn_ws_up), w_down], 2)
    identity, before, select, rope, mask = constants()
    arrays = {
        "x": x.reshape(TOK, D),
        "w_qkv_a": arr(L0_attn_a_w_qkv).T,
        "b_qkv_a": arr(L0_attn_a_b_qkv).reshape(6, P).T,
        "w_out_a": arr(L0_attn_a_w_out).T,
        "b_out_a": arr(L0_attn_a_b_out),
        "w_qkv_b": w_qkv_b,
        "w_out_b": arr(L0_attn_b_out_kernel),
        "q_scale": arr(L0_attn_b_q_norm_scale),
        "k_scale": arr(L0_attn_b_k_norm_scale),
        "w_router": arr(L0_ffn_wg_router).T,
        "w_moe": w_moe,
        "identity": identity,
        "before": before,
        "select": select,
        "rope": rope,
        "mask": mask,
    }
    arrays = {f"in_{n}": np.ascontiguousarray(v) for n, v in arrays.items()}
    nc = bacc.Bacc("TRN2", target_bir_lowering=False, num_devices=1)
    args = [nc.dram_tensor(n, v.shape, mybir.dt.from_np(v.dtype), kind="ExternalInput").ap()
            for n, v in arrays.items()]
    out = nc.dram_tensor("out_x", (TOK, D), F32, kind="ExternalOutput").ap()
    program(nc, *args, out)
    r = run_bass_kernel_spmd(nc, [arrays], core_ids=[0])
    return r.results[0]["out_x"].reshape(x.shape)
```

```python
from contextlib import ExitStack

import concourse.bass as bass
import numpy as np
from concourse import mybir

ALU = mybir.AluOpType
ACT = mybir.ActivationFunctionType
F32 = mybir.dt.float32
F32R = mybir.dt.float32r
BF16 = mybir.dt.bfloat16
I32 = mybir.dt.int32
U16 = mybir.dt.uint16
U32 = mybir.dt.uint32
X = mybir.AxisListType.X

P = 128
D = 256
DC = D // P
TOK = 1024
TILES = TOK // P
BATCHES = 2
BT = TILES // BATCHES
SEQ = BT * P

E = 32
TOP_K = 6
F_EXP = 176
F_SH = 352
CAP = 2 * (TOK * TOP_K // E)
SLOTS = E * CAP
ST = CAP // P
F_HALF = F_EXP // 2
ROW = ST * D
GU = 2 * F_EXP
EW = DC * GU + 2 * D
SHT = (F_SH + P - 1) // P
SW = 3 * D
NOWHERE = 1.0e6

NQ = 16
NKV = 8
HD = 128
WINDOW = 128
QKV_B = (NQ + 2 * NKV) * HD
WB = QKV_B - 4 * HD
CH = 4
K_CHUNKS = NKV // CH
Q_CHUNKS = NQ // CH
CHUNKS = 2 * K_CHUNKS + Q_CHUNKS
T_ORDER = [2, 3, 0, 1, 4, 5]
PLACE = [0, 1, 2, 3, 2, 3]
T_STEP = [3, 4, 4, 5, 6, 7]
SCALE_B = 0.08838834764831845
EPS_LN = 1e-5
EPS_RMS = 1e-6
MASKED = -1e30
OVER = 21504
STEPS_RSQRT = 12
STEPS_A = 2 * BT + STEPS_RSQRT + 2 * BT
STEPS_B = 2 * BT + STEPS_RSQRT + BT * (2 * STEPS_RSQRT + 1) + 3 * NKV * BT
RSQRT_MAGIC = float(0x5F3759DF)


class Steps:

    def __init__(self, engine, sem, base=0):
        self.engine, self.sem, self.base, self.n = engine, sem, base, 0

    def did(self, instruction):
        self.n += 1
        return instruction.then_inc(self.sem, 1)

    def wait(self):
        self.engine.wait_ge(self.sem, self.base + self.n)


def program(nc, x_in, w_qkv_a, b_qkv_a, w_out_a, b_out_a, w_qkv_b, w_out_b, q_scale, k_scale, w_router,
            w_shared, w_gate_up, w_down, identity_in, before_in, rope_in, mask_in, slot_rows, expert_out, out):
    with ExitStack() as ctx:
        def sb(name, shape, dt=F32):
            return ctx.enter_context(nc.sbuf_tensor(name, shape, dt))

        def sem(name):
            return ctx.enter_context(nc.semaphore(name))

        x_tok = sb("x_tok", [P, TILES, D])
        xn = sb("xn", [P, TILES, D])
        xT_hi = sb("xT_hi", [P, DC, TOK], F32R)
        xT_lo = sb("xT_lo", [P, DC, TOK], F32R)
        w_out_b_sb = sb("w_out_b_sb", [P, NQ, D])
        halves = sb("halves", [P, 2, DC * WB], F32R)
        raw = sb("raw", [P, 2, EW])
        gate_sb = sb("gate_sb", [P, 2, F_EXP])
        h_sb = sb("h_sb", [P, 2, F_EXP])
        identity = sb("identity", [P, P])
        before = sb("before", [P, 2, P], BF16)
        mask = sb("mask", [P, 2, HD])
        w_router_sb = sb("w_router_sb", [P, DC, E])
        b_qkv_sb = sb("b_qkv_sb", [P, 6])
        stats = sb("stats", [P, TILES, 6])
        mean_var = sb("mean_var", [P, TILES, 2])
        rstd = sb("rstd", [P, 3, NQ])
        ss = sb("ss", [P, 2, CHUNKS * CH])
        rqs = sb("rqs", [P, 2, NQ])
        rk = sb("rk", [P, 2, NKV])
        mx = sb("mx", [P, 4, 2])
        nb = sb("nb", [P, 4, 2])
        lsum = sb("lsum", [P, 4, 2])
        rl = sb("rl", [P, 4, 2])
        small = sb("small", [P, 3, TILES])
        turn = sb("turn", [P, 1])
        top = sb("top", [P, TILES, 8])
        over = sb("over", [P, OVER])

        def part(start, *shape):
            n = int(np.prod(shape))
            v = over[:, start:start + n]
            names = " ".join(f"d{k}" for k in range(len(shape)))
            if len(shape) > 1:
                v = v.rearrange(f"p ({names}) -> p {names}",
                                **{f"d{k}": s for k, s in enumerate(shape[:-1])})
            return v, start + n

        w_raw_b, _ = part(0, DC * QKV_B)
        qT, at = part(0, 2, NQ, P)
        kT, at = part(at, 3, NKV, P)
        v_b, at = part(at, 3, NKV * HD)
        s_b, at = part(at, 2, 2, 2 * P)
        p_b, at = part(at, 2, 2, 2 * P)
        pT_b, at = part(at, 2, 2, 2 * P)
        encT, at = part(at, NQ, P)
        roped_01, at = part(at, 2, CH, HD)
        squares, at = part(at, 2, CH * HD)
        rope_a, at = part(at, 2, CH, HD)
        rope_b, at = part(at, 2, CH, HD)
        tables, at = part(at, 4, BT, HD)
        assert at <= OVER
        roped = [roped_01[:, 0], roped_01[:, 1]] + [
            xn[:, 2 * k:2 * k + 2, :].rearrange("p i (h d) -> p (i h) d", d=HD) for k in range(2)]
        rope_raw, at = part(8192, 2, BT, HD)
        scales_raw, at = part(at, 4, HD)
        w_raw_a, at = part(8192, DC, 3 * D)
        w_out_a_sb, at = part(at, DC, D)
        qkT, at = part(at, 2 * DC, SEQ)
        v_a, at = part(at, BT, D)
        p_a, at = part(at, 2, SEQ)
        pT_a, at = part(at, BT, SEQ)
        ctxT, at = part(at, DC, SEQ)
        b_out_sb, at = part(at, D)
        at = 9728
        yT, at = part(at, DC, TOK)
        gated, at = part(at, 2, SEQ)
        hid, at = part(at, 2, SEQ)
        route, at = part(at, 6, TILES, E)
        rows_in, at = part(at, 2, ST, D)
        rows_out, at = part(at, 2, ST, D)
        assert at <= OVER - 2 * TOP_K * D
        picks, at = part(OVER - 2 * TOP_K * D, 2, TOP_K, D)
        zeros = over[:, OVER - 2 * TOP_K * D:OVER]
        matches = zeros[:, 0:TILES * TOP_K * E].rearrange("p (i k e) -> p i k e", i=TILES, k=TOP_K)
        picked = sb("picked", [P, TILES, E], BF16)
        expert_ids = sb("expert_ids", [P, E])
        top_ids = sb("top_ids", [P, TILES, 8], U32)
        slot_ids = sb("slot_ids", [P, TILES, TOP_K], U32)
        slot_gate = sb("slot_gate", [P, TILES, TOP_K])

        bank = [ctx.enter_context(nc.psum_tensor(f"bank{k}", [P, 512], F32)) for k in range(8)]

        x_loaded = sem("x_loaded")
        ids_ready = sem("ids_ready")
        zeros_ready = sem("zeros_ready")
        cleared = sem("cleared")
        const_loaded = sem("const_loaded")
        wa_loaded = sem("wa_loaded")
        wo_a_loaded = sem("wo_a_loaded")
        wb_loaded = sem("wb_loaded")
        rope_loaded = sem("rope_loaded")
        stored = sem("stored")

        def phase(prefix, names):
            return {n: sem(f"{prefix}_{n}") for n in names.split()}

        a = phase("a", "step xn xnT xhi xlo whi wlo qk_mm qk v_mm v s_mm max exp p pt_mm pt ctx_mm ctx"
                       " o_mm x bias")
        f = [phase(f"f{k}", "step xn xnT xhi xlo logits_mm logit exp picked pos_mm slots whi wlo g_mm u_mm"
                            " silu hid hhi hlo d_mm raw0 raw1 y0 y1 yt_mm x sent dhi ewlo edlo in0 in1 t_mm thi"
                            " tlo gu_mm gate h ht_mm hthi htlo dn_mm copied out0 out1 got0 got1 x2")
             for k in range(2)]
        bb = phase("b", "step xn xnT xhi xlo whi wlo tab proj sq rot_a rot_b sum rk rot krot t_mm t v"
                        " s_mm max exp p pt_mm pt e_mm e o_mm x")
        block = ctx.enter_context(nc.Block())

        def split(t, n):
            return t.rearrange("p (c n) -> p c n", c=n)

        def rsqrt_step(k, steps, value, eps, scale, n):
            v, y, t = (rstd[:, m, 0:n] for m in (2, 0, 1))
            steps.wait()
            if k == 0:
                op = nc.vector.tensor_scalar(v, value, scale, eps, ALU.mult, ALU.add)
            elif k == 1:
                op = nc.vector.tensor_scalar(t.bitcast(I32), v.bitcast(I32), 1, None,
                                             ALU.logical_shift_right)
            elif k == 2:
                op = nc.vector.tensor_scalar(y.bitcast(I32), t.bitcast(I32), -1.0, RSQRT_MAGIC,
                                             ALU.mult, ALU.add)
            elif k % 3 == 0:
                op = nc.vector.scalar_tensor_tensor(t, v, -0.5, y, ALU.mult, ALU.mult)
            elif k % 3 == 1:
                op = nc.vector.tensor_tensor(t, t, y, ALU.mult)
            else:
                op = nc.vector.scalar_tensor_tensor(y, t, 1.5, y, ALU.add, ALU.mult)
            steps.did(op)

        def normalise(steps, first, ready, count=BT):
            tiles = [x_tok[:, bass.ds(first + i, 1), :].rearrange("p o d -> p (o d)") for i in range(count)]
            for i in range(count):
                steps.did(nc.vector.bn_stats(stats[:, i, :], tiles[i]))
            steps.wait()
            nc.vector.memset(turn[:, :], 0.0)
            for i in range(count):
                steps.did(nc.vector.bn_aggr(mean_var[:, i, :], stats[:, i, :]))
            for k in range(STEPS_RSQRT):
                rsqrt_step(k, steps, mean_var[:, 0:count, 1], EPS_LN, 1.0, count)
            steps.wait()
            for i in range(count):
                nc.vector.tensor_scalar(xn[:, i, :], tiles[i], mean_var[:, i, 0:1], rstd[:, 0, i:i + 1],
                                        ALU.subtract, ALU.mult).then_inc(ready, 1)

        def transpose_batch(done):
            for c in range(DC):
                for i in range(BT):
                    last = nc.tensor.transpose(bank[c][:, i * P:(i + 1) * P], xn[:, i, c * P:(c + 1) * P],
                                               identity[:, :])
                last.then_inc(done, 1)

        def matmul3(out, hi, lo, rhs_hi, rhs_lo, start, stop):
            nc.tensor.matmul(out, hi, rhs_lo, start=start, stop=False)
            nc.tensor.matmul(out, lo, rhs_hi, start=False, stop=False)
            return nc.tensor.matmul(out, hi, rhs_hi, start=False, stop=stop)

        wa_hi = halves[:, 0, 0:DC * 3 * D].rearrange("p (c n) -> p c n", c=DC)
        wa_lo = halves[:, 1, 0:DC * 3 * D].rearrange("p (c n) -> p c n", c=DC)

        def wb(k, c, chunk):
            n = CH * HD
            if chunk == CHUNKS - 1:
                return (xT_hi, xT_lo)[k][:, c, SEQ:SEQ + n]
            return halves[:, k, c * WB + chunk * n:c * WB + (chunk + 1) * n]

        def places(n, start, *shape):
            size = int(np.prod(shape))
            return [halves[:, k, start:start + n * size].rearrange("p (k n) -> p k n", k=n) for k in range(2)], \
                start + n * size

        (wf_hi, wf_lo), at = places(2, 0, SW)
        (h_hi, h_lo), at = places(2, at, SEQ)
        (we_hi, we_lo), at = places(2, at, EW)
        (xe_hi, xe_lo), at = places(2, at, DC, CAP)
        (he_hi, he_lo), at = places(2, at, 2, P)
        assert at <= DC * WB

        def shared_loads(sp, s):
            for j in range(SHT):
                if j >= 2:
                    sp.wait_ge(s["whi"], j - 1)
                    sp.wait_ge(s["wlo"], j - 1)
                sp.dma_start(raw[:, j % 2, 0:SW], w_shared[j]).then_inc((s["raw0"], s["raw1"])[j % 2], 16)

        def expert_traffic(sp, s):
            ins, outs = (s["in0"], s["in1"]), (s["out0"], s["out1"])
            row_view = slot_rows.rearrange("(e p m) d -> e p (m d)", p=P, m=ST)
            out_view = expert_out.rearrange("(e p m) d -> e p (m d)", p=P, m=ST)

            def weights(e, par, early=False):
                if early:
                    sp.wait_ge(s["wlo"], e + 2)
                else:
                    sp.wait_ge(s["ewlo"], e - 1)
                    sp.wait_ge(s["edlo"], e - 1)
                done = (s["raw1"], s["raw0"])[par]
                sp.dma_start(raw[:, 1 - par, 0:DC * GU],
                             w_gate_up[bass.ds(e, 1)].rearrange("o p n -> p (o n)")).then_inc(done, 16)
                sp.dma_start(raw[0:F_HALF, 1 - par, DC * GU:EW],
                             w_down[bass.ds(e, 1)].rearrange("o p n -> p (o n)")).then_inc(done, 16)

            def rows(e, par, early=False):
                if not early:
                    sp.wait_ge(s["t_mm"], e - 1)
                sp.dma_start(rows_in[:, par].rearrange("p m d -> p (m d)"),
                             row_view[bass.ds(e, 1)].rearrange("o p n -> p (o n)")).then_inc(ins[par], 16)

            def results(e, par):
                sp.wait_ge(s["copied"], ST * e + ST)
                sp.dma_start(out_view[bass.ds(e, 1)].rearrange("o p n -> p (o n)"),
                             rows_out[:, par].rearrange("p m d -> p (m d)")).then_inc(outs[par], 16)

            for e in range(2):
                weights(e, e, early=True)
            sp.wait_ge(s["sent"], 16 * TILES * TOP_K)
            for e in range(2):
                rows(e, e, early=True)
            for e in range(2):
                weights(e + 2, e)
                rows(e + 2, e)
                if e:
                    results(e - 1, 1 - e)
            with sp.Fori(1, E // 2 - 1) as k:
                for par in range(2):
                    e = 2 * k + par
                    weights(e + 2, par)
                    rows(e + 2, par)
                    results(e - 1, 1 - par)
            for e in range(E - 3, E):
                results(e, e % 2)

        @block.sync
        def _(sp):
            xv = x_in.rearrange("(b i p) d -> b p i d", b=BATCHES, p=P)
            for b in range(BATCHES):
                sp.dma_start(x_tok[:, b * BT:(b + 1) * BT, :], xv[b]).then_inc(x_loaded, 16)
            sp.dma_start(identity[:, :], identity_in).then_inc(const_loaded, 16)
            sp.dma_start(w_raw_a[:, :, :], w_qkv_a.rearrange("(c p) n -> p c n", p=P)).then_inc(wa_loaded, 16)
            sp.dma_start(b_qkv_sb[:, :], b_qkv_a).then_inc(wa_loaded, 16)
            sp.dma_start(w_out_a_sb[:, :, :], w_out_a.rearrange("(c p) n -> p c n", p=P)) \
                .then_inc(wo_a_loaded, 16)
            sp.dma_start(b_out_sb, b_out_a.partition_broadcast(P)).then_inc(wo_a_loaded, 16)
            sp.dma_start(before[:, :, :].bitcast(U16), before_in).then_inc(const_loaded, 16)
            sp.dma_start(mask[:, :, :], mask_in).then_inc(const_loaded, 16)
            sp.dma_start(w_router_sb[:, :, :], w_router.rearrange("(c p) n -> p c n", p=P)) \
                .then_inc(const_loaded, 16)
            sp.wait_ge(zeros_ready, 1)
            n = 2 * TOP_K * D
            clear = slot_rows.rearrange("(p m) d -> p (m d)", p=P)
            for k in range(SLOTS * D // P // n):
                sp.dma_start(clear[:, k * n:(k + 1) * n], zeros).then_inc(cleared, 16)
            sp.dma_start(w_out_b_sb[:, :, :], w_out_b.rearrange("n p d -> p n d")).then_inc(wb_loaded, 16)
            sp.wait_ge(a["x"], 2 * BATCHES)
            sp.dma_start(w_raw_b, w_qkv_b.rearrange("p c n -> p (c n)")).then_inc(wb_loaded, 16)
            sp.dma_start(rope_raw, rope_in).then_inc(rope_loaded, 16)
            for k, s in enumerate((q_scale, k_scale)):
                sp.dma_start(scales_raw[:, 2 * k, :], s.partition_broadcast(P)).then_inc(rope_loaded, 16)
                for half in range(2):
                    sp.dma_start(scales_raw[:, 2 * k + 1, half * HD // 2:(half + 1) * HD // 2],
                                 s[(1 - half) * HD // 2:(2 - half) * HD // 2].partition_broadcast(P)) \
                        .then_inc(rope_loaded, 16)
            shared_loads(sp, f[0])
            expert_traffic(sp, f[0])
            sp.wait_ge(f[0]["dhi"], E)
            sp.wait_ge(f[0]["ewlo"], E)
            sp.wait_ge(f[0]["edlo"], E)
            shared_loads(sp, f[1])
            expert_traffic(sp, f[1])
            sp.wait_ge(f[1]["x2"], TILES)
            ov = out.rearrange("(b i p) d -> b p i d", b=BATCHES, p=P)
            for b in range(BATCHES):
                sp.dma_start(ov[b], x_tok[:, b * BT:(b + 1) * BT, :]).then_inc(stored, 16)
            sp.wait_ge(stored, 16 * BATCHES)

        def attention_a_pe(pe):
            pe.wait_ge(const_loaded, 64)
            pe.wait_ge(a["whi"], 1)
            pe.wait_ge(a["wlo"], 1)
            pe.wait_ge(wo_a_loaded, 32)
            with pe.Fori(0, BATCHES) as b:
                pe.wait_ge(a["xn"], BT * b + BT)
                transpose_batch(a["xnT"])
                pe.wait_ge(a["xhi"], DC * b + DC)
                pe.wait_ge(a["xlo"], DC * b + DC)
                for m in range(2 * DC):
                    for c in range(DC):
                        last = matmul3(bank[2 + m][:, :], wa_hi[:, c, m * P:(m + 1) * P],
                                       wa_lo[:, c, m * P:(m + 1) * P], xT_hi[:, c, 0:SEQ], xT_lo[:, c, 0:SEQ],
                                       c == 0, c == DC - 1)
                    last.then_inc(a["qk_mm"], 1)
                for i in range(BT):
                    for c in range(DC):
                        last = matmul3(bank[6 + i // 2][:, (i % 2) * D:(i % 2 + 1) * D],
                                       xT_hi[:, c, i * P:(i + 1) * P], xT_lo[:, c, i * P:(i + 1) * P],
                                       wa_hi[:, c, 2 * D:3 * D], wa_lo[:, c, 2 * D:3 * D],
                                       c == 0, c == DC - 1)
                    if i % 2:
                        last.then_inc(a["v_mm"], 1)
                pe.wait_ge(a["qk"], 2 * DC * b + 2 * DC)

                def scores(q):
                    if q >= 2:
                        pe.wait_ge(a["exp"], BT * b + q - 1)
                    for c in range(DC):
                        last = nc.tensor.matmul(bank[q % 2][:, :], qkT[:, c, q * P:(q + 1) * P],
                                                qkT[:, DC + c, :], start=c == 0, stop=c == DC - 1)
                    last.then_inc(a["s_mm"], 1)

                def probs_transposed(q):
                    pe.wait_ge(a["p"], BT * b + q + 1)
                    if q >= 2:
                        pe.wait_ge(a["pt"], BT * b + q - 1)
                    for k in range(BT):
                        last = nc.tensor.transpose(bank[2 + q % 2][:, k * P:(k + 1) * P],
                                                   p_a[:, q % 2, k * P:(k + 1) * P], identity[:, :])
                    last.then_inc(a["pt_mm"], 1)

                scores(0)
                for q in range(1, BT):
                    scores(q)
                    probs_transposed(q - 1)
                probs_transposed(BT - 1)
                pe.wait_ge(a["pt"], BT * b + BT)
                pe.wait_ge(a["v"], 2 * b + 2)
                for m in range(DC):
                    for k in range(BT):
                        last = nc.tensor.matmul(bank[4 + m][:, :], v_a[:, k, m * P:(m + 1) * P], pT_a[:, k, :],
                                                start=k == 0, stop=k == BT - 1)
                    last.then_inc(a["ctx_mm"], 1)
                pe.wait_ge(a["ctx"], DC * b + DC)
                for i in range(BT):
                    for c in range(DC):
                        last = nc.tensor.matmul(bank[6 + i // 2][:, (i % 2) * D:(i % 2 + 1) * D],
                                                ctxT[:, c, i * P:(i + 1) * P], w_out_a_sb[:, c, :],
                                                start=c == 0, stop=c == DC - 1)
                    if i % 2:
                        last.then_inc(a["o_mm"], 1)

        def ffn_pe(pe, s):
            for hb in range(BATCHES):
                pe.wait_ge(s["xn"], BT * (hb + 1))
                for c in range(DC):
                    for i in range(BT):
                        last = nc.tensor.transpose(bank[2 * hb + c][:, i * P:(i + 1) * P],
                                                   xn[:, BT * hb + i, c * P:(c + 1) * P], identity[:, :])
                    last.then_inc(s["xnT"], 1)
            for i in range(TILES):
                if i % BT == 0:
                    pe.wait_ge(s["xhi"], DC * (i // BT + 1))
                    pe.wait_ge(s["xlo"], DC * (i // BT + 1))
                for n, half in enumerate((xT_lo, xT_hi)):
                    for c in range(DC):
                        last = nc.tensor.matmul(bank[6][:, i * E:(i + 1) * E],
                                                half[:, c, i * P:(i + 1) * P].bitcast(F32),
                                                w_router_sb[:, c, :], start=n + c == 0, stop=n + c == 2)
            last.then_inc(s["logits_mm"], 1)

            def up(j, h):
                u = 2 * j + h
                tok = slice(h * SEQ, (h + 1) * SEQ)
                if h == 0:
                    pe.wait_ge(s["whi"], j + 1)
                    pe.wait_ge(s["wlo"], j + 1)
                if u >= 2:
                    pe.wait_ge(s["silu"], u - 1)
                for c in range(DC):
                    w = slice(c * P, (c + 1) * P)
                    last = matmul3(bank[4 + 3 * h][:, :], wf_hi[:, j % 2, w], wf_lo[:, j % 2, w],
                                   xT_hi[:, c, tok], xT_lo[:, c, tok], c == 0, c == DC - 1)
                last.then_inc(s["g_mm"], 1)
                if u >= 1:
                    pe.wait_ge(s["hid"], u)
                for c in range(DC):
                    w = slice(D + c * P, D + (c + 1) * P)
                    last = matmul3(bank[5][:, :], wf_hi[:, j % 2, w], wf_lo[:, j % 2, w],
                                   xT_hi[:, c, tok], xT_lo[:, c, tok], c == 0, c == DC - 1)
                last.then_inc(s["u_mm"], 1)

            def down(j, h):
                u = 2 * j + h
                pe.wait_ge(s["hhi"], u + 1)
                pe.wait_ge(s["hlo"], u + 1)
                for m in range(DC):
                    w = slice(2 * D + m * P, 2 * D + (m + 1) * P)
                    last = matmul3(bank[2 * h + m][:, :], wf_hi[:, j % 2, w], wf_lo[:, j % 2, w],
                                   h_hi[:, h, :], h_lo[:, h, :], j == 0, j == SHT - 1)
                last.then_inc(s["d_mm"], 1)

            up(0, 0)
            pe.wait_ge(s["picked"], 1)
            for i in range(TILES):
                for k in range(i + 1):
                    last = nc.tensor.matmul(bank[6][:, i * E:(i + 1) * E], before[:, 0 if k == i else 1, :],
                                            picked[:, k, :], start=k == 0, stop=k == i)
            last.then_inc(s["pos_mm"], 1)
            for u in range(1, 2 * SHT):
                up(u // 2, u % 2)
                down((u - 1) // 2, (u - 1) % 2)
            down(SHT - 1, 1)
            for i in range(TILES):
                if i % BT == 0:
                    pe.wait_ge(s["y0"], i // BT + 1)
                    pe.wait_ge(s["y1"], i // BT + 1)
                for m in range(DC):
                    last = nc.tensor.transpose(
                        bank[4 + i // 2][:, (i % 2) * D + m * P:(i % 2) * D + (m + 1) * P],
                        yT[:, m, i * P:(i + 1) * P], identity[:, :])
                if i % 2:
                    last.then_inc(s["yt_mm"], 1)

            def turn_rows(k, par, first=False):
                e = 2 * k + par
                pe.wait_ge((s["in0"], s["in1"])[par], 16 * k + 16)
                if first:
                    pe.wait_ge(s["x"], TILES // 2)
                else:
                    pe.wait_ge(s["tlo"], DC * e)
                for c in range(DC):
                    for m in range(ST):
                        last = nc.tensor.transpose(bank[c][:, m * P:(m + 1) * P],
                                                   rows_in[:, par, m, c * P:(c + 1) * P], identity[:, :])
                last.then_inc(s["t_mm"], 1)

            def gate_up(k, par, m, early):
                e = 2 * k + par
                u = ST * e + m
                v = ST * par + m
                if m == 0:
                    pe.wait_ge(s["whi"], e + SHT + 1)
                    pe.wait_ge(s["ewlo"], e + 1)
                    pe.wait_ge(s["tlo"], DC * e + DC)
                if not (early and v < 2):
                    pe.wait_ge(s["h"], u - 1)
                for c in range(DC):
                    x = slice(c * CAP + m * P, c * CAP + (m + 1) * P)
                    w = slice(c * GU, (c + 1) * GU)
                    last = matmul3(bank[2 + v % 2][:, 0:GU], xe_hi[:, par, x], xe_lo[:, par, x],
                                   we_hi[:, par, w], we_lo[:, par, w], c == 0, c == DC - 1)
                last.then_inc(s["gu_mm"], 1)

            def turn_hidden(u, v, early=False):
                pe.wait_ge(s["h"], u + 1)
                if not (early and v < 2):
                    pe.wait_ge(s["htlo"], u - 1)
                for k in range(2):
                    last = nc.tensor.transpose(bank[4 + v % 2][0:F_HALF, k * P:(k + 1) * P],
                                               h_sb[:, v % 2, k * F_HALF:(k + 1) * F_HALF], identity[:, :])
                last.then_inc(s["ht_mm"], 1)

            def down_rows(e, par, m, u, v, early=False):
                if m == 0:
                    pe.wait_ge(s["dhi"], e + 1)
                    pe.wait_ge(s["edlo"], e + 1)
                pe.wait_ge(s["htlo"], u + 1)
                if not (early and v < 2):
                    pe.wait_ge(s["copied"], u - 1)
                for k in range(2):
                    h = slice(k * P, (k + 1) * P)
                    w = slice(DC * GU + k * D, DC * GU + (k + 1) * D)
                    last = matmul3(bank[6 + v % 2][:, 0:D], he_hi[0:F_HALF, v % 2, h], he_lo[0:F_HALF, v % 2, h],
                                   we_hi[0:F_HALF, par, w], we_lo[0:F_HALF, par, w], k == 0, k == 1)
                last.then_inc(s["dn_mm"], 1)

            def pair(k, early=False, end=False):
                for v in range(2 * ST):
                    par, m = v // ST, v % ST
                    u = 2 * ST * k + v
                    gate_up(k, par, m, early)
                    if m == 0 and not (end and par):
                        turn_rows(k + par, 1 - par)
                    if not (early and v < 1):
                        turn_hidden(u - 1, (v - 1) % (2 * ST), early)
                    if not (early and v < 2):
                        w = (v - 2) % (2 * ST)
                        down_rows((u - 2 - w % ST) // ST if early else 2 * k + (v - 2) // ST, w // ST, w % ST,
                                  u - 2, w, early)

            turn_rows(0, 0, first=True)
            pair(0, early=True)
            with pe.Fori(1, E // 2 - 1) as k:
                pair(k)
            pair(E // 2 - 1, end=True)
            u = ST * E
            turn_hidden(u - 1, 2 * ST - 1)
            down_rows(E - 1, 1, ST - 2, u - 2, 2 * ST - 2)
            down_rows(E - 1, 1, ST - 1, u - 1, 2 * ST - 1)

        def attention_b_pe(pe):
            pe.wait_ge(bb["whi"], 2 * DC)
            pe.wait_ge(bb["wlo"], 2 * DC)
            pe.wait_ge(wb_loaded, 32)
            with pe.Fori(0, BATCHES) as b:
                pe.wait_ge(bb["xn"], BT * b + BT)
                transpose_batch(bb["xnT"])
                pe.wait_ge(bb["xhi"], DC * b + DC)
                pe.wait_ge(bb["xlo"], DC * b + DC)

                def project(i, c):
                    n = CHUNKS * i + c
                    if n >= 2:
                        prev = CHUNKS * ((n - 2) // CHUNKS), (n - 2) % CHUNKS
                        if prev[1] < K_CHUNKS + Q_CHUNKS:
                            done = (K_CHUNKS + Q_CHUNKS) * (prev[0] // CHUNKS) + prev[1] + 1
                            pe.wait_ge(bb["sq"], (K_CHUNKS + Q_CHUNKS) * BT * b + done)
                            pe.wait_ge(bb["rot_b"], (K_CHUNKS + Q_CHUNKS) * BT * b + done)
                        else:
                            pe.wait_ge(bb["v"], K_CHUNKS * BT * b + K_CHUNKS * (prev[0] // CHUNKS)
                                       + prev[1] - K_CHUNKS - Q_CHUNKS + 1)
                    for k in range(DC):
                        t = slice(i * P, (i + 1) * P)
                        last = matmul3(bank[n % 2][:, :], xT_hi[:, k, t], xT_lo[:, k, t], wb(0, k, c),
                                       wb(1, k, c), k == 0, k == DC - 1)
                    last.then_inc(bb["proj"], 1)

                def transposed(i, m):
                    c = T_ORDER[m]
                    base = (K_CHUNKS + Q_CHUNKS) * (BT * b + i)
                    if c < K_CHUNKS:
                        pe.wait_ge(bb["krot"], K_CHUNKS * (BT * b + i) + c + 1)
                    else:
                        pe.wait_ge(bb["rot"], base + c + 1)
                    if i or m:
                        pe.wait_ge(bb["t"], base + m)
                    for k in range(CH):
                        last = nc.tensor.transpose(bank[2][:, k * P:(k + 1) * P], roped[PLACE[c]][:, k, :],
                                                   identity[:, :])
                    last.then_inc(bb["t_mm"], 1)

                def scores(i, g):
                    n = NKV * i + g
                    base = NKV * BT * b
                    if g == 0:
                        pe.wait_ge(bb["t"], (K_CHUNKS + Q_CHUNKS) * (BT * b + i + 1))
                    if n >= 2:
                        pe.wait_ge(bb["max"], base + n - 1)
                    for h in range(2):
                        for k in range(2) if i else (1,):
                            last = nc.tensor.matmul(bank[5 + n % 2][:, (2 * h + k) * P:(2 * h + k + 1) * P],
                                                    qT[:, i % 2, 2 * g + h, :], kT[:, (i - 1 + k) % 3, g, :],
                                                    start=True, stop=True)
                    last.then_inc(bb["s_mm"], 1)

                def probs_transposed(i, g):
                    n = NKV * i + g
                    base = NKV * BT * b
                    pe.wait_ge(bb["p"], base + n + 1)
                    if n >= 1:
                        pe.wait_ge(bb["pt"], base + n)
                    for k in range(2) if i else (1,):
                        for h in range(2):
                            last = nc.tensor.transpose(bank[3][:, (2 * k + h) * P:(2 * k + h + 1) * P],
                                                       p_b[:, n % 2, h, k * P:(k + 1) * P], identity[:, :])
                    last.then_inc(bb["pt_mm"], 1)

                def encode(i, g):
                    n = NKV * i + g
                    base = NKV * BT * b
                    pe.wait_ge(bb["pt"], base + n + 1)
                    if g == 0:
                        pe.wait_ge(bb["v"], K_CHUNKS * (BT * b + i + 1))
                    if n >= 1:
                        pe.wait_ge(bb["e"], base + n)
                    for k in range(2) if i else (1,):
                        last = nc.tensor.matmul(bank[7][:, 0:D],
                                                v_b[:, (i - 1 + k) % 3, g * HD:(g + 1) * HD],
                                                pT_b[:, n % 2, k, :], start=(k == 0 or i == 0), stop=k == 1)
                    last.then_inc(bb["e_mm"], 1)

                def project_out(i, g):
                    pe.wait_ge(bb["e"], NKV * (BT * b + i) + g + 1)
                    if g == 0 and i:
                        pe.wait_ge(bb["x"], BT * b + i)
                    for h in range(2 * g, 2 * g + 2):
                        last = nc.tensor.matmul(bank[4][:, 0:D], encT[:, h, :], w_out_b_sb[:, h, :],
                                                start=h == 0, stop=h == NQ - 1)
                    last.then_inc(bb["o_mm"], 1)

                for c in range(CHUNKS):
                    project(0, c)
                for m in range(len(T_ORDER)):
                    transposed(0, m)
                scores(0, 0)
                for i in range(BT):
                    for g in range(NKV):
                        if g + 1 < NKV:
                            scores(i, g + 1)
                        if i + 1 < BT:
                            project(i + 1, g)
                        probs_transposed(i, g)
                        if i + 1 < BT and g in T_STEP:
                            transposed(i + 1, T_STEP.index(g))
                        if g:
                            encode(i, g - 1)
                        if i:
                            project_out(i - 1, g)
                        if i + 1 < BT and T_STEP.count(g) == 2:
                            transposed(i + 1, T_STEP.index(g) + 1)
                    encode(i, NKV - 1)
                    if i + 1 < BT:
                        scores(i + 1, 0)
                for g in range(NKV):
                    project_out(BT - 1, g)

        @block.tensor
        def _(pe):
            attention_a_pe(pe)
            ffn_pe(pe, f[0])
            attention_b_pe(pe)
            ffn_pe(pe, f[1])

        def attention_a_act(act):
            act.wait_ge(wa_loaded, 32)
            nc.scalar.activation(wa_hi, w_raw_a, ACT.Copy).then_inc(a["whi"], 1)
            with act.Fori(0, BATCHES) as b:
                for c in range(DC):
                    act.wait_ge(a["xnT"], DC * b + c + 1)
                    nc.scalar.activation(xT_hi[:, c, 0:SEQ], bank[c][:, :], ACT.Copy).then_inc(a["xhi"], 1)
                for m in range(2 * DC):
                    act.wait_ge(a["qk_mm"], 2 * DC * b + m + 1)
                    nc.scalar.activation(qkT[:, m, :], bank[2 + m][:, :], ACT.Identity,
                                         bias=b_qkv_sb[:, m:m + 1]).then_inc(a["qk"], 1)

                def exponentials(q):
                    act.wait_ge(a["max"], BT * b + q + 1)
                    if q >= 2:
                        act.wait_ge(a["pt_mm"], BT * b + q - 1)
                    nc.scalar.activation(p_a[:, q % 2, :], bank[q % 2][:, :], ACT.Exp, bias=nb[:, q, 0:1],
                                         scale=1.0 / 16.0, accum_out=lsum[:, q, 0:1]).then_inc(a["exp"], 1)

                def copy_probs(q):
                    act.wait_ge(a["pt_mm"], BT * b + q + 1)
                    nc.scalar.activation(pT_a[:, :, q * P:(q + 1) * P], split(bank[2 + q % 2][:, :], BT),
                                         ACT.Copy).then_inc(a["pt"], 1)

                exponentials(0)
                for q in range(1, BT):
                    exponentials(q)
                    copy_probs(q - 1)
                copy_probs(BT - 1)
                for m in range(DC):
                    act.wait_ge(a["ctx_mm"], DC * b + m + 1)
                    nc.scalar.activation(ctxT[:, m, :], bank[4 + m][:, :], ACT.Identity,
                                         bias=b_qkv_sb[:, 2 * DC + m:2 * DC + m + 1]).then_inc(a["ctx"], 1)

        def ffn_act(act, s):
            for hb in range(BATCHES):
                for c in range(DC):
                    act.wait_ge(s["xnT"], DC * hb + c + 1)
                    nc.scalar.activation(xT_hi[:, c, hb * SEQ:(hb + 1) * SEQ], bank[2 * hb + c][:, :], ACT.Copy) \
                        .then_inc(s["xhi"], 1)

            def shared_weights(j):
                act.wait_ge((s["raw0"], s["raw1"])[j % 2], 16 * (j // 2) + 16)
                if j >= 2:
                    act.wait_ge(s["d_mm"], 2 * (j - 1))
                nc.scalar.activation(wf_hi[:, j % 2, :], raw[:, j % 2, 0:SW], ACT.Copy).then_inc(s["whi"], 1)

            shared_weights(0)
            act.wait_ge(s["logit"], 1)
            nc.scalar.activation(route[:, 1], route[:, 0], ACT.Exp).then_inc(s["exp"], 1)
            shared_weights(1)
            for u in range(2 * SHT):
                j, h = u // 2, u % 2
                act.wait_ge(s["g_mm"], u + 1)
                if u >= 2:
                    act.wait_ge(s["hid"], u - 1)
                nc.scalar.activation(gated[:, h, :], bank[4 + 3 * h][:, :], ACT.Silu).then_inc(s["silu"], 1)
                act.wait_ge(s["hid"], u + 1)
                if u >= 2:
                    act.wait_ge(s["d_mm"], u - 1)
                nc.scalar.activation(h_hi[:, h, :], hid[:, h, :], ACT.Copy).then_inc(s["hhi"], 1)
                if h == 0 and 1 <= j < SHT - 1:
                    shared_weights(j + 1)
            for h in range(2):
                act.wait_ge(s["d_mm"], 2 * (SHT - 1) + h + 1)
                nc.scalar.activation(yT[:, 0, h * SEQ:(h + 1) * SEQ], bank[2 * h][:, :], ACT.Copy) \
                    .then_inc(s["y0"], 1)

            def split_gate_up(k, par, early=False):
                act.wait_ge((s["raw1"], s["raw0"])[par], 32 * k + (48, 64)[par])
                if not early:
                    act.wait_ge(s["gu_mm"], ST * (2 * k + par) - ST)
                nc.scalar.activation(we_hi[:, par, 0:DC * GU], raw[:, 1 - par, 0:DC * GU], ACT.Copy) \
                    .then_inc(s["whi"], 1)

            def split_down(k, par, early=False):
                if not early:
                    act.wait_ge(s["dn_mm"], ST * (2 * k + par) - ST)
                nc.scalar.activation(we_hi[0:F_HALF, par, DC * GU:EW], raw[0:F_HALF, 1 - par, DC * GU:EW],
                                     ACT.Copy).then_inc(s["dhi"], 1)

            def split_rows(k, par, early=False):
                e = 2 * k + par
                act.wait_ge(s["t_mm"], e + 1)
                if not early:
                    act.wait_ge(s["gu_mm"], ST * e - ST)
                for c in range(DC):
                    nc.scalar.activation(xe_hi[:, par, c * CAP:(c + 1) * CAP], bank[c][:, 0:CAP], ACT.Copy) \
                        .then_inc(s["thi"], 1)

            def silu(u, v, early=False):
                act.wait_ge(s["gu_mm"], u + 1)
                if not (early and v < 2):
                    act.wait_ge(s["h"], u - 1)
                nc.scalar.activation(gate_sb[:, v % 2, :], bank[2 + v % 2][:, 0:F_EXP], ACT.Silu) \
                    .then_inc(s["gate"], 1)

            def split_hidden(u, v, early=False):
                act.wait_ge(s["ht_mm"], u + 1)
                if not (early and v < 2):
                    act.wait_ge(s["dn_mm"], u - 1)
                nc.scalar.activation(he_hi[0:F_HALF, v % 2, :], bank[4 + v % 2][0:F_HALF, 0:2 * P], ACT.Copy) \
                    .then_inc(s["hthi"], 1)

            def copy_result(k, u, v, early=False):
                act.wait_ge(s["dn_mm"], u + 1)
                if v % ST == 0 and not early:
                    act.wait_ge((s["out0"], s["out1"])[v // ST], 16 * k)
                nc.scalar.activation(rows_out[:, v // ST, v % ST, :], bank[6 + v % 2][:, 0:D], ACT.Copy) \
                    .then_inc(s["copied"], 1)

            def pair(k, early=False, end=False, behind=0):
                for v in range(2 * ST):
                    par, m = v // ST, v % ST
                    u = 2 * ST * k + v
                    silu(u, v, early)
                    if m == 0 and not (end and par):
                        split_rows(k + par, 1 - par, early and par == 0)
                    if not (early and v < 1):
                        split_hidden(u - 1, (v - 1) % (2 * ST), early)
                    if not (early and v < 2):
                        copy_result(k if v >= 2 else k - 1, u - 2, (v - 2) % (2 * ST), early or (behind and v < 2))
                    if m == 0 and not (end and par):
                        split_gate_up(k + par, 1 - par, early and par == 0)
                    if m == 1 and not (end and par):
                        split_down(k + par, 1 - par, early and par == 0)

            split_gate_up(0, 0, early=True)
            split_down(0, 0, early=True)
            split_rows(0, 0, early=True)
            pair(0, early=True)
            pair(1, behind=1)
            with act.Fori(2, E // 2 - 1) as k:
                pair(k)
            pair(E // 2 - 1, end=True)
            u = ST * E
            split_hidden(u - 1, 2 * ST - 1)
            copy_result(E // 2 - 1, u - 2, 2 * ST - 2)
            copy_result(E // 2 - 1, u - 1, 2 * ST - 1)

        def attention_b_act(act):
            act.wait_ge(wb_loaded, 32)
            w_raw = split(w_raw_b, DC)
            for c in range(DC):
                nc.scalar.activation(halves[:, 0, c * WB:(c + 1) * WB], w_raw[:, c, 0:WB], ACT.Copy) \
                    .then_inc(bb["whi"], 1)
                nc.scalar.activation(wb(0, c, CHUNKS - 1), w_raw[:, c, WB:QKV_B], ACT.Copy).then_inc(bb["whi"], 1)
            with act.Fori(0, BATCHES) as b:
                for c in range(DC):
                    act.wait_ge(bb["xnT"], DC * b + c + 1)
                    nc.scalar.activation(xT_hi[:, c, 0:SEQ], bank[c][:, :], ACT.Copy).then_inc(bb["xhi"], 1)

                def square(i, c):
                    act.wait_ge(bb["proj"], CHUNKS * (BT * b + i) + c + 1)
                    src = bank[c % 2][:, :]
                    if c < K_CHUNKS + Q_CHUNKS:
                        n = (K_CHUNKS + Q_CHUNKS) * i + c
                        if n >= 2:
                            act.wait_ge(bb["sum"], (K_CHUNKS + Q_CHUNKS) * BT * b + n - 1)
                        nc.scalar.activation(squares[:, c % 2, :], src, ACT.Square).then_inc(bb["sq"], 1)
                    else:
                        k = (c - K_CHUNKS - Q_CHUNKS) * CH * HD
                        nc.scalar.activation(v_b[:, i % 3, k:k + CH * HD], src, ACT.Copy).then_inc(bb["v"], 1)

                def copy_transposed(i, m):
                    c = T_ORDER[m]
                    act.wait_ge(bb["t_mm"], (K_CHUNKS + Q_CHUNKS) * (BT * b + i) + m + 1)
                    if c < K_CHUNKS:
                        dst = kT[:, i % 3, c * CH:(c + 1) * CH, :]
                    else:
                        dst = qT[:, i % 2, (c - K_CHUNKS) * CH:(c - K_CHUNKS + 1) * CH, :]
                    nc.scalar.activation(dst, split(bank[2][:, :], CH), ACT.Copy).then_inc(bb["t"], 1)

                def exponentials(i, g):
                    n = NKV * i + g
                    keys = slice(0 if i else P, 2 * P)
                    act.wait_ge(bb["max"], NKV * BT * b + n + 1)
                    if n >= 2:
                        act.wait_ge(bb["pt_mm"], NKV * BT * b + n - 1)
                    for h in range(2):
                        last = nc.scalar.activation(p_b[:, n % 2, h, keys], s_b[:, n % 2, h, keys], ACT.Exp,
                                                    bias=nb[:, n % 4, h:h + 1],
                                                    scale=rqs[:, i % 2, 2 * g + h:2 * g + h + 1],
                                                    accum_out=lsum[:, n % 4, h:h + 1])
                    last.then_inc(bb["exp"], 1)

                def copy_probs(i, g):
                    n = NKV * i + g
                    act.wait_ge(bb["pt_mm"], NKV * BT * b + n + 1)
                    if n >= 2:
                        act.wait_ge(bb["e_mm"], NKV * BT * b + n - 1)
                    k = slice(0 if i else 1, 2)
                    nc.scalar.activation(pT_b[:, n % 2, k, :], split(bank[3][:, :], 2)[:, k, :],
                                         ACT.Copy).then_inc(bb["pt"], 1)

                def copy_encoded(i, g):
                    act.wait_ge(bb["e_mm"], NKV * (BT * b + i) + g + 1)
                    if i:
                        act.wait_ge(bb["o_mm"], NKV * (BT * b + i - 1) + g + 1)
                    nc.scalar.activation(encT[:, 2 * g:2 * g + 2, :], split(bank[7][:, 0:D], 2),
                                         ACT.Copy).then_inc(bb["e"], 1)

                for c in range(CHUNKS):
                    square(0, c)
                for m in range(len(T_ORDER)):
                    copy_transposed(0, m)
                exponentials(0, 0)
                for i in range(BT):
                    for g in range(NKV):
                        if i + 1 < BT:
                            square(i + 1, g)
                        if g + 1 < NKV:
                            exponentials(i, g + 1)
                        copy_probs(i, g)
                        if i + 1 < BT and g in T_STEP:
                            copy_transposed(i + 1, T_STEP.index(g))
                        if g:
                            copy_encoded(i, g - 1)
                        if i + 1 < BT and T_STEP.count(g) == 2:
                            copy_transposed(i + 1, T_STEP.index(g) + 1)
                    copy_encoded(i, NKV - 1)
                    if i + 1 < BT:
                        exponentials(i + 1, 0)

        @block.scalar
        def _(act):
            attention_a_act(act)
            ffn_act(act, f[0])
            attention_b_act(act)
            ffn_act(act, f[1])

        def spread(t, n):
            return t.unsqueeze(2).to_broadcast([P, t.shape[1], n])

        def attention_a_dve(dve):
            dve.wait_ge(a["whi"], 1)
            nc.vector.tensor_tensor(wa_lo, w_raw_a, wa_hi.bitcast(F32), ALU.subtract).then_inc(a["wlo"], 1)
            dve.wait_ge(x_loaded, 16 * BATCHES)
            with dve.Fori(0, BATCHES) as b:
                steps = Steps(dve, a["step"], b * STEPS_A)
                normalise(steps, BT * b, a["xn"])
                for c in range(DC):
                    dve.wait_ge(a["xhi"], DC * b + c + 1)
                    nc.vector.tensor_tensor(xT_lo[:, c, 0:SEQ], bank[c][:, :], xT_hi[:, c, 0:SEQ].bitcast(F32),
                                            ALU.subtract).then_inc(a["xlo"], 1)
                for k in range(2):
                    dve.wait_ge(a["v_mm"], 2 * b + k + 1)
                    nc.vector.tensor_copy(v_a[:, 2 * k:2 * k + 2, :], split(bank[6 + k][:, :], 2)) \
                        .then_inc(a["v"], 1)

                def maximum(q):
                    dve.wait_ge(a["s_mm"], BT * b + q + 1)
                    steps.did(nc.vector.reduce_max(mx[:, q, 0:1], bank[q % 2][:, :], axis=X))
                    steps.wait()
                    nc.vector.tensor_scalar(nb[:, q, 0:1], mx[:, q, 0:1], -1.0 / 16.0, None, ALU.mult) \
                        .then_inc(a["max"], 1)

                def probabilities(q):
                    dve.wait_ge(a["exp"], BT * b + q + 1)
                    steps.did(nc.vector.reciprocal(rl[:, q, 0:1], lsum[:, q, 0:1]))
                    steps.wait()
                    nc.vector.tensor_scalar(p_a[:, q % 2, :], p_a[:, q % 2, :], rl[:, q, 0:1], None, ALU.mult) \
                        .then_inc(a["p"], 1)

                maximum(0)
                for q in range(1, BT):
                    maximum(q)
                    probabilities(q - 1)
                probabilities(BT - 1)
                dve.wait_ge(a["bias"], b + 1)
                for k in range(2):
                    dve.wait_ge(a["o_mm"], 2 * b + k + 1)
                    xt = x_tok[:, bass.ds(BT * b + 2 * k, 2), :]
                    nc.vector.tensor_tensor(xt, xt, split(bank[6 + k][:, :], 2), ALU.add).then_inc(a["x"], 1)
                assert steps.n == STEPS_A, steps.n

        def ffn_dve(dve, s, x_ready, x_count):
            steps = Steps(dve, s["step"])
            dve.wait_ge(x_ready, x_count)
            normalise(steps, 0, s["xn"], TILES)
            for hb in range(BATCHES):
                for c in range(DC):
                    dve.wait_ge(s["xhi"], DC * hb + c + 1)
                    tok = slice(hb * SEQ, (hb + 1) * SEQ)
                    nc.vector.tensor_tensor(xT_lo[:, c, tok], bank[2 * hb + c][:, :],
                                            xT_hi[:, c, tok].bitcast(F32), ALU.subtract).then_inc(s["xlo"], 1)

            dve.wait_ge(s["logits_mm"], 1)
            logits = split(bank[6][:, 0:TILES * E], TILES)
            steps.did(nc.vector.reduce_max(small[:, 0, :], logits, axis=X))
            steps.wait()
            nc.vector.tensor_tensor(route[:, 0], logits, spread(small[:, 0, :], E), ALU.subtract) \
                .then_inc(s["logit"], 1)

            def shared_weights(j):
                dve.wait_ge(s["whi"], j + 1)
                nc.vector.tensor_tensor(wf_lo[:, j % 2, :], raw[:, j % 2, 0:SW],
                                        wf_hi[:, j % 2, :].bitcast(F32), ALU.subtract).then_inc(s["wlo"], 1)

            shared_weights(0)
            dve.wait_ge(s["exp"], 1)
            steps.did(nc.vector.reduce_sum(small[:, 1, :], route[:, 1], axis=X))
            steps.wait()
            steps.did(nc.vector.reciprocal(small[:, 2, :], small[:, 1, :]))
            steps.wait()
            steps.did(nc.vector.tensor_tensor(route[:, 2], route[:, 1], spread(small[:, 2, :], E), ALU.mult))
            steps.wait()
            for i in range(TILES):
                steps.did(nc.vector.max(top[:, i, :], route[:, 2, i, :]))
            steps.wait()
            for i in range(TILES):
                steps.did(nc.vector.max_index(top_ids[:, i, :], top[:, i, :], route[:, 2, i, :]))
            steps.did(nc.vector.reduce_sum(small[:, 0, :], top[:, :, 0:TOP_K], axis=X))
            steps.wait()
            steps.did(nc.vector.tensor_scalar(small[:, 1, :], small[:, 0, :], 1e-20, None, ALU.add))
            dve.wait_ge(ids_ready, 1)
            ids = expert_ids[:, :].unsqueeze(1).to_broadcast([P, TOP_K, E])
            for i in range(TILES):
                chosen = top_ids[:, i, 0:TOP_K].unsqueeze(2).to_broadcast([P, TOP_K, E])
                steps.did(nc.vector.tensor_tensor(matches[:, i], ids, chosen, ALU.is_equal))
            steps.wait()
            steps.did(nc.vector.reciprocal(small[:, 2, :], small[:, 1, :]))
            steps.did(nc.vector.reduce_sum(route[:, 3], matches.rearrange("p i k e -> p i e k"), axis=X))
            steps.wait()
            nc.vector.tensor_copy(picked[:, :, :], route[:, 3]).then_inc(s["picked"], 1)
            base = expert_ids[:, :].unsqueeze(1).to_broadcast([P, TILES, E])
            steps.did(nc.vector.scalar_tensor_tensor(route[:, 4], base, float(CAP), route[:, 3], ALU.mult,
                                                     ALU.mult))
            steps.wait()
            steps.did(nc.vector.tensor_tensor(route[:, 4], route[:, 4], route[:, 3], ALU.add))
            dve.wait_ge(s["pos_mm"], 1)
            before_me = split(bank[6][:, 0:TILES * E], TILES)
            steps.did(nc.vector.scalar_tensor_tensor(route[:, 3], before_me, float(CAP), route[:, 3], ALU.is_lt,
                                                     ALU.mult))
            steps.wait()
            steps.did(nc.vector.tensor_tensor(route[:, 5], before_me, route[:, 4], ALU.add))
            steps.wait()
            steps.did(nc.vector.tensor_tensor(route[:, 5], route[:, 5], route[:, 3], ALU.mult))
            steps.wait()
            for i in range(TILES):
                steps.did(nc.vector.max(top[:, i, :], route[:, 5, i, :]))
            steps.wait()
            slots = top[:, :, 0:TOP_K]
            rest = route[:, 0].rearrange("p i e -> p (i e)")[:, 0:TILES * TOP_K] \
                .rearrange("p (i k) -> p i k", i=TILES)
            steps.did(nc.vector.tensor_scalar(rest, slots, 0.5, NOWHERE, ALU.is_lt, ALU.mult))
            steps.wait()
            nc.vector.scalar_tensor_tensor(slot_ids[:, :, :], slots, -1.0, rest, ALU.add, ALU.add) \
                .then_inc(s["slots"], 1)
            steps.did(nc.vector.tensor_tensor(route[:, 4], route[:, 2], route[:, 3], ALU.mult))
            steps.wait()
            steps.did(nc.vector.tensor_tensor(route[:, 4], route[:, 4], spread(small[:, 2, :], E), ALU.mult))
            for i in range(TILES):
                mine = route[:, 5, i, :].unsqueeze(1).to_broadcast([P, TOP_K, E])
                slot = top[:, i, 0:TOP_K].unsqueeze(2).to_broadcast([P, TOP_K, E])
                steps.did(nc.vector.tensor_tensor(matches[:, i], mine, slot, ALU.is_equal))
            steps.wait()
            for i in range(TILES):
                weight = route[:, 4, i, :].unsqueeze(1).to_broadcast([P, TOP_K, E])
                steps.did(nc.vector.tensor_tensor(matches[:, i], matches[:, i], weight, ALU.mult))
            steps.wait()
            steps.did(nc.vector.reduce_sum(slot_gate[:, :, :], matches, axis=X))

            shared_weights(1)
            for u in range(2 * SHT):
                j, h = u // 2, u % 2
                dve.wait_ge(s["u_mm"], u + 1)
                dve.wait_ge(s["silu"], u + 1)
                if u >= 2:
                    dve.wait_ge(s["hhi"], u - 1)
                nc.vector.tensor_tensor(hid[:, h, :], gated[:, h, :], bank[5][:, :], ALU.mult) \
                    .then_inc(s["hid"], 1)
                dve.wait_ge(s["hhi"], u + 1)
                if u >= 2:
                    dve.wait_ge(s["d_mm"], u - 1)
                nc.vector.tensor_tensor(h_lo[:, h, :], hid[:, h, :], h_hi[:, h, :].bitcast(F32),
                                        ALU.subtract).then_inc(s["hlo"], 1)
                if h == 0 and 1 <= j < SHT - 1:
                    shared_weights(j + 1)
            for h in range(2):
                dve.wait_ge(s["d_mm"], 2 * (SHT - 1) + h + 1)
                nc.vector.tensor_copy(yT[:, 1, h * SEQ:(h + 1) * SEQ], bank[2 * h + 1][:, :]) \
                    .then_inc(s["y1"], 1)
            for k in range(TILES // 2):
                dve.wait_ge(s["yt_mm"], k + 1)
                xt = x_tok[:, 2 * k:2 * k + 2, :]
                nc.vector.tensor_tensor(xt, xt, split(bank[4 + k][:, :], 2), ALU.add).then_inc(s["x"], 1)

            def split_rows(k, par, early=False):
                e = 2 * k + par
                if not early:
                    dve.wait_ge(s["gu_mm"], ST * e - ST)
                for c in range(DC):
                    x = slice(c * CAP, (c + 1) * CAP)
                    dve.wait_ge(s["thi"], DC * e + c + 1)
                    nc.vector.tensor_tensor(xe_lo[:, par, x], bank[c][:, 0:CAP], xe_hi[:, par, x].bitcast(F32),
                                            ALU.subtract).then_inc(s["tlo"], 1)

            def hidden(u, v, early=False):
                dve.wait_ge(s["gate"], u + 1)
                if not (early and v < 2):
                    dve.wait_ge(s["ht_mm"], u - 1)
                nc.vector.tensor_tensor(h_sb[:, v % 2, :], gate_sb[:, v % 2, :], bank[2 + v % 2][:, F_EXP:GU],
                                        ALU.mult).then_inc(s["h"], 1)

            def split_hidden(u, v, early=False):
                dve.wait_ge(s["hthi"], u + 1)
                if not (early and v < 2):
                    dve.wait_ge(s["dn_mm"], u - 1)
                nc.vector.tensor_tensor(he_lo[0:F_HALF, v % 2, :], bank[4 + v % 2][0:F_HALF, 0:2 * P],
                                        he_hi[0:F_HALF, v % 2, :].bitcast(F32), ALU.subtract) \
                    .then_inc(s["htlo"], 1)

            def pair(k, early=False, end=False):
                for v in range(2 * ST):
                    par, m = v // ST, v % ST
                    u = 2 * ST * k + v
                    hidden(u, v, early)
                    if m == 0 and not (end and par):
                        split_rows(k + par, 1 - par, early and par == 0)
                    if not (early and v < 1):
                        split_hidden(u - 1, (v - 1) % (2 * ST), early)

            split_rows(0, 0, early=True)
            pair(0, early=True)
            with dve.Fori(1, E // 2 - 1) as k:
                pair(k)
            pair(E // 2 - 1, end=True)
            split_hidden(ST * E - 1, 2 * ST - 1)

            steps.wait()
            for i in range(TILES):
                dve.wait_ge((s["got0"], s["got1"])[i % 2], 16 * TOP_K * (i // 2 + 1))
                for k in range(TOP_K):
                    op = nc.vector.scalar_tensor_tensor(x_tok[:, i, :], picks[:, i % 2, k, :],
                                                        slot_gate[:, i, k:k + 1], x_tok[:, i, :], ALU.mult,
                                                        ALU.add)
                    if k < TOP_K - 1:
                        steps.did(op)
                        steps.wait()
                op.then_inc(s["x2"], 1)

        def attention_b_dve(dve):
            w_raw = split(w_raw_b, DC)
            for c in range(DC):
                dve.wait_ge(bb["whi"], 2 * c + 2)
                part_hi = halves[:, 0, c * WB:(c + 1) * WB]
                nc.vector.tensor_tensor(halves[:, 1, c * WB:(c + 1) * WB], w_raw[:, c, 0:WB],
                                        part_hi.bitcast(F32), ALU.subtract).then_inc(bb["wlo"], 1)
                nc.vector.tensor_tensor(wb(1, c, CHUNKS - 1), w_raw[:, c, WB:QKV_B],
                                        wb(0, c, CHUNKS - 1).bitcast(F32), ALU.subtract).then_inc(bb["wlo"], 1)
            dve.wait_ge(f[0]["x2"], TILES)
            dve.wait_ge(bb["tab"], 4)
            KQ = K_CHUNKS + Q_CHUNKS
            with dve.Fori(0, BATCHES) as b:
                steps = Steps(dve, bb["step"], b * STEPS_B)
                normalise(steps, BT * b, bb["xn"])
                for c in range(DC):
                    dve.wait_ge(bb["xhi"], DC * b + c + 1)
                    nc.vector.tensor_tensor(xT_lo[:, c, 0:SEQ], bank[c][:, :], xT_hi[:, c, 0:SEQ].bitcast(F32),
                                            ALU.subtract).then_inc(bb["xlo"], 1)

                def residual(i):
                    dve.wait_ge(bb["o_mm"], NKV * (BT * b + i + 1))
                    xt = x_tok[:, bass.ds(BT * b + i, 1), :].rearrange("p o d -> p (o d)")
                    nc.vector.tensor_tensor(xt, xt, bank[4][:, 0:D], ALU.add).then_inc(bb["x"], 1)

                def rotate(i, c, newton):
                    n = KQ * i + c
                    tab = 2 if c < K_CHUNKS else 0
                    heads = split(bank[c % 2][:, :], CH)
                    dve.wait_ge(bb["sq"], KQ * BT * b + n + 1)
                    if n >= 2:
                        dve.wait_ge(bb["rot"], KQ * BT * b + n - 1)
                    cos = tables[:, tab, i, :].unsqueeze(1).to_broadcast([P, CH, HD])
                    nc.vector.tensor_tensor(rope_a[:, c % 2], heads, cos, ALU.mult).then_inc(bb["rot_a"], 1)
                    newton()
                    for half in range(2):
                        to = slice(half * HD // 2, (half + 1) * HD // 2)
                        of = slice((1 - half) * HD // 2, (2 - half) * HD // 2)
                        sin = tables[:, tab + 1, i, to].unsqueeze(1).to_broadcast([P, CH, HD // 2])
                        last = nc.vector.tensor_tensor(rope_b[:, c % 2, :, to], heads[:, :, of], sin, ALU.mult)
                        if half == 0:
                            newton()
                    last.then_inc(bb["rot_b"], 1)

                def sums(i, c):
                    dve.wait_ge(bb["sq"], KQ * (BT * b + i) + c + 1)
                    nc.vector.reduce_sum(ss[:, i % 2, c * CH:(c + 1) * CH], split(squares[:, c % 2, :], CH),
                                         axis=X).then_inc(bb["sum"], 1)

                def maximum(i, g, newton):
                    n = NKV * i + g
                    keys = slice(0 if i else P, 2 * P)
                    dve.wait_ge(bb["s_mm"], NKV * BT * b + n + 1)
                    nc.vector.memset(turn[:, :], 0.0)
                    for h in range(2):
                        of = slice(2 * P * h + (0 if i else P), 2 * P * (h + 1))
                        steps.did(nc.vector.tensor_tensor_reduce(
                            out=s_b[:, n % 2, h, keys], in0=bank[5 + n % 2][:, of],
                            in1=mask[:, :, :].rearrange("p k s -> p (k s)")[:, keys], scale=1.0, scalar=-3e38,
                            op0=ALU.add, op1=ALU.max, accum_out=mx[:, n % 4, h:h + 1]))
                        newton()
                    steps.wait()
                    nc.vector.scalar_tensor_tensor(nb[:, n % 4, :], mx[:, n % 4, :], -1.0,
                                                   rqs[:, i % 2, 2 * g:2 * g + 2], ALU.mult, ALU.mult) \
                        .then_inc(bb["max"], 1)

                def probabilities(i, g, newton):
                    n = NKV * i + g
                    keys = slice(0 if i else P, 2 * P)
                    dve.wait_ge(bb["exp"], NKV * BT * b + n + 1)
                    steps.did(nc.vector.reciprocal(rl[:, n % 4, :], lsum[:, n % 4, :]))
                    newton()
                    steps.wait()
                    for h in range(2):
                        last = nc.vector.tensor_scalar(p_b[:, n % 2, h, keys], p_b[:, n % 2, h, keys],
                                                       rl[:, n % 4, h:h + 1], None, ALU.mult)
                    last.then_inc(bb["p"], 1)
                    newton()

                class Norms:

                    def __init__(self, i):
                        self.i, self.k, self.keys, self.on = i, 0, True, False

                    def start(self, c):
                        if c in (K_CHUNKS - 1, KQ - 1):
                            self.on, self.k, self.keys = True, 0, c == K_CHUNKS - 1

                    def step(self):
                        if not self.on:
                            return
                        heads = slice(0, NKV) if self.keys else slice(NKV, NKV + NQ)
                        n = heads.stop - heads.start
                        if self.k == 0:
                            dve.wait_ge(bb["sum"], KQ * (BT * b + self.i) + (K_CHUNKS if self.keys else KQ))
                        if self.k < STEPS_RSQRT:
                            rsqrt_step(self.k, steps, ss[:, self.i % 2, heads], EPS_RMS, 1.0 / HD, n)
                        elif self.keys:
                            steps.wait()
                            nc.vector.tensor_copy(rk[:, self.i % 2, :], rstd[:, 0, 0:n]).then_inc(bb["rk"], 1)
                            self.on = False
                        else:
                            steps.wait()
                            steps.did(nc.vector.tensor_scalar(rqs[:, self.i % 2, :], rstd[:, 0, 0:n], SCALE_B,
                                                              None, ALU.mult))
                            self.on = False
                        self.k += 1

                    def finish(self):
                        while self.on:
                            self.step()

                norms = Norms(0)
                for c in range(KQ):
                    rotate(0, c, norms.step)
                    sums(0, c)
                    norms.start(c)
                    norms.finish()
                maximum(0, 0, norms.step)
                for i in range(BT):
                    norms = Norms(i + 1)
                    for g in range(NKV):
                        probabilities(i, g, norms.step)
                        if g + 1 < NKV:
                            maximum(i, g + 1, norms.step)
                        if g == K_CHUNKS + 1:
                            norms.finish()
                        if i + 1 < BT and g < KQ:
                            rotate(i + 1, g, norms.step)
                            sums(i + 1, g)
                            norms.start(g)
                        else:
                            for _ in range(3):
                                norms.step()
                    norms.finish()
                    if i + 1 < BT:
                        maximum(i + 1, 0, norms.step)
                    if i:
                        residual(i - 1)
                residual(BT - 1)
                assert steps.n == STEPS_B, steps.n

        @block.vector
        def _(dve):
            attention_a_dve(dve)
            ffn_dve(dve, f[0], a["x"], 2 * BATCHES)
            attention_b_dve(dve)
            ffn_dve(dve, f[1], bb["x"], TILES)

        def ffn_pool(pool, s):
            pool.wait_ge(s["slots"], 1)
            for i in range(TILES):
                for k in range(TOP_K):
                    nc.gpsimd.indirect_dma_start(
                        out=slot_rows, out_offset=bass.IndirectOffsetOnAxis(ap=slot_ids[:, i, k:k + 1], axis=0),
                        in_=xn[:, i, :], in_offset=None, bounds_check=SLOTS - 1, oob_is_err=False) \
                        .then_inc(s["sent"], 16)

            def split_gate_up(k, par, early=False):
                e = 2 * k + par
                pool.wait_ge(s["whi"], e + SHT + 1)
                if not early:
                    pool.wait_ge(s["gu_mm"], ST * e - ST)
                w = slice(0, DC * GU)
                nc.gpsimd.tensor_tensor(we_lo[:, par, w], raw[:, 1 - par, w], we_hi[:, par, w].bitcast(F32),
                                        ALU.subtract).then_inc(s["ewlo"], 1)

            def split_down(k, par, early=False):
                e = 2 * k + par
                pool.wait_ge(s["dhi"], e + 1)
                if not early:
                    pool.wait_ge(s["dn_mm"], ST * e - ST)
                w = slice(DC * GU, EW)
                nc.gpsimd.tensor_tensor(we_lo[0:F_HALF, par, w], raw[0:F_HALF, 1 - par, w],
                                        we_hi[0:F_HALF, par, w].bitcast(F32), ALU.subtract) \
                    .then_inc(s["edlo"], 1)

            for par in range(2):
                split_gate_up(0, par, early=True)
                split_down(0, par, early=True)
            with pool.Fori(1, E // 2) as k:
                for par in range(2):
                    split_gate_up(k, par)
                    split_down(k, par)
            for par in range(2):
                pool.wait_ge((s["out0"], s["out1"])[par], 16 * (E // 2))
            for i in range(TILES):
                if i >= 2:
                    pool.wait_ge(s["x2"], i - 1)
                for k in range(TOP_K):
                    nc.gpsimd.indirect_dma_start(
                        out=picks[:, i % 2, k, :], out_offset=None, in_=expert_out,
                        in_offset=bass.IndirectOffsetOnAxis(ap=slot_ids[:, i, k:k + 1], axis=0),
                        bounds_check=SLOTS - 1, oob_is_err=False).then_inc((s["got0"], s["got1"])[i % 2], 16)

        @block.gpsimd
        def _(pool):
            nc.gpsimd.iota(expert_ids[:, :], pattern=[[1, E]], base=0, channel_multiplier=0,
                           allow_small_or_imprecise_dtypes=True).then_inc(ids_ready, 1)
            nc.gpsimd.memset(zeros, 0.0).then_inc(zeros_ready, 1)
            pool.wait_ge(wo_a_loaded, 32)
            with pool.Fori(0, BATCHES) as b:
                pool.wait_ge(a["xn"], BT * b + BT)
                xt = x_tok[:, bass.ds(BT * b, BT), :]
                nc.gpsimd.tensor_tensor(xt, xt, b_out_sb.unsqueeze(1).to_broadcast([P, BT, D]), ALU.add) \
                    .then_inc(a["bias"], 1)
            pool.wait_ge(cleared, 16 * (SLOTS // P // (2 * TOP_K)))
            ffn_pool(pool, f[0])
            pool.wait_ge(rope_loaded, 16 * 7)
            pool.wait_ge(f[0]["x2"], TILES)
            for k in range(4):
                nc.gpsimd.tensor_tensor(tables[:, k], rope_raw[:, k % 2],
                                        scales_raw[:, k, :].unsqueeze(1).to_broadcast([P, BT, HD]), ALU.mult) \
                    .then_inc(bb["tab"], 1)
            KQ = K_CHUNKS + Q_CHUNKS
            with pool.Fori(0, BATCHES) as b:
                for i in range(BT):
                    for c in range(KQ):
                        n = KQ * i + c
                        pool.wait_ge(bb["rot_a"], KQ * BT * b + n + 1)
                        pool.wait_ge(bb["rot_b"], KQ * BT * b + n + 1)
                        if c >= 4:
                            pool.wait_ge(bb["t_mm"], KQ * (BT * b + i) + T_ORDER.index(c - 2) + 1)
                        elif i:
                            last = c if c < K_CHUNKS else c + 2
                            pool.wait_ge(bb["t_mm"], KQ * (BT * b + i - 1) + T_ORDER.index(last) + 1)
                        nc.gpsimd.tensor_tensor(roped[PLACE[c]], rope_a[:, c % 2], rope_b[:, c % 2],
                                                ALU.add).then_inc(bb["rot"], 1)
                        if c == K_CHUNKS:
                            pool.wait_ge(bb["rk"], BT * b + i + 1)
                            pool.wait_ge(bb["rot"], KQ * BT * b + n)
                            for k in range(K_CHUNKS):
                                nc.gpsimd.tensor_tensor(roped[k], roped[k],
                                                        spread(rk[:, i % 2, k * CH:(k + 1) * CH], HD),
                                                        ALU.mult).then_inc(bb["krot"], 1)
            ffn_pool(pool, f[1])


def constants():
    one = np.uint16(0x3F80)
    identity = np.eye(P, dtype=np.float32)
    before = np.stack([np.triu(np.full((P, P), one), 1), np.full((P, P), one)], 1)
    frac = np.arange(0, HD, 2, dtype=np.float32) / HD
    angle = np.arange(SEQ, dtype=np.float32)[:, None] / np.float32(10000.0) ** frac
    cos, sin = np.cos(angle), np.sin(angle)
    rope = np.stack([np.concatenate([cos, cos], 1), np.concatenate([-sin, sin], 1)])
    rope = np.ascontiguousarray(rope.reshape(2, BT, P, HD).transpose(2, 0, 1, 3)).astype(np.float32)
    q, s = np.arange(P)[:, None], np.arange(P)[None, :]
    mask = np.stack([np.where(s > q, 0, MASKED), np.where(s <= q, 0, MASKED)], 1).astype(np.float32)
    return identity, before, rope, mask


def kernel(L0_attn_a_hidden_states, L0_attn_a_w_qkv, L0_attn_a_b_qkv, L0_attn_a_w_out, L0_attn_a_b_out,
           L0_attn_b_q_kernel, L0_attn_b_kv_kernel, L0_attn_b_out_kernel, L0_attn_b_q_norm_scale,
           L0_attn_b_k_norm_scale, L0_ffn_wg_router, L0_ffn_w_gate, L0_ffn_w_up, L0_ffn_w_down,
           L0_ffn_ws_gate, L0_ffn_ws_up, L0_ffn_ws_down):
    import concourse.bacc as bacc
    from concourse.bass_utils import run_bass_kernel_spmd

    def arr(t):
        return np.asarray(t)

    x = arr(L0_attn_a_hidden_states)
    kv = arr(L0_attn_b_kv_kernel)
    w_qkv_b = np.concatenate([kv[0], arr(L0_attn_b_q_kernel), kv[1]])
    w_qkv_b = w_qkv_b.transpose(1, 0, 2).reshape(DC, P, QKV_B).transpose(1, 0, 2)

    pad = SHT * P - F_SH

    def hidden_tiles(w):
        w = np.pad(arr(w), ((0, 0), (0, pad)))
        return w.reshape(DC, P, SHT, P).transpose(2, 1, 0, 3).reshape(SHT, P, D)

    w_shared = np.concatenate([hidden_tiles(L0_ffn_ws_gate), hidden_tiles(L0_ffn_ws_up),
                               np.pad(arr(L0_ffn_ws_down), ((0, pad), (0, 0))).reshape(SHT, P, D)], 2)
    w_gate_up = np.concatenate([arr(L0_ffn_w_gate), arr(L0_ffn_w_up)], 2)
    w_gate_up = w_gate_up.reshape(E, DC, P, GU).transpose(0, 2, 1, 3).reshape(E, P, DC * GU)
    w_down = arr(L0_ffn_w_down).reshape(E, 2, F_HALF, D).transpose(0, 2, 1, 3).reshape(E, F_HALF, 2 * D)
    identity, before, rope, mask = constants()
    arrays = {
        "x": x.reshape(TOK, D),
        "w_qkv_a": arr(L0_attn_a_w_qkv).T,
        "b_qkv_a": arr(L0_attn_a_b_qkv).reshape(6, P).T,
        "w_out_a": arr(L0_attn_a_w_out).T,
        "b_out_a": arr(L0_attn_a_b_out),
        "w_qkv_b": w_qkv_b,
        "w_out_b": arr(L0_attn_b_out_kernel),
        "q_scale": arr(L0_attn_b_q_norm_scale),
        "k_scale": arr(L0_attn_b_k_norm_scale),
        "w_router": arr(L0_ffn_wg_router).T,
        "w_shared": w_shared,
        "w_gate_up": w_gate_up,
        "w_down": w_down,
        "identity": identity,
        "before": before,
        "rope": rope,
        "mask": mask,
    }
    arrays = {f"in_{n}": np.ascontiguousarray(v) for n, v in arrays.items()}
    nc = bacc.Bacc("TRN2", target_bir_lowering=False, num_devices=1)
    args = [nc.dram_tensor(n, v.shape, mybir.dt.from_np(v.dtype), kind="ExternalInput").ap()
            for n, v in arrays.items()]
    out = nc.dram_tensor("out_x", (TOK, D), F32, kind="ExternalOutput").ap()
    slot_rows, expert_out = (nc.dram_tensor(n, (SLOTS, D), F32, kind="Internal").ap()
                             for n in ("slot_rows", "expert_out"))
    program(nc, *args, slot_rows, expert_out, out)
    r = run_bass_kernel_spmd(nc, [arrays], core_ids=[0])
    return r.results[0]["out_x"].reshape(x.shape)
```

```python
from contextlib import ExitStack

import concourse.bass as bass
import numpy as np
from concourse import mybir

ALU = mybir.AluOpType
ACT = mybir.ActivationFunctionType
F32 = mybir.dt.float32
F32R = mybir.dt.float32r
BF16 = mybir.dt.bfloat16
I32 = mybir.dt.int32
U16 = mybir.dt.uint16
U32 = mybir.dt.uint32
X = mybir.AxisListType.X

P = 128
D = 256
DC = D // P
TOK = 1024
TILES = TOK // P
BATCHES = 2
BT = TILES // BATCHES
SEQ = BT * P

E = 32
TOP_K = 6
F_EXP = 176
F_SH = 352
CAP = 2 * (TOK * TOP_K // E)
SLOTS = E * CAP
ST = 2
MAIN = ST * P
assert CAP == MAIN + P
MOST_FULL = min(E, (TOK * TOP_K) // (MAIN + 1))
CLEARED = 16 * (SLOTS // P // (2 * TOP_K) + -(-E // (2 * TOP_K)))
ROUNDS = (MOST_FULL + 7) // 8
F_HALF = F_EXP // 2
GU = 2 * F_EXP
EW = DC * GU + 2 * D
SHT = (F_SH + P - 1) // P
SW = 3 * D
LOGITS, PICKS, PLACES = range(1, 4)
FULL = 1 + BATCHES * PLACES
NOWHERE = 1.0e6

SCORE_BANKS = (0, 1, 4, 5)

NQ = 16
NKV = 8
HD = 128
WINDOW = 128
assert WINDOW == P
QKV_B = (NQ + 2 * NKV) * HD
WB = QKV_B - 4 * HD
CH = 4
K_CHUNKS = NKV // CH
Q_CHUNKS = NQ // CH
CHUNKS = 2 * K_CHUNKS + Q_CHUNKS
T_ORDER = [2, 3, 0, 1, 4, 5]
PLACE = [0, 1, 2, 3, 2, 3]
T_STEP = [3, 4, 4, 5, 6, 7]
SCALE_B = 0.08838834764831845
EPS_LN = 1e-5
EPS_RMS = 1e-6
MASKED = -1e30
OVER = 21504
STEPS_RSQRT = 12
STEPS_LN = 2 * BT + STEPS_RSQRT
STEPS_A = STEPS_LN + 2 * BT
STEPS_B = STEPS_LN + BT * (2 * STEPS_RSQRT + 1) + 3 * NKV * BT
RSQRT_MAGIC = float(0x5F3759DF)


class Steps:

    def __init__(self, engine, sem, base=0):
        self.engine, self.sem, self.base, self.n = engine, sem, base, 0

    def did(self, instruction):
        self.n += 1
        return instruction.then_inc(self.sem, 1)

    def wait(self):
        self.engine.wait_ge(self.sem, self.base + self.n)


def program(nc, x_in, w_qkv_a, b_qkv_a, w_out_a, b_out_a, w_qkv_b, w_out_b, q_scale, k_scale, w_router,
            w_shared, w_gate_up, w_down, identity_in, before_in, rope_in, mask_in, slot_rows, expert_out, out):
    with ExitStack() as ctx:
        def sb(name, shape, dt=F32):
            return ctx.enter_context(nc.sbuf_tensor(name, shape, dt))

        def sem(name):
            return ctx.enter_context(nc.semaphore(name))

        x_tok = sb("x_tok", [P, TILES, D])
        xn = sb("xn", [P, TILES, D])
        xT_hi = sb("xT_hi", [P, DC, TOK], F32R)
        xT_lo = sb("xT_lo", [P, DC, TOK], F32R)
        w_out_b_sb = sb("w_out_b_sb", [P, NQ, D])
        halves = sb("halves", [P, 2, DC * WB], F32R)
        raw = sb("raw", [P, 2, EW])
        gate_sb = sb("gate_sb", [P, 2, F_EXP])
        h_sb = sb("h_sb", [P, 2, F_EXP])
        identity = sb("identity", [P, P])
        before = sb("before", [P, 2, P], BF16)
        mask = sb("mask", [P, 2, HD])
        wr_hi = sb("wr_hi", [P, DC, P], F32R)
        wr_lo = sb("wr_lo", [P, DC, P], F32R)
        b_qkv_sb = sb("b_qkv_sb", [P, 6])
        stats = sb("stats", [P, TILES, 6])
        mean_var = sb("mean_var", [P, TILES, 2])
        rstd = sb("rstd", [P, 3, NQ])
        ss = sb("ss", [P, 2, CHUNKS * CH])
        rqs = sb("rqs", [P, 2, NQ])
        rk = sb("rk", [P, 2, NKV])
        mx = sb("mx", [P, 4, 2])
        nb = sb("nb", [P, 4, 2])
        lsum = sb("lsum", [P, 4, 2])
        rl = sb("rl", [P, 4, 2])
        small = sb("small", [P, 3, TILES])
        turn = sb("turn", [P, 1])
        pool_turn = sb("pool_turn", [P, 1])
        top = sb("top", [P, TILES, 8])
        over = sb("over", [P, OVER])

        def part(start, *shape):
            n = int(np.prod(shape))
            v = over[:, start:start + n]
            names = " ".join(f"d{k}" for k in range(len(shape)))
            if len(shape) > 1:
                v = v.rearrange(f"p ({names}) -> p {names}",
                                **{f"d{k}": s for k, s in enumerate(shape[:-1])})
            return v, start + n

        w_raw_b, _ = part(0, DC * QKV_B)
        w_raw_router, _ = part(0, DC, P)
        qT, at = part(0, 2, NQ, P)
        kT, at = part(at, 3, NKV, P)
        v_b, at = part(at, 3, NKV * HD)
        s_b, at = part(at, 2, 2, 2 * P)
        tables, at = part(at, 4, BT, HD)
        p_b, at = part(at, 2, 2, 2 * P)
        pT_b, at = part(at, 2, 2, 2 * P)
        encT, at = part(at, NQ, P)
        roped_01, at = part(at, 2, CH, HD)
        squares, at = part(at, 2, CH * HD)
        rope_a, at = part(at, 2, CH, HD)
        rope_b, at = part(at, 2, CH, HD)
        assert at <= OVER
        roped = [roped_01[:, 0], roped_01[:, 1]] + [
            xn[:, 2 * k:2 * k + 2, :].rearrange("p i (h d) -> p (i h) d", d=HD) for k in range(2)]
        rope_raw, at = part(8192, 2, BT, HD)
        scales_raw, at = part(at, 4, HD)
        w_raw_a, at = part(8192, DC, 3 * D)
        w_out_a_sb, at = part(at, DC, D)
        qkT, at = part(at, 2 * DC, SEQ)
        v_a, at = part(at, BT, D)
        p_a, at = part(at, 2, SEQ)
        pT_a, at = part(at, BT, SEQ)
        ctxT, at = part(at, DC, SEQ)
        b_out_sb, at = part(at, D)
        at = 9728
        route, at = part(at, 6, TILES, E)
        gated, at = part(at, 2, SEQ)
        hid, at = part(at, 2, SEQ)
        yT, at = part(at, DC, TOK)
        rows_in, at = part(at, 2, ST, D)
        rows_out, at = part(at, 2, ST, D)
        assert at <= OVER - 2 * TOP_K * D
        picks, at = part(OVER - 2 * TOP_K * D, 2, TOP_K, D)
        late_picks = raw.rearrange("p a n -> p (a n)")[:, 0:TOP_K * D].rearrange("p (k d) -> p k d", k=TOP_K)
        zeros = over[:, OVER - 2 * TOP_K * D:OVER]
        matches = zeros[:, 0:TILES * TOP_K * E].rearrange("p (i k e) -> p i k e", i=TILES, k=TOP_K)
        picked = sb("picked", [P, TILES, E], BF16)
        expert_ids = sb("expert_ids", [P, E])
        fuller = sb("fuller", [P, 2, E])
        full_top = sb("full_top", [P, 8 * ROUNDS])
        full_ids = sb("full_ids", [P, 8 * ROUNDS], I32)
        full_count = sb("full_count", [P, 1], I32)
        top_ids = sb("top_ids", [P, TILES, 8], U32)
        slot_ids = sb("slot_ids", [P, TILES, TOP_K], U32)
        slot_gate = sb("slot_gate", [P, TILES, TOP_K])

        bank = [ctx.enter_context(nc.psum_tensor(f"bank{k}", [P, 512], F32)) for k in range(8)]

        x_loaded = sem("x_loaded")
        made = sem("made")
        cleared = sem("cleared")
        const_loaded = sem("const_loaded")
        wa_loaded = sem("wa_loaded")
        wo_a_loaded = sem("wo_a_loaded")
        wb_loaded = sem("wb_loaded")
        rope_loaded = sem("rope_loaded")
        stored = sem("stored")
        added = sem("added")

        def phase(prefix, names):
            return {n: sem(f"{prefix}_{n}") for n in names.split()}

        a = phase("a", "step xn xnT xhi xlo whi wlo qk_mm qk v_mm v s_mm max exp p pt_mm pt ctx_mm ctx"
                       " o_mm x bias")
        f = [phase(f"f{k}", "step xn xnT xhi xlo route_mm logitT routed exp whi wlo g_mm u_mm"
                            " silu hid hhi hlo d_mm raw0 raw1 dn0 dn1 y0 y1 yt_mm x sent dhi ewlo edlo in0 in1 t_mm thi"
                            " tlo gu_mm gate h ht_mm hthi htlo dn_mm copied out0 out1 got0 got1 x2")
             for k in range(2)]
        bb = phase("b", "step xn xnT xhi xlo whi wlo tab proj sq rotated sum rk rot krot t_mm t v"
                        " s_mm max exp p pt_mm pt e_mm e o_mm x")
        block = ctx.enter_context(nc.Block())

        def split(t, n):
            return t.rearrange("p (c n) -> p c n", c=n)

        def rsqrt_step(k, steps, value, eps, scale, n):
            v, y, t = (rstd[:, m, 0:n] for m in (2, 0, 1))
            steps.wait()
            if k == 0:
                op = nc.vector.tensor_scalar(v, value, scale, eps, ALU.mult, ALU.add)
            elif k == 1:
                op = nc.vector.tensor_scalar(t.bitcast(I32), v.bitcast(I32), 1, None,
                                             ALU.logical_shift_right)
            elif k == 2:
                op = nc.vector.tensor_scalar(y.bitcast(I32), t.bitcast(I32), -1.0, RSQRT_MAGIC,
                                             ALU.mult, ALU.add)
            elif k % 3 == 0:
                op = nc.vector.scalar_tensor_tensor(t, v, -0.5, y, ALU.mult, ALU.mult)
            elif k % 3 == 1:
                op = nc.vector.tensor_tensor(t, t, y, ALU.mult)
            else:
                op = nc.vector.scalar_tensor_tensor(y, t, 1.5, y, ALU.add, ALU.mult)
            steps.did(op)

        def normalising(steps, first, ready, place=BT):
            tiles = [x_tok[:, bass.ds(first + i, 1), :].rearrange("p o d -> p (o d)") for i in range(BT)]
            for i in range(BT):
                yield steps.did(nc.vector.bn_stats(stats[:, i, :], tiles[i]))
            steps.wait()
            nc.vector.memset(turn[:, :], 0.0)
            for i in range(BT):
                yield steps.did(nc.vector.bn_aggr(mean_var[:, i, :], stats[:, i, :]))
            for k in range(STEPS_RSQRT):
                yield rsqrt_step(k, steps, mean_var[:, 0:BT, 1], EPS_LN, 1.0, BT)
            steps.wait()
            for i in range(BT):
                yield nc.vector.tensor_scalar(xn[:, place + i, :], tiles[i], mean_var[:, i, 0:1],
                                              rstd[:, 0, i:i + 1], ALU.subtract, ALU.mult).then_inc(ready, 1)

        def normalise(*what, **where):
            for _ in normalising(*what, **where):
                pass

        def xn_tile(i):
            return (i + BT) % TILES

        def transpose_batch(done):
            for c in range(DC):
                for i in range(BT):
                    last = nc.tensor.transpose(bank[c][:, i * P:(i + 1) * P], xn[:, BT + i, c * P:(c + 1) * P],
                                               identity[:, :])
                last.then_inc(done, 1)

        def matmul3(out, hi, lo, rhs_hi, rhs_lo, start, stop):
            nc.tensor.matmul(out, hi, rhs_lo, start=start, stop=False)
            nc.tensor.matmul(out, lo, rhs_hi, start=False, stop=False)
            return nc.tensor.matmul(out, hi, rhs_hi, start=False, stop=stop)

        wa_hi = halves[:, 0, 0:DC * 3 * D].rearrange("p (c n) -> p c n", c=DC)
        wa_lo = halves[:, 1, 0:DC * 3 * D].rearrange("p (c n) -> p c n", c=DC)

        def wb(k, c, chunk):
            n = CH * HD
            if chunk == CHUNKS - 1:
                return (xT_hi, xT_lo)[k][:, c, SEQ:SEQ + n]
            return halves[:, k, c * WB + chunk * n:c * WB + (chunk + 1) * n]

        def places(n, start, *shape):
            size = int(np.prod(shape))
            return [halves[:, k, start:start + n * size].rearrange("p (k n) -> p k n", k=n) for k in range(2)], \
                start + n * size

        (wf_hi, wf_lo), at = places(2, 0, SW)
        (h_hi, h_lo), at = places(2, at, SEQ)
        (we_hi, we_lo), at = places(2, at, EW)
        (xe_hi, xe_lo), at = places(2, at, DC, MAIN)
        (he_hi, he_lo), at = places(2, at, 2, P)
        assert at <= DC * WB

        def shared_loads(sp, s, first=0, end=SHT):
            for j in range(first, end):
                if j >= 2:
                    sp.wait_ge(s["whi"], j - 1)
                    sp.wait_ge(s["wlo"], j - 1)
                sp.dma_start(raw[:, j % 2, 0:SW], w_shared[j]).then_inc((s["raw0"], s["raw1"])[j % 2], 16)

        def expert_traffic(sp, s):
            ins, outs = (s["in0"], s["in1"]), (s["out0"], s["out1"])
            rows_of, out_of = (t.rearrange("(e r) d -> e r d", r=CAP) for t in (slot_rows, expert_out))
            row_view, out_view = (t[:, 0:MAIN, :].rearrange("e (p m) d -> e p (m d)", m=ST)
                                  for t in (rows_of, out_of))

            def gate_up(e, par, early=False):
                if early:
                    sp.wait_ge(s["wlo"], e + 2)
                else:
                    sp.wait_ge(s["ewlo"], e - 1)
                sp.dma_start(raw[:, 1 - par, 0:DC * GU],
                             w_gate_up[bass.ds(e, 1)].rearrange("o p n -> p (o n)")) \
                    .then_inc((s["raw1"], s["raw0"])[par], 16)

            def down(e, par, early=False):
                if not early:
                    sp.wait_ge(s["edlo"], e - 1)
                sp.dma_start(raw[0:F_HALF, 1 - par, DC * GU:EW],
                             w_down[bass.ds(e, 1)].rearrange("o p n -> p (o n)")) \
                    .then_inc((s["dn0"], s["dn1"])[par], 16)

            def rows(e, par, early=False):
                if not early:
                    sp.wait_ge(s["t_mm"], e - 1)
                sp.dma_start(rows_in[:, par].rearrange("p m d -> p (m d)"),
                             row_view[bass.ds(e, 1)].rearrange("o p n -> p (o n)")).then_inc(ins[par], 16)

            def results(e, par):
                sp.wait_ge(s["copied"], ST * e + ST)
                sp.dma_start(out_view[bass.ds(e, 1)].rearrange("o p n -> p (o n)"),
                             rows_out[:, par].rearrange("p m d -> p (m d)")).then_inc(outs[par], 16)

            for e in range(2):
                gate_up(e, e, early=True)
                down(e, e, early=True)
            sp.wait_ge(s["sent"], 16 * TILES * TOP_K)
            for e in range(2):
                rows(e, e, early=True)
            for e in range(2):
                rows(e + 2, e)
                gate_up(e + 2, e)
                if e:
                    results(e - 1, 1 - e)
                down(e + 2, e)
            with sp.Fori(1, E // 2 - 1) as k:
                for par in range(2):
                    e = 2 * k + par
                    rows(e + 2, par)
                    gate_up(e + 2, par)
                    results(e - 1, 1 - par)
                    down(e + 2, par)
            results(E - 3, (E - 3) % 2)

            sp.wait_ge(s["routed"], FULL)
            count = sp.value_load(full_count[0:1, 0:1], min_val=1, max_val=MOST_FULL)

            def load_more(j, first=False):
                for done in (s["ewlo"], s["edlo"], s["t_mm"]):
                    sp.wait_ge(done, E - 1 if first else j + E)
                e = sp.value_load(full_ids[0:1, bass.ds(j, 1)], min_val=0, max_val=E - 1)
                sp.dma_start(raw[:, 1, 0:DC * GU],
                             w_gate_up[bass.ds(e, 1)].rearrange("o p n -> p (o n)")).then_inc(s["raw1"], 16)
                sp.dma_start(raw[0:F_HALF, 1, DC * GU:EW],
                             w_down[bass.ds(e, 1)].rearrange("o p n -> p (o n)")).then_inc(s["dn0"], 16)
                sp.dma_start(rows_in[:, 0, 0, :], rows_of[bass.ds(e, 1), MAIN:CAP, :]
                             .rearrange("o p d -> p (o d)")).then_inc(s["in0"], 16)
                return e

            load_more(0, first=True)
            for e in range(E - 2, E):
                results(e, e % 2)
            with sp.Fori(0, count) as j:
                e = sp.value_load(full_ids[0:1, bass.ds(j, 1)], min_val=0, max_val=E - 1)
                load_more(j + 1)
                sp.wait_ge(s["copied"], j + (ST * E + 1))
                sp.dma_start(out_of[bass.ds(e, 1), MAIN:CAP, :].rearrange("o p d -> p (o d)"),
                             rows_out[:, 0, 0, :]).then_inc(s["out0"], 16)

        @block.sync
        def _(sp):
            xv = x_in.rearrange("(b i p) d -> b p i d", b=BATCHES, p=P)
            sp.dma_start(x_tok[:, 0:BT, :], xv[0]).then_inc(x_loaded, 16)
            sp.dma_start(identity[:, :], identity_in).then_inc(x_loaded, 16)
            sp.dma_start(w_raw_a[:, :, :], w_qkv_a.rearrange("(c p) n -> p c n", p=P)).then_inc(wa_loaded, 16)
            sp.dma_start(b_qkv_sb[:, :], b_qkv_a).then_inc(wa_loaded, 16)
            sp.dma_start(x_tok[:, BT:TILES, :], xv[1]).then_inc(const_loaded, 16)
            sp.dma_start(w_out_a_sb[:, :, :], w_out_a.rearrange("(c p) n -> p c n", p=P)) \
                .then_inc(wo_a_loaded, 16)
            sp.dma_start(b_out_sb, b_out_a.partition_broadcast(P)).then_inc(wo_a_loaded, 16)
            sp.dma_start(before[:, :, :].bitcast(U16), before_in).then_inc(const_loaded, 16)
            sp.dma_start(mask[:, :, :], mask_in).then_inc(const_loaded, 16)
            sp.dma_start(w_raw_router, w_router.rearrange("(c p) n -> p c n", p=P)) \
                .then_inc(const_loaded, 16)
            sp.wait_ge(made, 3)
            n = 2 * TOP_K * D
            clear = slot_rows.rearrange("(p m) d -> p (m d)", p=P)
            for k in range(SLOTS * D // P // n):
                sp.dma_start(clear[:, k * n:(k + 1) * n], zeros).then_inc(cleared, 16)
            rest = expert_out.rearrange("(e r) d -> r e d", r=CAP)[MAIN:CAP]
            for k in range(0, E, 2 * TOP_K):
                n = min(2 * TOP_K, E - k)
                sp.dma_start(rest[:, k:k + n, :], zeros[:, 0:n * D].rearrange("p (e d) -> p e d", e=n)) \
                    .then_inc(cleared, 16)
            sp.dma_start(w_out_b_sb[:, :, :], w_out_b.rearrange("n p d -> p n d")).then_inc(wb_loaded, 16)
            shared_loads(sp, f[0], end=2)
            sp.wait_ge(a["x"], 2 * BATCHES)
            sp.dma_start(w_raw_b, w_qkv_b.rearrange("p c n -> p (c n)")).then_inc(wb_loaded, 16)
            sp.dma_start(rope_raw, rope_in).then_inc(rope_loaded, 16)
            for k, s in enumerate((q_scale, k_scale)):
                sp.dma_start(scales_raw[:, 2 * k, :], s.partition_broadcast(P)).then_inc(rope_loaded, 16)
                for half in range(2):
                    sp.dma_start(scales_raw[:, 2 * k + 1, half * HD // 2:(half + 1) * HD // 2],
                                 s[(1 - half) * HD // 2:(2 - half) * HD // 2].partition_broadcast(P)) \
                        .then_inc(rope_loaded, 16)
            shared_loads(sp, f[0], first=2)
            expert_traffic(sp, f[0])
            sp.wait_ge(f[0]["x2"], TILES)
            shared_loads(sp, f[1])
            expert_traffic(sp, f[1])
            for i in range(TILES):
                sp.wait_ge(f[1]["x2"], i + 1)
                sp.dma_start(out[i * P:(i + 1) * P, :], x_tok[:, i, :]).then_inc(stored, 16)
            sp.wait_ge(stored, 16 * TILES)

        def attention_a_pe(pe):
            pe.wait_ge(x_loaded, 32)
            with pe.Fori(0, BATCHES) as b:
                pe.wait_ge(a["xn"], BT * b + BT)
                transpose_batch(a["xnT"])
                pe.wait_ge(a["whi"], 1)
                pe.wait_ge(a["wlo"], 1)
                pe.wait_ge(wo_a_loaded, 32)
                pe.wait_ge(a["xhi"], DC * b + DC)
                pe.wait_ge(a["xlo"], DC * b + DC)
                for m in range(2 * DC):
                    for c in range(DC):
                        last = matmul3(bank[2 + m][:, :], wa_hi[:, c, m * P:(m + 1) * P],
                                       wa_lo[:, c, m * P:(m + 1) * P], xT_hi[:, c, 0:SEQ], xT_lo[:, c, 0:SEQ],
                                       c == 0, c == DC - 1)
                    last.then_inc(a["qk_mm"], 1)
                for i in range(BT):
                    for c in range(DC):
                        last = matmul3(bank[6 + i // 2][:, (i % 2) * D:(i % 2 + 1) * D],
                                       xT_hi[:, c, i * P:(i + 1) * P], xT_lo[:, c, i * P:(i + 1) * P],
                                       wa_hi[:, c, 2 * D:3 * D], wa_lo[:, c, 2 * D:3 * D],
                                       c == 0, c == DC - 1)
                    if i % 2:
                        last.then_inc(a["v_mm"], 1)
                pe.wait_ge(a["qk"], 2 * DC * b + 2 * DC)

                def scores(q):
                    for c in range(DC):
                        last = nc.tensor.matmul(bank[SCORE_BANKS[q]][:, :], qkT[:, c, q * P:(q + 1) * P],
                                                qkT[:, DC + c, :], start=c == 0, stop=c == DC - 1)
                    last.then_inc(a["s_mm"], 1)

                def probs_transposed(q):
                    pe.wait_ge(a["p"], BT * b + q + 1)
                    if q >= 2:
                        pe.wait_ge(a["pt"], BT * b + q - 1)
                    for k in range(BT):
                        last = nc.tensor.transpose(bank[2 + q % 2][:, k * P:(k + 1) * P],
                                                   p_a[:, q % 2, k * P:(k + 1) * P], identity[:, :])
                    last.then_inc(a["pt_mm"], 1)

                for q in range(BT):
                    scores(q)
                for q in range(BT):
                    probs_transposed(q)
                pe.wait_ge(a["pt"], BT * b + BT)
                pe.wait_ge(a["v"], 2 * b + 2)
                for m in range(DC):
                    for k in range(BT):
                        last = nc.tensor.matmul(bank[4 + m][:, :], v_a[:, k, m * P:(m + 1) * P], pT_a[:, k, :],
                                                start=k == 0, stop=k == BT - 1)
                    last.then_inc(a["ctx_mm"], 1)
                pe.wait_ge(a["ctx"], DC * b + DC)
                for i in range(BT):
                    for c in range(DC):
                        last = nc.tensor.matmul(bank[6 + i // 2][:, (i % 2) * D:(i % 2 + 1) * D],
                                                ctxT[:, c, i * P:(i + 1) * P], w_out_a_sb[:, c, :],
                                                start=c == 0, stop=c == DC - 1)
                    if i % 2:
                        last.then_inc(a["o_mm"], 1)

        def ffn_pe(pe, s, first_xn):
            def count_earlier(hb):
                pe.wait_ge(s["routed"], PICKS + PLACES * hb)
                for i in range(BT * hb, BT * hb + BT):
                    for k in range(i + 1):
                        last = nc.tensor.matmul(bank[6][:, i * E:(i + 1) * E], before[:, 0 if k == i else 1, :],
                                                picked[:, k, :], start=k == 0, stop=k == i)
                if hb == BATCHES - 1:
                    for k in range(TILES):
                        last = nc.tensor.matmul(bank[6][:, TILES * E:(TILES + 1) * E], before[:, 1, :],
                                                picked[:, k, :], start=k == 0, stop=k == TILES - 1)
                last.then_inc(s["route_mm"], 1)

            pe.wait_ge(const_loaded, 64)
            pe.wait_ge(a["wlo"], 2)
            for hb in range(BATCHES):
                if hb == 0:
                    pe.wait_ge(first_xn, BT * (BATCHES + 1))
                else:
                    pe.wait_ge(s["xn"], BT)
                for c in range(DC):
                    for i in range(BT):
                        last = nc.tensor.transpose(bank[2 * hb + c][:, i * P:(i + 1) * P],
                                                   xn[:, xn_tile(BT * hb + i), c * P:(c + 1) * P], identity[:, :])
                    last.then_inc(s["xnT"], 1)
                pe.wait_ge(s["xhi"], DC * hb + DC)
                pe.wait_ge(s["xlo"], DC * hb + DC)
                for c in range(DC):
                    tok = slice(hb * SEQ, (hb + 1) * SEQ)
                    last = matmul3(bank[6 + hb][:, :], wr_hi[:, c, :], wr_lo[:, c, :], xT_hi[:, c, tok],
                                   xT_lo[:, c, tok], c == 0, c == DC - 1)
                last.then_inc(s["route_mm"], 1)
                pe.wait_ge(s["logitT"], hb + 1)
                for i in range(BT):
                    last = nc.tensor.transpose(bank[6 + hb][:, i * P:(i + 1) * P],
                                               hid[:, hb, i * P:(i + 1) * P], identity[:, :])
                last.then_inc(s["route_mm"], 1)
                if hb == 0:
                    count_earlier(0)

            def up(j, h):
                u = 2 * j + h
                tok = slice(h * SEQ, (h + 1) * SEQ)
                if h == 0:
                    pe.wait_ge(s["whi"], j + 1)
                    pe.wait_ge(s["wlo"], j + 1)
                if u == 1:
                    pe.wait_ge(s["routed"], LOGITS + PLACES)
                if u >= 2:
                    pe.wait_ge(s["silu"], u - 1)
                for c in range(DC):
                    w = slice(c * P, (c + 1) * P)
                    last = matmul3(bank[4 + 3 * h][:, :], wf_hi[:, j % 2, w], wf_lo[:, j % 2, w],
                                   xT_hi[:, c, tok], xT_lo[:, c, tok], c == 0, c == DC - 1)
                last.then_inc(s["g_mm"], 1)
                if u >= 1:
                    pe.wait_ge(s["hid"], u)
                for c in range(DC):
                    w = slice(D + c * P, D + (c + 1) * P)
                    last = matmul3(bank[5][:, :], wf_hi[:, j % 2, w], wf_lo[:, j % 2, w],
                                   xT_hi[:, c, tok], xT_lo[:, c, tok], c == 0, c == DC - 1)
                last.then_inc(s["u_mm"], 1)

            def down(j, h):
                u = 2 * j + h
                pe.wait_ge(s["hhi"], u + 1)
                pe.wait_ge(s["hlo"], u + 1)
                for m in range(DC):
                    w = slice(2 * D + m * P, 2 * D + (m + 1) * P)
                    last = matmul3(bank[2 * h + m][:, :], wf_hi[:, j % 2, w], wf_lo[:, j % 2, w],
                                   h_hi[:, h, :], h_lo[:, h, :], j == 0, j == SHT - 1)
                last.then_inc(s["d_mm"], 1)

            up(0, 0)
            count_earlier(1)
            for u in range(1, 2 * SHT):
                up(u // 2, u % 2)
                down((u - 1) // 2, (u - 1) % 2)
            down(SHT - 1, 1)
            for i in range(TILES):
                if i % BT == 0:
                    pe.wait_ge(s["y0"], i // BT + 1)
                    pe.wait_ge(s["y1"], i // BT + 1)
                for m in range(DC):
                    last = nc.tensor.transpose(
                        bank[4 + i // 2][:, (i % 2) * D + m * P:(i % 2) * D + (m + 1) * P],
                        yT[:, m, i * P:(i + 1) * P], identity[:, :])
                if i % 2:
                    last.then_inc(s["yt_mm"], 1)

            def turn_rows(k, par, first=False):
                e = 2 * k + par
                pe.wait_ge((s["in0"], s["in1"])[par], 16 * k + 16)
                if first:
                    pe.wait_ge(s["x"], TILES // 2)
                else:
                    pe.wait_ge(s["tlo"], DC * e)
                for c in range(DC):
                    for m in range(ST):
                        last = nc.tensor.transpose(bank[c][:, m * P:(m + 1) * P],
                                                   rows_in[:, par, m, c * P:(c + 1) * P], identity[:, :])
                last.then_inc(s["t_mm"], 1)

            def gate_up(k, par, m, early):
                e = 2 * k + par
                u = ST * e + m
                v = ST * par + m
                if m == 0:
                    pe.wait_ge(s["whi"], e + SHT + 1)
                    pe.wait_ge(s["ewlo"], e + 1)
                    pe.wait_ge(s["tlo"], DC * e + DC)
                if not (early and v < 2):
                    pe.wait_ge(s["h"], u - 1)
                for c in range(DC):
                    x = slice(c * MAIN + m * P, c * MAIN + (m + 1) * P)
                    w = slice(c * GU, (c + 1) * GU)
                    last = matmul3(bank[2 + v % 2][:, 0:GU], xe_hi[:, par, x], xe_lo[:, par, x],
                                   we_hi[:, par, w], we_lo[:, par, w], c == 0, c == DC - 1)
                last.then_inc(s["gu_mm"], 1)

            def turn_hidden(u, v, early=False):
                pe.wait_ge(s["h"], u + 1)
                if not (early and v < 2):
                    pe.wait_ge(s["htlo"], u - 1)
                for k in range(2):
                    last = nc.tensor.transpose(bank[4 + v % 2][0:F_HALF, k * P:(k + 1) * P],
                                               h_sb[:, v % 2, k * F_HALF:(k + 1) * F_HALF], identity[:, :])
                last.then_inc(s["ht_mm"], 1)

            def down_rows(e, par, m, u, v, early=False):
                if m == 0:
                    pe.wait_ge(s["dhi"], e + 1)
                    pe.wait_ge(s["edlo"], e + 1)
                pe.wait_ge(s["htlo"], u + 1)
                if not (early and v < 2):
                    pe.wait_ge(s["copied"], u - 1)
                for k in range(2):
                    h = slice(k * P, (k + 1) * P)
                    w = slice(DC * GU + k * D, DC * GU + (k + 1) * D)
                    last = matmul3(bank[6 + v % 2][:, 0:D], he_hi[0:F_HALF, v % 2, h], he_lo[0:F_HALF, v % 2, h],
                                   we_hi[0:F_HALF, par, w], we_lo[0:F_HALF, par, w], k == 0, k == 1)
                last.then_inc(s["dn_mm"], 1)

            def pair(k, early=False, end=False):
                for v in range(2 * ST):
                    par, m = v // ST, v % ST
                    u = 2 * ST * k + v
                    gate_up(k, par, m, early)
                    if m == 0 and not (end and par):
                        turn_rows(k + par, 1 - par)
                    if not (early and v < 1):
                        turn_hidden(u - 1, (v - 1) % (2 * ST), early)
                    if not (early and v < 2):
                        w = (v - 2) % (2 * ST)
                        down_rows((u - 2 - w % ST) // ST if early else 2 * k + (v - 2) // ST, w // ST, w % ST,
                                  u - 2, w, early)

            turn_rows(0, 0, first=True)
            pair(0, early=True)
            with pe.Fori(1, E // 2 - 1) as k:
                pair(k)
            pair(E // 2 - 1, end=True)

            def turn_more(j):
                pe.wait_ge(s["in0"], 16 * j + 16 * (E // 2 + 1))
                pe.wait_ge(s["tlo"], DC * j + DC * E)
                for c in range(DC):
                    last = nc.tensor.transpose(bank[c][:, 0:P], rows_in[:, 0, 0, c * P:(c + 1) * P],
                                               identity[:, :])
                last.then_inc(s["t_mm"], 1)

            u = ST * E
            turn_hidden(u - 1, 2 * ST - 1)
            down_rows(E - 1, 1, ST - 2, u - 2, 2 * ST - 2)
            turn_more(0)
            down_rows(E - 1, 1, ST - 1, u - 1, 2 * ST - 1)
            count = pe.value_load(full_count[0:1, 0:1], min_val=1, max_val=MOST_FULL)
            with pe.Fori(0, count) as j:
                pe.wait_ge(s["whi"], j + (E + SHT + 1))
                pe.wait_ge(s["ewlo"], j + (E + 1))
                pe.wait_ge(s["tlo"], DC * j + DC * (E + 1))
                pe.wait_ge(s["h"], j + ST * E)
                for c in range(DC):
                    x, w = slice(c * MAIN, c * MAIN + P), slice(c * GU, (c + 1) * GU)
                    last = matmul3(bank[2][:, 0:GU], xe_hi[:, 0, x], xe_lo[:, 0, x], we_hi[:, 0, w],
                                   we_lo[:, 0, w], c == 0, c == DC - 1)
                last.then_inc(s["gu_mm"], 1)
                pe.wait_ge(s["h"], j + (ST * E + 1))
                pe.wait_ge(s["htlo"], j + ST * E)
                for k in range(2):
                    last = nc.tensor.transpose(bank[4][0:F_HALF, k * P:(k + 1) * P],
                                               h_sb[:, 0, k * F_HALF:(k + 1) * F_HALF], identity[:, :])
                last.then_inc(s["ht_mm"], 1)
                pe.wait_ge(s["dhi"], j + (E + 1))
                pe.wait_ge(s["edlo"], j + (E + 1))
                pe.wait_ge(s["htlo"], j + (ST * E + 1))
                pe.wait_ge(s["copied"], j + ST * E)
                for k in range(2):
                    h, w = slice(k * P, (k + 1) * P), slice(DC * GU + k * D, DC * GU + (k + 1) * D)
                    last = matmul3(bank[6][:, 0:D], he_hi[0:F_HALF, 0, h], he_lo[0:F_HALF, 0, h],
                                   we_hi[0:F_HALF, 0, w], we_lo[0:F_HALF, 0, w], k == 0, k == 1)
                last.then_inc(s["dn_mm"], 1)
                turn_more(j + 1)

        def attention_b_pe(pe):
            pe.wait_ge(bb["whi"], 2 * DC)
            pe.wait_ge(bb["wlo"], 2 * DC)
            pe.wait_ge(wb_loaded, 32)
            with pe.Fori(0, BATCHES) as b:
                pe.wait_ge(bb["xn"], BT * b + BT)
                transpose_batch(bb["xnT"])
                pe.wait_ge(bb["xhi"], DC * b + DC)
                pe.wait_ge(bb["xlo"], DC * b + DC)

                def project(i, c):
                    n = CHUNKS * i + c
                    if n >= 2:
                        prev = CHUNKS * ((n - 2) // CHUNKS), (n - 2) % CHUNKS
                        if prev[1] < K_CHUNKS + Q_CHUNKS:
                            done = (K_CHUNKS + Q_CHUNKS) * (prev[0] // CHUNKS) + prev[1] + 1
                            pe.wait_ge(bb["sq"], (K_CHUNKS + Q_CHUNKS) * BT * b + done)
                            pe.wait_ge(bb["rotated"], (K_CHUNKS + Q_CHUNKS) * BT * b + done)
                        else:
                            pe.wait_ge(bb["v"], K_CHUNKS * BT * b + K_CHUNKS * (prev[0] // CHUNKS)
                                       + prev[1] - K_CHUNKS - Q_CHUNKS + 1)
                    for k in range(DC):
                        t = slice(i * P, (i + 1) * P)
                        last = matmul3(bank[n % 2][:, :], xT_hi[:, k, t], xT_lo[:, k, t], wb(0, k, c),
                                       wb(1, k, c), k == 0, k == DC - 1)
                    last.then_inc(bb["proj"], 1)

                def transposed(i, m):
                    c = T_ORDER[m]
                    base = (K_CHUNKS + Q_CHUNKS) * (BT * b + i)
                    if c < K_CHUNKS:
                        pe.wait_ge(bb["krot"], K_CHUNKS * (BT * b + i) + c + 1)
                    else:
                        pe.wait_ge(bb["rot"], base + c + 1)
                    if i or m:
                        pe.wait_ge(bb["t"], base + m)
                    for k in range(CH):
                        last = nc.tensor.transpose(bank[2][:, k * P:(k + 1) * P], roped[PLACE[c]][:, k, :],
                                                   identity[:, :])
                    last.then_inc(bb["t_mm"], 1)

                def scores(i, g):
                    n = NKV * i + g
                    base = NKV * BT * b
                    if g == 0:
                        pe.wait_ge(bb["t"], (K_CHUNKS + Q_CHUNKS) * (BT * b + i + 1))
                    if n >= 2:
                        pe.wait_ge(bb["max"], base + n - 1)
                    for h in range(2):
                        for k in range(2) if i else (1,):
                            last = nc.tensor.matmul(bank[5 + n % 2][:, (2 * h + k) * P:(2 * h + k + 1) * P],
                                                    qT[:, i % 2, 2 * g + h, :], kT[:, (i - 1 + k) % 3, g, :],
                                                    start=True, stop=True)
                    last.then_inc(bb["s_mm"], 1)

                def probs_transposed(i, g):
                    n = NKV * i + g
                    base = NKV * BT * b
                    pe.wait_ge(bb["p"], base + n + 1)
                    if n >= 1:
                        pe.wait_ge(bb["pt"], base + n)
                    for k in range(2) if i else (1,):
                        for h in range(2):
                            last = nc.tensor.transpose(bank[3][:, (2 * k + h) * P:(2 * k + h + 1) * P],
                                                       p_b[:, n % 2, h, k * P:(k + 1) * P], identity[:, :])
                    last.then_inc(bb["pt_mm"], 1)

                def encode(i, g):
                    n = NKV * i + g
                    base = NKV * BT * b
                    pe.wait_ge(bb["pt"], base + n + 1)
                    if g == 0:
                        pe.wait_ge(bb["v"], K_CHUNKS * (BT * b + i + 1))
                    if n >= 1:
                        pe.wait_ge(bb["e"], base + n)
                    for k in range(2) if i else (1,):
                        last = nc.tensor.matmul(bank[7][:, 0:D],
                                                v_b[:, (i - 1 + k) % 3, g * HD:(g + 1) * HD],
                                                pT_b[:, n % 2, k, :], start=(k == 0 or i == 0), stop=k == 1)
                    last.then_inc(bb["e_mm"], 1)

                def project_out(i, g):
                    pe.wait_ge(bb["e"], NKV * (BT * b + i) + g + 1)
                    if g == 0 and i:
                        pe.wait_ge(bb["x"], BT * b + i)
                    for h in range(2 * g, 2 * g + 2):
                        last = nc.tensor.matmul(bank[4][:, 0:D], encT[:, h, :], w_out_b_sb[:, h, :],
                                                start=h == 0, stop=h == NQ - 1)
                    last.then_inc(bb["o_mm"], 1)

                for c in range(CHUNKS):
                    project(0, c)
                for m in range(len(T_ORDER)):
                    transposed(0, m)
                scores(0, 0)
                scores(0, 1)
                for i in range(BT):
                    for g in range(NKV):
                        if g + 2 < NKV:
                            scores(i, g + 2)
                        if i + 1 < BT:
                            project(i + 1, g)
                        if g:
                            encode(i, g - 1)
                        probs_transposed(i, g)
                        if i + 1 < BT and g in T_STEP:
                            transposed(i + 1, T_STEP.index(g))
                        if i:
                            project_out(i - 1, g)
                        if i + 1 < BT and T_STEP.count(g) == 2:
                            transposed(i + 1, T_STEP.index(g) + 1)
                    encode(i, NKV - 1)
                    if i + 1 < BT:
                        scores(i + 1, 0)
                        scores(i + 1, 1)
                for g in range(NKV):
                    project_out(BT - 1, g)

        @block.tensor
        def _(pe):
            attention_a_pe(pe)
            ffn_pe(pe, f[0], a["xn"])
            attention_b_pe(pe)
            ffn_pe(pe, f[1], bb["xn"])

        def attention_a_act(act):
            act.wait_ge(wa_loaded, 32)
            nc.scalar.activation(wa_hi, w_raw_a, ACT.Copy).then_inc(a["whi"], 1)
            act.wait_ge(const_loaded, 64)
            nc.scalar.activation(wr_hi[:, :, :], w_raw_router, ACT.Copy).then_inc(a["whi"], 1)
            with act.Fori(0, BATCHES) as b:
                for c in range(DC):
                    act.wait_ge(a["xnT"], DC * b + c + 1)
                    nc.scalar.activation(xT_hi[:, c, 0:SEQ], bank[c][:, :], ACT.Copy).then_inc(a["xhi"], 1)
                for m in range(2 * DC):
                    act.wait_ge(a["qk_mm"], 2 * DC * b + m + 1)
                    nc.scalar.activation(qkT[:, m, :], bank[2 + m][:, :], ACT.Identity,
                                         bias=b_qkv_sb[:, m:m + 1]).then_inc(a["qk"], 1)

                def exponentials(q):
                    act.wait_ge(a["max"], BT * b + q + 1)
                    if q >= 2:
                        act.wait_ge(a["pt_mm"], BT * b + q - 1)
                    nc.scalar.activation(p_a[:, q % 2, :], bank[SCORE_BANKS[q]][:, :], ACT.Exp, bias=nb[:, q, 0:1],
                                         scale=1.0 / 16.0, accum_out=lsum[:, q, 0:1]).then_inc(a["exp"], 1)

                def copy_probs(q):
                    act.wait_ge(a["pt_mm"], BT * b + q + 1)
                    nc.scalar.activation(pT_a[:, :, q * P:(q + 1) * P], split(bank[2 + q % 2][:, :], BT),
                                         ACT.Copy).then_inc(a["pt"], 1)

                exponentials(0)
                for q in range(1, BT):
                    exponentials(q)
                    copy_probs(q - 1)
                copy_probs(BT - 1)
                for m in range(DC):
                    act.wait_ge(a["ctx_mm"], DC * b + m + 1)
                    nc.scalar.activation(ctxT[:, m, :], bank[4 + m][:, :], ACT.Identity,
                                         bias=b_qkv_sb[:, 2 * DC + m:2 * DC + m + 1]).then_inc(a["ctx"], 1)

        def ffn_act(act, s):
            def split_tokens(hb):
                for c in range(DC):
                    act.wait_ge(s["xnT"], DC * hb + c + 1)
                    nc.scalar.activation(xT_hi[:, c, hb * SEQ:(hb + 1) * SEQ], bank[2 * hb + c][:, :], ACT.Copy) \
                        .then_inc(s["xhi"], 1)
                act.wait_ge(s["route_mm"], 3 * hb + 1)
                nc.scalar.activation(hid[:, hb, :], bank[6 + hb][:, :], ACT.Copy).then_inc(s["logitT"], 1)

            def shared_weights(j):
                act.wait_ge((s["raw0"], s["raw1"])[j % 2], 16 * (j // 2) + 16)
                if j >= 2:
                    act.wait_ge(s["d_mm"], 2 * (j - 1))
                nc.scalar.activation(wf_hi[:, j % 2, :], raw[:, j % 2, 0:SW], ACT.Copy).then_inc(s["whi"], 1)

            def exponentials(hb):
                act.wait_ge(s["routed"], LOGITS + PLACES * hb)
                tiles = slice(BT * hb, BT * hb + BT)
                nc.scalar.activation(route[:, 1, tiles], route[:, 0, tiles], ACT.Exp).then_inc(s["exp"], 1)

            split_tokens(0)
            exponentials(0)
            shared_weights(0)
            split_tokens(1)
            exponentials(1)
            shared_weights(1)
            for u in range(2 * SHT):
                j, h = u // 2, u % 2
                act.wait_ge(s["g_mm"], u + 1)
                if u >= 2:
                    act.wait_ge(s["hid"], u - 1)
                nc.scalar.activation(gated[:, h, :], bank[4 + 3 * h][:, :], ACT.Silu).then_inc(s["silu"], 1)
                act.wait_ge(s["hid"], u + 1)
                if u >= 2:
                    act.wait_ge(s["d_mm"], u - 1)
                nc.scalar.activation(h_hi[:, h, :], hid[:, h, :], ACT.Copy).then_inc(s["hhi"], 1)
                if h == 0 and 1 <= j < SHT - 1:
                    shared_weights(j + 1)
            for h in range(2):
                act.wait_ge(s["d_mm"], 2 * (SHT - 1) + h + 1)
                nc.scalar.activation(yT[:, 0, h * SEQ:(h + 1) * SEQ], bank[2 * h][:, :], ACT.Copy) \
                    .then_inc(s["y0"], 1)

            def split_gate_up(k, par, early=False):
                act.wait_ge((s["raw1"], s["raw0"])[par], 16 * k + (32, 48)[par])
                if not early:
                    act.wait_ge(s["gu_mm"], ST * (2 * k + par) - ST)
                nc.scalar.activation(we_hi[:, par, 0:DC * GU], raw[:, 1 - par, 0:DC * GU], ACT.Copy) \
                    .then_inc(s["whi"], 1)

            def split_down(k, par, early=False):
                act.wait_ge((s["dn0"], s["dn1"])[par], 16 * k + 16)
                if not early:
                    act.wait_ge(s["dn_mm"], ST * (2 * k + par) - ST)
                nc.scalar.activation(we_hi[0:F_HALF, par, DC * GU:EW], raw[0:F_HALF, 1 - par, DC * GU:EW],
                                     ACT.Copy).then_inc(s["dhi"], 1)

            def split_rows(k, par, early=False):
                e = 2 * k + par
                act.wait_ge(s["t_mm"], e + 1)
                if not early:
                    act.wait_ge(s["gu_mm"], ST * e - ST)
                for c in range(DC):
                    nc.scalar.activation(xe_hi[:, par, c * MAIN:(c + 1) * MAIN], bank[c][:, 0:MAIN], ACT.Copy) \
                        .then_inc(s["thi"], 1)

            def silu(u, v, early=False):
                act.wait_ge(s["gu_mm"], u + 1)
                if not (early and v < 2):
                    act.wait_ge(s["h"], u - 1)
                nc.scalar.activation(gate_sb[:, v % 2, :], bank[2 + v % 2][:, 0:F_EXP], ACT.Silu) \
                    .then_inc(s["gate"], 1)

            def split_hidden(u, v, early=False):
                act.wait_ge(s["ht_mm"], u + 1)
                if not (early and v < 2):
                    act.wait_ge(s["dn_mm"], u - 1)
                nc.scalar.activation(he_hi[0:F_HALF, v % 2, :], bank[4 + v % 2][0:F_HALF, 0:2 * P], ACT.Copy) \
                    .then_inc(s["hthi"], 1)

            def copy_result(k, u, v, early=False):
                act.wait_ge(s["dn_mm"], u + 1)
                if v % ST == 0 and not early:
                    act.wait_ge((s["out0"], s["out1"])[v // ST], 16 * k)
                nc.scalar.activation(rows_out[:, v // ST, v % ST, :], bank[6 + v % 2][:, 0:D], ACT.Copy) \
                    .then_inc(s["copied"], 1)

            def pair(k, early=False, end=False, behind=0):
                for v in range(2 * ST):
                    par, m = v // ST, v % ST
                    u = 2 * ST * k + v
                    if m == 0 and not (end and par):
                        split_gate_up(k + par, 1 - par, early and par == 0)
                    silu(u, v, early)
                    if not (early and v < 1):
                        split_hidden(u - 1, (v - 1) % (2 * ST), early)
                    if m == 0 and not (end and par):
                        split_rows(k + par, 1 - par, early and par == 0)
                    if not (early and v < 2):
                        copy_result(k if v >= 2 else k - 1, u - 2, (v - 2) % (2 * ST), early or (behind and v < 2))
                    if m == 1 and not (end and par):
                        split_down(k + par, 1 - par, early and par == 0)

            split_gate_up(0, 0, early=True)
            split_down(0, 0, early=True)
            split_rows(0, 0, early=True)
            pair(0, early=True)
            pair(1, behind=1)
            with act.Fori(2, E // 2 - 1) as k:
                pair(k)
            pair(E // 2 - 1, end=True)

            def more_gate_up(j):
                act.wait_ge(s["raw1"], 16 * j + 16 * (E // 2 + 2))
                act.wait_ge(s["gu_mm"], j + ST * (E - 1))
                nc.scalar.activation(we_hi[:, 0, 0:DC * GU], raw[:, 1, 0:DC * GU], ACT.Copy) \
                    .then_inc(s["whi"], 1)

            def more_rows(j):
                act.wait_ge(s["t_mm"], j + (E + 1))
                for c in range(DC):
                    nc.scalar.activation(xe_hi[:, 0, c * MAIN:c * MAIN + P], bank[c][:, 0:P], ACT.Copy) \
                        .then_inc(s["thi"], 1)

            def more_down(j):
                act.wait_ge(s["dn0"], 16 * j + 16 * (E // 2 + 1))
                act.wait_ge(s["dn_mm"], j + ST * (E - 1))
                nc.scalar.activation(we_hi[0:F_HALF, 0, DC * GU:EW], raw[0:F_HALF, 1, DC * GU:EW], ACT.Copy) \
                    .then_inc(s["dhi"], 1)

            u = ST * E
            split_hidden(u - 1, 2 * ST - 1)
            more_gate_up(0)
            copy_result(E // 2 - 1, u - 2, 2 * ST - 2)
            more_rows(0)
            more_down(0)
            copy_result(E // 2 - 1, u - 1, 2 * ST - 1)
            count = act.value_load(full_count[0:1, 0:1], min_val=1, max_val=MOST_FULL)
            with act.Fori(0, count) as j:
                act.wait_ge(s["gu_mm"], j + (ST * E + 1))
                nc.scalar.activation(gate_sb[:, 0, :], bank[2][:, 0:F_EXP], ACT.Silu).then_inc(s["gate"], 1)
                act.wait_ge(s["ht_mm"], j + (ST * E + 1))
                nc.scalar.activation(he_hi[0:F_HALF, 0, :], bank[4][0:F_HALF, 0:2 * P], ACT.Copy) \
                    .then_inc(s["hthi"], 1)
                act.wait_ge(s["raw1"], 16 * j + 16 * (E // 2 + 3))
                nc.scalar.activation(we_hi[:, 0, 0:DC * GU], raw[:, 1, 0:DC * GU], ACT.Copy) \
                    .then_inc(s["whi"], 1)
                act.wait_ge(s["dn_mm"], j + (ST * E + 1))
                act.wait_ge(s["out0"], 16 * j + 16 * (E // 2))
                nc.scalar.activation(rows_out[:, 0, 0, :], bank[6][:, 0:D], ACT.Copy).then_inc(s["copied"], 1)
                more_rows(j + 1)
                act.wait_ge(s["dn0"], 16 * j + 16 * (E // 2 + 2))
                nc.scalar.activation(we_hi[0:F_HALF, 0, DC * GU:EW], raw[0:F_HALF, 1, DC * GU:EW], ACT.Copy) \
                    .then_inc(s["dhi"], 1)
            act.wait_ge(s["ewlo"], count + (E + 1))
            act.wait_ge(s["edlo"], count + (E + 1))
            nc.scalar.activation(gate_sb[:, 0, 0:1], expert_ids[:, 0:1], ACT.Copy)

        def attention_b_act(act):
            act.wait_ge(wb_loaded, 32)
            w_raw = split(w_raw_b, DC)
            for c in range(DC):
                nc.scalar.activation(halves[:, 0, c * WB:(c + 1) * WB], w_raw[:, c, 0:WB], ACT.Copy) \
                    .then_inc(bb["whi"], 1)
                nc.scalar.activation(wb(0, c, CHUNKS - 1), w_raw[:, c, WB:QKV_B], ACT.Copy).then_inc(bb["whi"], 1)
            with act.Fori(0, BATCHES) as b:
                for c in range(DC):
                    act.wait_ge(bb["xnT"], DC * b + c + 1)
                    nc.scalar.activation(xT_hi[:, c, 0:SEQ], bank[c][:, :], ACT.Copy).then_inc(bb["xhi"], 1)

                def square(i, c):
                    act.wait_ge(bb["proj"], CHUNKS * (BT * b + i) + c + 1)
                    src = bank[c % 2][:, :]
                    if c < K_CHUNKS + Q_CHUNKS:
                        n = (K_CHUNKS + Q_CHUNKS) * i + c
                        if n >= 2:
                            act.wait_ge(bb["sum"], (K_CHUNKS + Q_CHUNKS) * BT * b + n - 1)
                        nc.scalar.activation(squares[:, c % 2, :], src, ACT.Square).then_inc(bb["sq"], 1)
                    else:
                        k = (c - K_CHUNKS - Q_CHUNKS) * CH * HD
                        nc.scalar.activation(v_b[:, i % 3, k:k + CH * HD], src, ACT.Copy).then_inc(bb["v"], 1)

                def copy_transposed(i, m):
                    c = T_ORDER[m]
                    act.wait_ge(bb["t_mm"], (K_CHUNKS + Q_CHUNKS) * (BT * b + i) + m + 1)
                    if c < K_CHUNKS:
                        dst = kT[:, i % 3, c * CH:(c + 1) * CH, :]
                    else:
                        dst = qT[:, i % 2, (c - K_CHUNKS) * CH:(c - K_CHUNKS + 1) * CH, :]
                    nc.scalar.activation(dst, split(bank[2][:, :], CH), ACT.Copy).then_inc(bb["t"], 1)

                def exponentials(i, g):
                    n = NKV * i + g
                    keys = slice(0 if i else P, 2 * P)
                    act.wait_ge(bb["max"], NKV * BT * b + n + 1)
                    if n >= 2:
                        act.wait_ge(bb["pt_mm"], NKV * BT * b + n - 1)
                    for h in range(2):
                        last = nc.scalar.activation(p_b[:, n % 2, h, keys], s_b[:, n % 2, h, keys], ACT.Exp,
                                                    bias=nb[:, n % 4, h:h + 1],
                                                    scale=rqs[:, i % 2, 2 * g + h:2 * g + h + 1],
                                                    accum_out=lsum[:, n % 4, h:h + 1])
                    last.then_inc(bb["exp"], 1)

                def copy_probs(i, g):
                    n = NKV * i + g
                    act.wait_ge(bb["pt_mm"], NKV * BT * b + n + 1)
                    if n >= 2:
                        act.wait_ge(bb["e_mm"], NKV * BT * b + n - 1)
                    k = slice(0 if i else 1, 2)
                    nc.scalar.activation(pT_b[:, n % 2, k, :], split(bank[3][:, :], 2)[:, k, :],
                                         ACT.Copy).then_inc(bb["pt"], 1)

                def copy_encoded(i, g):
                    act.wait_ge(bb["e_mm"], NKV * (BT * b + i) + g + 1)
                    if i:
                        act.wait_ge(bb["o_mm"], NKV * (BT * b + i - 1) + g + 1)
                    nc.scalar.activation(encT[:, 2 * g:2 * g + 2, :], split(bank[7][:, 0:D], 2),
                                         ACT.Copy).then_inc(bb["e"], 1)

                for c in range(CHUNKS):
                    square(0, c)
                for m in range(len(T_ORDER)):
                    copy_transposed(0, m)
                exponentials(0, 0)
                for i in range(BT):
                    for g in range(NKV):
                        if i + 1 < BT:
                            square(i + 1, g)
                        if g + 1 < NKV:
                            exponentials(i, g + 1)
                        if g:
                            copy_encoded(i, g - 1)
                        copy_probs(i, g)
                        if i + 1 < BT and g in T_STEP:
                            copy_transposed(i + 1, T_STEP.index(g))
                        if i + 1 < BT and T_STEP.count(g) == 2:
                            copy_transposed(i + 1, T_STEP.index(g) + 1)
                    copy_encoded(i, NKV - 1)
                    if i + 1 < BT:
                        exponentials(i + 1, 0)

        @block.scalar
        def _(act):
            attention_a_act(act)
            ffn_act(act, f[0])
            attention_b_act(act)
            ffn_act(act, f[1])

        def spread(t, n):
            return t.unsqueeze(2).to_broadcast([P, t.shape[1], n])

        def attention_a_dve(dve):
            dve.wait_ge(x_loaded, 32)
            normalise(Steps(dve, a["step"]), 0, a["xn"])
            dve.wait_ge(a["whi"], 1)
            nc.vector.tensor_tensor(wa_lo, w_raw_a, wa_hi.bitcast(F32), ALU.subtract).then_inc(a["wlo"], 1)
            dve.wait_ge(const_loaded, 64)
            dve.wait_ge(a["whi"], 2)
            nc.vector.tensor_tensor(wr_lo[:, :, :], w_raw_router, wr_hi[:, :, :].bitcast(F32), ALU.subtract) \
                .then_inc(a["wlo"], 1)
            with dve.Fori(0, BATCHES) as b:
                steps = Steps(dve, a["step"], b * STEPS_A + STEPS_LN)
                for c in range(DC):
                    dve.wait_ge(a["xhi"], DC * b + c + 1)
                    nc.vector.tensor_tensor(xT_lo[:, c, 0:SEQ], bank[c][:, :], xT_hi[:, c, 0:SEQ].bitcast(F32),
                                            ALU.subtract).then_inc(a["xlo"], 1)
                for k in range(2):
                    dve.wait_ge(a["v_mm"], 2 * b + k + 1)
                    nc.vector.tensor_copy(v_a[:, 2 * k:2 * k + 2, :], split(bank[6 + k][:, :], 2)) \
                        .then_inc(a["v"], 1)

                def maximum(q):
                    dve.wait_ge(a["s_mm"], BT * b + q + 1)
                    steps.did(nc.vector.reduce_max(mx[:, q, 0:1], bank[SCORE_BANKS[q]][:, :], axis=X))
                    steps.wait()
                    nc.vector.tensor_scalar(nb[:, q, 0:1], mx[:, q, 0:1], -1.0 / 16.0, None, ALU.mult) \
                        .then_inc(a["max"], 1)

                def probabilities(q):
                    dve.wait_ge(a["exp"], BT * b + q + 1)
                    steps.did(nc.vector.reciprocal(rl[:, q, 0:1], lsum[:, q, 0:1]))
                    steps.wait()
                    nc.vector.tensor_scalar(p_a[:, q % 2, :], p_a[:, q % 2, :], rl[:, q, 0:1], None, ALU.mult) \
                        .then_inc(a["p"], 1)

                maximum(0)
                for q in range(1, BT):
                    maximum(q)
                    probabilities(q - 1)
                probabilities(BT - 1)
                normalise(steps, BT - BT * b, a["xn"])
                dve.wait_ge(a["bias"], b + 1)
                for k in range(2):
                    dve.wait_ge(a["o_mm"], 2 * b + k + 1)
                    xt = x_tok[:, bass.ds(BT * b + 2 * k, 2), :]
                    nc.vector.tensor_tensor(xt, xt, split(bank[6 + k][:, :], 2), ALU.add).then_inc(a["x"], 1)
                assert steps.n == STEPS_A, steps.n

        def add_experts(dve, s, steps, i, picks):
            dve.wait_ge((s["got0"], s["got1"])[i % 2], 16 * TOP_K * (i // 2 + 1))
            for k in range(TOP_K):
                op = nc.vector.scalar_tensor_tensor(x_tok[:, i, :], picks[:, k, :], slot_gate[:, i, k:k + 1],
                                                    x_tok[:, i, :], ALU.mult, ALU.add)
                if k < TOP_K - 1:
                    steps.did(op)
                    steps.wait()
            op.then_inc(s["x2"], 1)

        def ffn_dve(dve, s, x_ready, x_count, tiles, between=None):
            steps = Steps(dve, s["step"])

            def split_tokens(hb):
                for c in range(DC):
                    dve.wait_ge(s["xhi"], DC * hb + c + 1)
                    tok = slice(hb * SEQ, (hb + 1) * SEQ)
                    nc.vector.tensor_tensor(xT_lo[:, c, tok], bank[2 * hb + c][:, :],
                                            xT_hi[:, c, tok].bitcast(F32), ALU.subtract).then_inc(s["xlo"], 1)

            def shared_weights(j):
                dve.wait_ge(s["whi"], j + 1)
                nc.vector.tensor_tensor(wf_lo[:, j % 2, :], raw[:, j % 2, 0:SW],
                                        wf_hi[:, j % 2, :].bitcast(F32), ALU.subtract).then_inc(s["wlo"], 1)

            def less_maximum(hb):
                of = slice(BT * hb, BT * hb + BT)
                logits = split(bank[6 + hb][:, :], BT)[:, :, 0:E]
                dve.wait_ge(s["route_mm"], 3 * hb + 2)
                steps.did(nc.vector.reduce_max(small[:, 0, of], logits, axis=X))
                steps.wait()
                nc.vector.tensor_tensor(route[:, 0, of, :], logits, spread(small[:, 0, of], E), ALU.subtract) \
                    .then_inc(s["routed"], 1)

            def routing(hb):
                tiles = range(BT * hb, BT * hb + BT)
                of = slice(BT * hb, BT * hb + BT)
                dve.wait_ge(s["exp"], hb + 1)
                steps.did(nc.vector.reduce_sum(small[:, 1, of], route[:, 1, of], axis=X))
                steps.wait()
                steps.did(nc.vector.reciprocal(small[:, 2, of], small[:, 1, of]))
                steps.wait()
                steps.did(nc.vector.tensor_tensor(route[:, 2, of], route[:, 1, of], spread(small[:, 2, of], E),
                                                  ALU.mult))
                steps.wait()
                for i in tiles:
                    steps.did(nc.vector.max(top[:, i, :], route[:, 2, i, :]))
                steps.wait()
                for i in tiles:
                    steps.did(nc.vector.max_index(top_ids[:, i, :], top[:, i, :], route[:, 2, i, :]))
                dve.wait_ge(made, 1)
                every = expert_ids[:, :].unsqueeze(1).to_broadcast([P, BT, E])
                least = top[:, of, TOP_K - 1:TOP_K].to_broadcast([P, BT, E])
                steps.did(nc.vector.tensor_tensor(route[:, 4, of], route[:, 2, of], least, ALU.is_gt))
                steps.did(nc.vector.tensor_tensor(route[:, 3, of], route[:, 2, of], least, ALU.is_equal))
                steps.wait()
                steps.did(nc.vector.tensor_tensor(
                    route[:, 5, of], every, top_ids[:, of, TOP_K - 1:TOP_K].to_broadcast([P, BT, E]), ALU.is_le))
                steps.wait()
                steps.did(nc.vector.tensor_tensor(route[:, 3, of], route[:, 3, of], route[:, 5, of], ALU.mult))
                steps.wait()
                nc.vector.tensor_tensor(picked[:, of, :], route[:, 3, of], route[:, 4, of], ALU.add) \
                    .then_inc(s["routed"], 1)
                steps.did(nc.vector.tensor_tensor(route[:, 3, of], route[:, 3, of], route[:, 4, of], ALU.add))
                steps.did(nc.vector.reduce_sum(small[:, 0, of], top[:, of, 0:TOP_K], axis=X))
                steps.wait()
                steps.did(nc.vector.tensor_scalar(small[:, 1, of], small[:, 0, of], 1e-20, None, ALU.add))
                steps.did(nc.vector.scalar_tensor_tensor(route[:, 4, of], every, float(CAP), route[:, 3, of],
                                                         ALU.mult, ALU.mult))
                steps.wait()
                steps.did(nc.vector.reciprocal(small[:, 2, of], small[:, 1, of]))
                steps.did(nc.vector.tensor_tensor(route[:, 4, of], route[:, 4, of], route[:, 3, of], ALU.add))
                if hb == 0:
                    shared_weights(0)
                dve.wait_ge(s["route_mm"], 3 * hb + 3)
                before_me = split(bank[6][:, BT * hb * E:BT * (hb + 1) * E], BT)
                steps.did(nc.vector.scalar_tensor_tensor(route[:, 3, of], before_me, float(CAP), route[:, 3, of],
                                                         ALU.is_lt, ALU.mult))
                steps.wait()
                steps.did(nc.vector.tensor_tensor(route[:, 5, of], before_me, route[:, 4, of], ALU.add))
                steps.wait()
                steps.did(nc.vector.tensor_tensor(route[:, 5, of], route[:, 5, of], route[:, 3, of], ALU.mult))
                steps.wait()
                for i in tiles:
                    steps.did(nc.vector.max(top[:, i, :], route[:, 5, i, :]))
                steps.wait()
                slots = top[:, of, 0:TOP_K]
                nowhere = route[:, 0, of].rearrange("p i e -> p (i e)")[:, 0:BT * TOP_K] \
                    .rearrange("p (i k) -> p i k", i=BT)
                steps.did(nc.vector.tensor_scalar(nowhere, slots, 0.5, NOWHERE, ALU.is_lt, ALU.mult))
                steps.wait()
                nc.vector.scalar_tensor_tensor(slot_ids[:, of, :], slots, -1.0, nowhere, ALU.add, ALU.add) \
                    .then_inc(s["routed"], 1)

            split_tokens(0)
            dve.wait_ge(x_ready, x_count)
            second = normalising(steps, BT, s["xn"], place=0)
            for _ in range(2 * BT + 4):
                next(second)
            less_maximum(0)
            routing(0)
            for _ in second:
                pass
            split_tokens(1)
            less_maximum(1)
            routing(1)
            steps.did(nc.vector.tensor_tensor(route[:, 4], route[:, 2], route[:, 3], ALU.mult))
            steps.wait()
            steps.did(nc.vector.tensor_tensor(route[:, 4], route[:, 4], spread(small[:, 2, :], E), ALU.mult))
            dve.wait_ge(cleared, CLEARED)
            for i in range(TILES):
                mine = route[:, 5, i, :].unsqueeze(1).to_broadcast([P, TOP_K, E])
                slot = top[:, i, 0:TOP_K].unsqueeze(2).to_broadcast([P, TOP_K, E])
                steps.did(nc.vector.tensor_tensor(matches[:, i], mine, slot, ALU.is_equal))
            steps.wait()
            for i in range(TILES):
                weight = route[:, 4, i, :].unsqueeze(1).to_broadcast([P, TOP_K, E])
                steps.did(nc.vector.tensor_tensor(matches[:, i], matches[:, i], weight, ALU.mult))
            steps.wait()
            steps.did(nc.vector.reduce_sum(slot_gate[:, :, :], matches, axis=X))
            fill = bank[6][:, TILES * E:(TILES + 1) * E]
            steps.did(nc.vector.tensor_scalar(fuller[:, 0, :], fill, float(MAIN), None, ALU.is_gt))
            steps.did(nc.vector.tensor_scalar(fuller[:, 1, :], expert_ids[:, :], -1.0, float(E), ALU.mult,
                                              ALU.add))
            steps.wait()
            steps.did(nc.vector.reduce_sum(small[:, 0, 0:1], fuller[:, 0, :], axis=X))
            steps.did(nc.vector.tensor_tensor(fuller[:, 1, :], fuller[:, 0, :], fuller[:, 1, :], ALU.mult))
            for r in range(ROUNDS):
                steps.wait()
                best = full_top[:, 8 * r:8 * r + 8]
                steps.did(nc.vector.max(best, fuller[:, 1, :]))
                if r < ROUNDS - 1:
                    steps.wait()
                    steps.did(nc.vector.scalar_tensor_tensor(fuller[:, 1, :], fuller[:, 1, :], best[:, 7:8],
                                                             fuller[:, 1, :], ALU.is_lt, ALU.mult))
            steps.wait()
            steps.did(nc.vector.tensor_scalar(full_top[:, :], full_top[:, :], 1.0, None, ALU.max))
            steps.wait()
            steps.did(nc.vector.tensor_scalar(full_ids[:, :], full_top[:, :], -1.0, float(E), ALU.mult,
                                              ALU.add))
            nc.vector.tensor_scalar(full_count[:, :], small[:, 0, 0:1], 1.0, None, ALU.max)
            steps.wait()
            nc.vector.memset(turn[:, :], 0.0).then_inc(s["routed"], 1)

            shared_weights(1)
            for u in range(2 * SHT):
                j, h = u // 2, u % 2
                dve.wait_ge(s["u_mm"], u + 1)
                dve.wait_ge(s["silu"], u + 1)
                if u >= 2:
                    dve.wait_ge(s["hhi"], u - 1)
                nc.vector.tensor_tensor(hid[:, h, :], gated[:, h, :], bank[5][:, :], ALU.mult) \
                    .then_inc(s["hid"], 1)
                dve.wait_ge(s["hhi"], u + 1)
                if u >= 2:
                    dve.wait_ge(s["d_mm"], u - 1)
                nc.vector.tensor_tensor(h_lo[:, h, :], hid[:, h, :], h_hi[:, h, :].bitcast(F32),
                                        ALU.subtract).then_inc(s["hlo"], 1)
                if h == 0 and 1 <= j < SHT - 1:
                    shared_weights(j + 1)
            for h in range(2):
                dve.wait_ge(s["d_mm"], 2 * (SHT - 1) + h + 1)
                nc.vector.tensor_copy(yT[:, 1, h * SEQ:(h + 1) * SEQ], bank[2 * h + 1][:, :]) \
                    .then_inc(s["y1"], 1)
            for k in range(TILES // 2):
                dve.wait_ge(s["yt_mm"], k + 1)
                xt = x_tok[:, 2 * k:2 * k + 2, :]
                nc.vector.tensor_tensor(xt, xt, split(bank[4 + k][:, :], 2), ALU.add).then_inc(s["x"], 1)

            def split_rows(k, par, early=False):
                e = 2 * k + par
                if not early:
                    dve.wait_ge(s["gu_mm"], ST * e - ST)
                for c in range(DC):
                    x = slice(c * MAIN, (c + 1) * MAIN)
                    dve.wait_ge(s["thi"], DC * e + c + 1)
                    nc.vector.tensor_tensor(xe_lo[:, par, x], bank[c][:, 0:MAIN], xe_hi[:, par, x].bitcast(F32),
                                            ALU.subtract).then_inc(s["tlo"], 1)

            def hidden(u, v, early=False):
                dve.wait_ge(s["gate"], u + 1)
                if not (early and v < 2):
                    dve.wait_ge(s["ht_mm"], u - 1)
                nc.vector.tensor_tensor(h_sb[:, v % 2, :], gate_sb[:, v % 2, :], bank[2 + v % 2][:, F_EXP:GU],
                                        ALU.mult).then_inc(s["h"], 1)

            def split_hidden(u, v, early=False):
                dve.wait_ge(s["hthi"], u + 1)
                if not (early and v < 2):
                    dve.wait_ge(s["dn_mm"], u - 1)
                nc.vector.tensor_tensor(he_lo[0:F_HALF, v % 2, :], bank[4 + v % 2][0:F_HALF, 0:2 * P],
                                        he_hi[0:F_HALF, v % 2, :].bitcast(F32), ALU.subtract) \
                    .then_inc(s["htlo"], 1)

            def split_down(k, par, early=False):
                e = 2 * k + par
                dve.wait_ge(s["dhi"], e + 1)
                if not early:
                    dve.wait_ge(s["dn_mm"], ST * e - ST)
                w = slice(DC * GU, EW)
                nc.vector.tensor_tensor(we_lo[0:F_HALF, par, w], raw[0:F_HALF, 1 - par, w],
                                        we_hi[0:F_HALF, par, w].bitcast(F32), ALU.subtract) \
                    .then_inc(s["edlo"], 1)

            def pair(k, early=False, end=False):
                for v in range(2 * ST):
                    par, m = v // ST, v % ST
                    u = 2 * ST * k + v
                    hidden(u, v, early)
                    if not (early and v < 1):
                        split_hidden(u - 1, (v - 1) % (2 * ST), early)
                    if m == 0 and not (end and par):
                        split_rows(k + par, 1 - par, early and par == 0)
                    if m == 1 and not (end and par):
                        split_down(k + par, 1 - par, early and par == 0)

            split_rows(0, 0, early=True)
            split_down(0, 0, early=True)
            pair(0, early=True)
            with dve.Fori(1, E // 2 - 1) as k:
                pair(k)
            pair(E // 2 - 1, end=True)

            def more_gate_up(j):
                w = slice(0, DC * GU)
                dve.wait_ge(s["whi"], j + (E + SHT + 1))
                nc.vector.tensor_tensor(we_lo[:, 0, w], raw[:, 1, w], we_hi[:, 0, w].bitcast(F32),
                                        ALU.subtract).then_inc(s["ewlo"], 1)

            def more_rows(j):
                for c in range(DC):
                    x = slice(c * MAIN, c * MAIN + P)
                    dve.wait_ge(s["thi"], DC * j + (DC * E + c + 1))
                    nc.vector.tensor_tensor(xe_lo[:, 0, x], bank[c][:, 0:P], xe_hi[:, 0, x].bitcast(F32),
                                            ALU.subtract).then_inc(s["tlo"], 1)

            def more_down(j):
                w = slice(DC * GU, EW)
                dve.wait_ge(s["dhi"], j + (E + 1))
                nc.vector.tensor_tensor(we_lo[0:F_HALF, 0, w], raw[0:F_HALF, 1, w],
                                        we_hi[0:F_HALF, 0, w].bitcast(F32), ALU.subtract).then_inc(s["edlo"], 1)

            split_hidden(ST * E - 1, 2 * ST - 1)
            dve.wait_ge(s["ewlo"], E)
            more_gate_up(0)
            more_rows(0)
            more_down(0)
            count = dve.value_load(full_count[0:1, 0:1], min_val=1, max_val=MOST_FULL)
            with dve.Fori(0, count) as j:
                dve.wait_ge(s["gate"], j + (ST * E + 1))
                nc.vector.tensor_tensor(h_sb[:, 0, :], gate_sb[:, 0, :], bank[2][:, F_EXP:GU], ALU.mult) \
                    .then_inc(s["h"], 1)
                dve.wait_ge(s["hthi"], j + (ST * E + 1))
                nc.vector.tensor_tensor(he_lo[0:F_HALF, 0, :], bank[4][0:F_HALF, 0:2 * P],
                                        he_hi[0:F_HALF, 0, :].bitcast(F32), ALU.subtract) \
                    .then_inc(s["htlo"], 1)
                more_gate_up(j + 1)
                more_rows(j + 1)
                more_down(j + 1)

            steps.wait()
            for i in range(tiles):
                add_experts(dve, s, steps, i, picks[:, i % 2])
                if between and i < DC:
                    between(i)

        def split_weights_b(c):
            w_raw = split(w_raw_b, DC)
            nc.vector.wait_ge(bb["whi"], 2 * c + 2)
            part_hi = halves[:, 0, c * WB:(c + 1) * WB]
            nc.vector.tensor_tensor(halves[:, 1, c * WB:(c + 1) * WB], w_raw[:, c, 0:WB],
                                    part_hi.bitcast(F32), ALU.subtract).then_inc(bb["wlo"], 1)
            nc.vector.tensor_tensor(wb(1, c, CHUNKS - 1), w_raw[:, c, WB:QKV_B],
                                    wb(0, c, CHUNKS - 1).bitcast(F32), ALU.subtract).then_inc(bb["wlo"], 1)

        def attention_b_dve(dve):
            KQ = K_CHUNKS + Q_CHUNKS
            dve.wait_ge(f[0]["x2"], BT)
            normalise(Steps(dve, bb["step"]), 0, bb["xn"])
            dve.wait_ge(bb["tab"], 4)
            with dve.Fori(0, BATCHES) as b:
                steps = Steps(dve, bb["step"], b * STEPS_B + STEPS_LN)
                for c in range(DC):
                    dve.wait_ge(bb["xhi"], DC * b + c + 1)
                    nc.vector.tensor_tensor(xT_lo[:, c, 0:SEQ], bank[c][:, :], xT_hi[:, c, 0:SEQ].bitcast(F32),
                                            ALU.subtract).then_inc(bb["xlo"], 1)

                def residual(i):
                    dve.wait_ge(bb["o_mm"], NKV * (BT * b + i + 1))
                    xt = x_tok[:, bass.ds(BT * b + i, 1), :].rearrange("p o d -> p (o d)")
                    nc.vector.tensor_tensor(xt, xt, bank[4][:, 0:D], ALU.add).then_inc(bb["x"], 1)

                def rotate(i, c, newton):
                    n = KQ * i + c
                    tab = 2 if c < K_CHUNKS else 0
                    heads = split(bank[c % 2][:, :], CH)
                    dve.wait_ge(bb["sq"], KQ * BT * b + n + 1)
                    if n >= 2:
                        dve.wait_ge(bb["rot"], KQ * BT * b + n - 1)
                    cos = tables[:, tab, i, :].unsqueeze(1).to_broadcast([P, CH, HD])
                    nc.vector.tensor_tensor(rope_a[:, c % 2], heads, cos, ALU.mult)
                    newton()
                    for half in range(2):
                        to = slice(half * HD // 2, (half + 1) * HD // 2)
                        of = slice((1 - half) * HD // 2, (2 - half) * HD // 2)
                        sin = tables[:, tab + 1, i, to].unsqueeze(1).to_broadcast([P, CH, HD // 2])
                        last = nc.vector.tensor_tensor(rope_b[:, c % 2, :, to], heads[:, :, of], sin, ALU.mult)
                        if half == 0:
                            newton()
                    last.then_inc(bb["rotated"], 1)

                def sums(i, c):
                    dve.wait_ge(bb["sq"], KQ * (BT * b + i) + c + 1)
                    nc.vector.reduce_sum(ss[:, i % 2, c * CH:(c + 1) * CH], split(squares[:, c % 2, :], CH),
                                         axis=X).then_inc(bb["sum"], 1)

                def maximum(i, g, newton):
                    n = NKV * i + g
                    keys = slice(0 if i else P, 2 * P)
                    dve.wait_ge(bb["s_mm"], NKV * BT * b + n + 1)
                    nc.vector.memset(turn[:, :], 0.0)
                    for h in range(2):
                        of = slice(2 * P * h + (0 if i else P), 2 * P * (h + 1))
                        steps.did(nc.vector.tensor_tensor_reduce(
                            out=s_b[:, n % 2, h, keys], in0=bank[5 + n % 2][:, of],
                            in1=mask[:, :, :].rearrange("p k s -> p (k s)")[:, keys], scale=1.0, scalar=-3e38,
                            op0=ALU.add, op1=ALU.max, accum_out=mx[:, n % 4, h:h + 1]))
                        newton()
                    steps.wait()
                    nc.vector.scalar_tensor_tensor(nb[:, n % 4, :], mx[:, n % 4, :], -1.0,
                                                   rqs[:, i % 2, 2 * g:2 * g + 2], ALU.mult, ALU.mult) \
                        .then_inc(bb["max"], 1)

                def probabilities(i, g, newton):
                    n = NKV * i + g
                    keys = slice(0 if i else P, 2 * P)
                    dve.wait_ge(bb["exp"], NKV * BT * b + n + 1)
                    steps.did(nc.vector.reciprocal(rl[:, n % 4, :], lsum[:, n % 4, :]))
                    newton()
                    steps.wait()
                    for h in range(2):
                        last = nc.vector.tensor_scalar(p_b[:, n % 2, h, keys], p_b[:, n % 2, h, keys],
                                                       rl[:, n % 4, h:h + 1], None, ALU.mult)
                    last.then_inc(bb["p"], 1)
                    newton()

                class Norms:

                    def __init__(self, i):
                        self.i, self.k, self.keys, self.on = i, 0, True, False

                    def start(self, c):
                        if c in (K_CHUNKS - 1, KQ - 1):
                            self.on, self.k, self.keys = True, 0, c == K_CHUNKS - 1

                    def step(self):
                        if not self.on:
                            return
                        heads = slice(0, NKV) if self.keys else slice(NKV, NKV + NQ)
                        n = heads.stop - heads.start
                        if self.k == 0:
                            dve.wait_ge(bb["sum"], KQ * (BT * b + self.i) + (K_CHUNKS if self.keys else KQ))
                        if self.k < STEPS_RSQRT:
                            rsqrt_step(self.k, steps, ss[:, self.i % 2, heads], EPS_RMS, 1.0 / HD, n)
                        elif self.keys:
                            steps.wait()
                            nc.vector.tensor_copy(rk[:, self.i % 2, :], rstd[:, 0, 0:n]).then_inc(bb["rk"], 1)
                            self.on = False
                        else:
                            steps.wait()
                            steps.did(nc.vector.tensor_scalar(rqs[:, self.i % 2, :], rstd[:, 0, 0:n], SCALE_B,
                                                              None, ALU.mult))
                            self.on = False
                        self.k += 1

                    def finish(self):
                        while self.on:
                            self.step()

                norms = Norms(0)
                for c in range(KQ):
                    rotate(0, c, norms.step)
                    sums(0, c)
                    norms.start(c)
                    norms.finish()
                maximum(0, 0, norms.step)
                maximum(0, 1, norms.step)
                for i in range(BT):
                    norms = Norms(i + 1)
                    if i == BT - 1:
                        dve.wait_ge(f[0]["x2"], TILES)
                        other = normalising(steps, BT - BT * b, bb["xn"])
                    for g in range(NKV):
                        probabilities(i, g, norms.step)
                        if g + 2 < NKV:
                            maximum(i, g + 2, norms.step)
                        if g == K_CHUNKS + 1:
                            norms.finish()
                        if i + 1 < BT and g < KQ:
                            rotate(i + 1, g, norms.step)
                            sums(i + 1, g)
                            norms.start(g)
                        elif i + 1 < BT:
                            for _ in range(3):
                                norms.step()
                        else:
                            for _ in range(4):
                                next(other, None)
                    norms.finish()
                    if i + 1 < BT:
                        maximum(i + 1, 0, norms.step)
                        maximum(i + 1, 1, norms.step)
                    if i:
                        residual(i - 1)
                residual(BT - 1)
                assert steps.n == STEPS_B, steps.n

        @block.vector
        def _(dve):
            attention_a_dve(dve)
            ffn_dve(dve, f[0], a["x"], 2 * BATCHES, BT, split_weights_b)
            attention_b_dve(dve)
            ffn_dve(dve, f[1], bb["x"], TILES, TILES)

        def fetch(s, i, picks):
            for k in range(TOP_K):
                nc.gpsimd.indirect_dma_start(
                    out=picks[:, k, :], out_offset=None, in_=expert_out,
                    in_offset=bass.IndirectOffsetOnAxis(ap=slot_ids[:, i, k:k + 1], axis=0),
                    bounds_check=SLOTS - 1, oob_is_err=False).then_inc((s["got0"], s["got1"])[i % 2], 16)

        def add_late_experts(i, steps):
            nc.gpsimd.wait_ge((f[0]["got0"], f[0]["got1"])[i % 2], 16 * TOP_K * (i // 2 + 1))
            weights = slot_gate[:, i, :].unsqueeze(2).to_broadcast([P, TOP_K, D])
            steps.did(nc.gpsimd.tensor_tensor(late_picks, late_picks, weights, ALU.mult))
            for n, of in ((3, 3), (1, 1), (1, 2)):
                steps.wait()
                steps.did(nc.gpsimd.tensor_tensor(late_picks[:, 0:n, :], late_picks[:, 0:n, :],
                                                  late_picks[:, of:of + n, :], ALU.add))
            steps.wait()
            nc.gpsimd.tensor_tensor(x_tok[:, i, :], x_tok[:, i, :], late_picks[:, 0, :], ALU.add) \
                .then_inc(f[0]["x2"], 1)

        def make_tables(pool):
            pool.wait_ge(rope_loaded, 16 * 7)
            pool.wait_ge(f[0]["hlo"], 2 * SHT)
            for k in range(4):
                nc.gpsimd.tensor_tensor(tables[:, k], rope_raw[:, k % 2],
                                        scales_raw[:, k, :].unsqueeze(1).to_broadcast([P, BT, HD]), ALU.mult) \
                    .then_inc(bb["tab"], 1)

        def ffn_pool(pool, s, tiles, between=None):
            for i in range(TILES):
                if i % BT == 0:
                    pool.wait_ge(s["routed"], PLACES * (i // BT + 1))
                for k in range(TOP_K):
                    nc.gpsimd.indirect_dma_start(
                        out=slot_rows, out_offset=bass.IndirectOffsetOnAxis(ap=slot_ids[:, i, k:k + 1], axis=0),
                        in_=xn[:, xn_tile(i), :], in_offset=None, bounds_check=SLOTS - 1, oob_is_err=False) \
                        .then_inc(s["sent"], 16)

            def split_gate_up(k, par, early=False):
                e = 2 * k + par
                pool.wait_ge(s["whi"], e + SHT + 1)
                if not early:
                    pool.wait_ge(s["gu_mm"], ST * e - ST)
                w = slice(0, DC * GU)
                nc.gpsimd.tensor_tensor(we_lo[:, par, w], raw[:, 1 - par, w], we_hi[:, par, w].bitcast(F32),
                                        ALU.subtract).then_inc(s["ewlo"], 1)

            for par in range(2):
                split_gate_up(0, par, early=True)
            if between:
                between(pool)
            with pool.Fori(1, E // 2) as k:
                for par in range(2):
                    split_gate_up(k, par)
            pool.wait_ge(s["routed"], FULL)
            count = pool.value_load(full_count[0:1, 0:1], min_val=1, max_val=MOST_FULL)
            pool.wait_ge(s["raw1"], 16 * count + 16 * (E // 2 + 2))
            pool.wait_ge(s["dn0"], 16 * count + 16 * (E // 2 + 1))
            pool.wait_ge(s["in0"], 16 * count + 16 * (E // 2 + 1))
            pool.wait_ge(s["out0"], 16 * count + 16 * (E // 2))
            pool.wait_ge(s["out1"], 16 * (E // 2))
            nc.gpsimd.tensor_tensor(pool_turn[:, :], expert_ids[:, 0:1], expert_ids[:, 0:1],
                                    ALU.add)
            for i in range(tiles):
                if i >= 2:
                    pool.wait_ge(s["x2"], i - 1)
                fetch(s, i, picks[:, i % 2])

        @block.gpsimd
        def _(pool):
            nc.gpsimd.iota(expert_ids[:, :], pattern=[[1, E]], base=0, channel_multiplier=0,
                           allow_small_or_imprecise_dtypes=True).then_inc(made, 1)
            nc.gpsimd.memset(zeros, 0.0).then_inc(made, 1)
            nc.gpsimd.memset(raw[:, :, SW:EW], 0.0).then_inc(made, 1)
            pool.wait_ge(wo_a_loaded, 32)
            with pool.Fori(0, BATCHES) as b:
                pool.wait_ge(a["xn"], BT * b + BT)
                xt = x_tok[:, bass.ds(BT * b, BT), :]
                nc.gpsimd.tensor_tensor(xt, xt, b_out_sb.unsqueeze(1).to_broadcast([P, BT, D]), ALU.add) \
                    .then_inc(a["bias"], 1)
            pool.wait_ge(cleared, CLEARED)
            ffn_pool(pool, f[0], BT, make_tables)
            KQ = K_CHUNKS + Q_CHUNKS
            steps = Steps(pool, added)
            for b in range(BATCHES):
                for i in range(BT):
                    if b == 0:
                        pool.wait_ge(f[0]["x2"], BT + i if i else BT - 1)
                        fetch(f[0], BT + i, late_picks)
                    for c in range(KQ):
                        n = KQ * (BT * b + i) + c
                        pool.wait_ge(bb["rotated"], n + 1)
                        if c >= 4:
                            pool.wait_ge(bb["t_mm"], KQ * (BT * b + i) + T_ORDER.index(c - 2) + 1)
                        elif i:
                            last = c if c < K_CHUNKS else c + 2
                            pool.wait_ge(bb["t_mm"], KQ * (BT * b + i - 1) + T_ORDER.index(last) + 1)
                        nc.gpsimd.tensor_tensor(roped[PLACE[c]], rope_a[:, c % 2], rope_b[:, c % 2],
                                                ALU.add).then_inc(bb["rot"], 1)
                        if c == K_CHUNKS:
                            pool.wait_ge(bb["rk"], BT * b + i + 1)
                            pool.wait_ge(bb["rot"], n)
                            for k in range(K_CHUNKS):
                                nc.gpsimd.tensor_tensor(roped[k], roped[k],
                                                        spread(rk[:, i % 2, k * CH:(k + 1) * CH], HD),
                                                        ALU.mult).then_inc(bb["krot"], 1)
                    if b == 0:
                        pool.wait_ge(f[0]["x2"], BT + i)
                        add_late_experts(BT + i, steps)
            ffn_pool(pool, f[1], TILES)


def constants():
    one = np.uint16(0x3F80)
    identity = np.eye(P, dtype=np.float32)
    before = np.stack([np.triu(np.full((P, P), one), 1), np.full((P, P), one)], 1)
    frac = np.arange(0, HD, 2, dtype=np.float32) / HD
    angle = np.arange(SEQ, dtype=np.float32)[:, None] / np.float32(10000.0) ** frac
    cos, sin = np.cos(angle), np.sin(angle)
    rope = np.stack([np.concatenate([cos, cos], 1), np.concatenate([-sin, sin], 1)])
    rope = np.ascontiguousarray(rope.reshape(2, BT, P, HD).transpose(2, 0, 1, 3)).astype(np.float32)
    q, s = np.arange(P)[:, None], np.arange(P)[None, :]
    mask = np.stack([np.where(s > q, 0, MASKED), np.where(s <= q, 0, MASKED)], 1).astype(np.float32)
    return identity, before, rope, mask


def kernel(L0_attn_a_hidden_states, L0_attn_a_w_qkv, L0_attn_a_b_qkv, L0_attn_a_w_out, L0_attn_a_b_out,
           L0_attn_b_q_kernel, L0_attn_b_kv_kernel, L0_attn_b_out_kernel, L0_attn_b_q_norm_scale,
           L0_attn_b_k_norm_scale, L0_ffn_wg_router, L0_ffn_w_gate, L0_ffn_w_up, L0_ffn_w_down,
           L0_ffn_ws_gate, L0_ffn_ws_up, L0_ffn_ws_down):
    import concourse.bacc as bacc
    from concourse.bass_utils import run_bass_kernel_spmd

    def arr(t):
        return np.asarray(t)

    x = arr(L0_attn_a_hidden_states)
    kv = arr(L0_attn_b_kv_kernel)
    w_qkv_b = np.concatenate([kv[0], arr(L0_attn_b_q_kernel), kv[1]])
    w_qkv_b = w_qkv_b.transpose(1, 0, 2).reshape(DC, P, QKV_B).transpose(1, 0, 2)

    pad = SHT * P - F_SH

    def hidden_tiles(w):
        w = np.pad(arr(w), ((0, 0), (0, pad)))
        return w.reshape(DC, P, SHT, P).transpose(2, 1, 0, 3).reshape(SHT, P, D)

    w_shared = np.concatenate([hidden_tiles(L0_ffn_ws_gate), hidden_tiles(L0_ffn_ws_up),
                               np.pad(arr(L0_ffn_ws_down), ((0, pad), (0, 0))).reshape(SHT, P, D)], 2)
    w_gate_up = np.concatenate([arr(L0_ffn_w_gate), arr(L0_ffn_w_up)], 2)
    w_gate_up = w_gate_up.reshape(E, DC, P, GU).transpose(0, 2, 1, 3).reshape(E, P, DC * GU)
    w_down = arr(L0_ffn_w_down).reshape(E, 2, F_HALF, D).transpose(0, 2, 1, 3).reshape(E, F_HALF, 2 * D)
    identity, before, rope, mask = constants()
    arrays = {
        "x": x.reshape(TOK, D),
        "w_qkv_a": arr(L0_attn_a_w_qkv).T,
        "b_qkv_a": arr(L0_attn_a_b_qkv).reshape(6, P).T,
        "w_out_a": arr(L0_attn_a_w_out).T,
        "b_out_a": arr(L0_attn_a_b_out),
        "w_qkv_b": w_qkv_b,
        "w_out_b": arr(L0_attn_b_out_kernel),
        "q_scale": arr(L0_attn_b_q_norm_scale),
        "k_scale": arr(L0_attn_b_k_norm_scale),
        "w_router": np.pad(arr(L0_ffn_wg_router).T, ((0, 0), (0, P - E))),
        "w_shared": w_shared,
        "w_gate_up": w_gate_up,
        "w_down": w_down,
        "identity": identity,
        "before": before,
        "rope": rope,
        "mask": mask,
    }
    arrays = {f"in_{n}": np.ascontiguousarray(v) for n, v in arrays.items()}
    nc = bacc.Bacc("TRN2", target_bir_lowering=False, num_devices=1)
    args = [nc.dram_tensor(n, v.shape, mybir.dt.from_np(v.dtype), kind="ExternalInput").ap()
            for n, v in arrays.items()]
    out = nc.dram_tensor("out_x", (TOK, D), F32, kind="ExternalOutput").ap()
    slot_rows, expert_out = (nc.dram_tensor(n, (SLOTS, D), F32, kind="Internal").ap()
                             for n in ("slot_rows", "expert_out"))
    program(nc, *args, slot_rows, expert_out, out)
    r = run_bass_kernel_spmd(nc, [arrays], core_ids=[0])
    return r.results[0]["out_x"].reshape(x.shape)
```
